# Optimizing a Trainium2 kernel written in Bass

```python
import numpy as np
import jax
import jax.numpy as jnp

def _softmax(x, axis=-1):
    return jax.nn.softmax(x, axis=axis)

def _gelu(x):
    return jax.nn.gelu(x, approximate=True)

def _silu(x):
    return jax.nn.silu(x)

def _sigmoid(x):
    return jax.nn.sigmoid(x)

def _layernorm(x, axis=-1, eps=1e-05):
    m = jnp.mean(x, axis=axis, keepdims=True)
    v = jnp.var(x, axis=axis, keepdims=True)
    return (x - m) / jnp.sqrt(v + eps)

def _scatter_add(tgt, idx, src, axis=0):
    return tgt.at[idx].add(src)

def _segment_sum(src, seg, n):
    return jax.ops.segment_sum(src, seg, n)
kernel_name = 'mk_cond_seq_d4_seqx_r4_dd6f15'

def setup_inputs(seed: int=0):
    np.random.seed(seed)
    _w = jnp.asarray

    def _rec_inputs():
        import jax
        import jax.numpy as jnp
        _rk = jax.random.key(seed)
        x = -0.000125 + 0.9999 * jax.random.normal(jax.random.fold_in(_rk, 1), (16, 256, 256), jnp.float32)
        _lenS = 256 - jax.random.randint(jax.random.fold_in(_rk, 7), (16,), 0, max(1, 256 // 4) + 1, jnp.int32)
        _lenS2 = 256 - jax.random.randint(jax.random.fold_in(_rk, 8), (16,), 0, max(1, 256 // 4) + 1, jnp.int32)
        condB_t = jax.random.uniform(jax.random.fold_in(_rk, 11), (16,), jnp.float32, 0.0, 0.983423)
        itok_B_0_2 = jax.random.randint(jax.random.fold_in(_rk, 12), (16,), 0, 3, jnp.int32)
        itok_B_34_63 = jax.random.randint(jax.random.fold_in(_rk, 14), (16,), 34, 64, jnp.int32)
        fside_Bx16xSxS_0 = -1.47943e-05 + 1.00017 * jax.random.normal(jax.random.fold_in(_rk, 15), (16, 16, 256, 256), jnp.float32)
        condB_theta = jax.random.uniform(jax.random.fold_in(_rk, 16), (16,), jnp.float32, 0.0, 0.983423)
        condB_phi = jax.random.uniform(jax.random.fold_in(_rk, 17), (16,), jnp.float32, 0.0, 0.961312)
        _validS = jnp.arange(256)[None, :] < _lenS[:, None]
        _validS2 = jnp.arange(256)[None, :] < _lenS2[:, None]
        _causal = jnp.tril(jnp.ones((256, 256), dtype=bool))
        mask_Bx1xSxS_bk0 = jnp.logical_not(jnp.broadcast_to(_validS[:, None, None, :], (16, 1, 256, 256)))
        return (x, condB_t, itok_B_0_2, itok_B_34_63, fside_Bx16xSxS_0, condB_theta, condB_phi, mask_Bx1xSxS_bk0)
    x, condB_t, itok_B_0_2, itok_B_34_63, fside_Bx16xSxS_0, condB_theta, condB_phi, mask_Bx1xSxS_bk0 = _rec_inputs()

    def _L0_cond_setup():
        import jax, jax.numpy as jnp
        import numpy as np
        import math
        B, S, D, E = (32, 256, 256, 128)

        def _layer_norm(x, gamma, beta, eps=1e-05):
            mean = jnp.mean(x, axis=(-2, -1), keepdims=True)
            var = jnp.mean(jnp.square(x - mean), axis=(-2, -1), keepdims=True)
            return (x - mean) * jax.lax.rsqrt(var + eps) * gamma + beta

        def _noise_encoding(t, channels):
            half = channels // 2
            freqs = jnp.exp(jnp.arange(half, dtype=jnp.float32) * (-math.log(10000.0) / (half - 1)))
            emb = 5000.0 * t[:, None] * freqs[None, :]
            return jnp.concatenate([jnp.sin(emb), jnp.cos(emb)], axis=1)
        key = jax.random.key(seed)
        ks = jax.random.split(key, 20)

        def lin(k, fan_in, shape):
            return jax.random.normal(k, shape, jnp.float32) / np.sqrt(fan_in)
        inp = {'x': jax.random.normal(ks[0], (B, S, D), jnp.float32), 't': jax.random.uniform(ks[1], (B,), jnp.float32), 'W1': lin(ks[2], E, (E, 4 * E)), 'b1': jnp.zeros((4 * E,), jnp.float32), 'W2': lin(ks[3], 4 * E, (4 * E, 4 * E)), 'b2': jnp.zeros((4 * E,), jnp.float32), 'Wsc': lin(ks[4], 4 * E, (4 * E, D)), 'bsc': jnp.zeros((D,), jnp.float32), 'Wsh': lin(ks[5], 4 * E, (4 * E, D)), 'bsh': jnp.zeros((D,), jnp.float32), 'gamma': jnp.ones((S, D), jnp.float32), 'beta': jnp.zeros((S, D), jnp.float32), 'W_in': lin(ks[6], D, (D, D)), 'b_in': jnp.zeros((D,), jnp.float32), 'W_out': lin(ks[7], D, (D, D)), 'b_out': jnp.zeros((D,), jnp.float32)}
        return inp
    _L0_cond_all = _L0_cond_setup()
    _L0_cond_in = {k: v for k, v in _L0_cond_all.items() if k in ('W1', 'b1', 'W2', 'b2', 'Wsc', 'bsc', 'Wsh', 'bsh', 'gamma', 'beta', 'W_in', 'b_in', 'W_out', 'b_out')}
    del _L0_cond_all

    def _L1_cond_setup():
        import jax, jax.numpy as jnp
        import numpy as np
        H = 256
        EPS = 1e-05

        def _gelu(x):
            return jax.nn.gelu(x, approximate=False)
        key = jax.random.key(seed)
        ks = jax.random.split(key, 16)
        s = 1.0 / np.sqrt(H)
        inp = {'x': jax.random.normal(ks[0], (64, 256, H), dtype=jnp.float32), 'condition': jax.random.randint(ks[1], (64,), 0, 3), 'w1_nr': jax.random.normal(ks[2], (H, H), dtype=jnp.float32) * s, 'b1_nr': jnp.zeros((H,), dtype=jnp.float32), 'w2_nr': jax.random.normal(ks[3], (H, H), dtype=jnp.float32) * s, 'b2_nr': jnp.zeros((H,), dtype=jnp.float32), 'w1_tsr': jax.random.normal(ks[4], (H, H), dtype=jnp.float32) * s, 'b1_tsr': jnp.zeros((H,), dtype=jnp.float32), 'w2_tsr': jax.random.normal(ks[5], (H, H), dtype=jnp.float32) * s, 'b2_tsr': jnp.zeros((H,), dtype=jnp.float32), 'w1_sr': jax.random.normal(ks[6], (H, 2 * H), dtype=jnp.float32) * s, 'b1_sr': jnp.zeros((2 * H,), dtype=jnp.float32), 'w2_sr': jax.random.normal(ks[7], (2 * H, H), dtype=jnp.float32) * (1.0 / np.sqrt(2 * H)), 'b2_sr': jnp.zeros((H,), dtype=jnp.float32), 'w3_sr': jax.random.normal(ks[8], (H, H), dtype=jnp.float32) * s, 'b3_sr': jnp.zeros((H,), dtype=jnp.float32), 'gamma': jnp.ones((H,), dtype=jnp.float32), 'beta': jnp.zeros((H,), dtype=jnp.float32)}
        return inp
    _L1_cond_all = _L1_cond_setup()
    _L1_cond_in = {k: v for k, v in _L1_cond_all.items() if k in ('w1_nr', 'b1_nr', 'w2_nr', 'b2_nr', 'w1_tsr', 'b1_tsr', 'w2_tsr', 'b2_tsr', 'w1_sr', 'b1_sr', 'w2_sr', 'b2_sr', 'w3_sr', 'b3_sr', 'gamma', 'beta')}
    del _L1_cond_all

    def _L2_cond_setup():
        import jax, jax.numpy as jnp
        import numpy as np
        import math
        D_MODEL = 256
        N_HEAD = 16
        HEAD_DIM = D_MODEL // N_HEAD
        D_FF = 1024
        NUM_STEPS = 100.0
        RESCALE = 4000.0
        EPS = 1e-05

        def _sin_emb(t):
            half = D_MODEL // 2
            x = t.astype(jnp.float32) / NUM_STEPS * RESCALE
            freqs = jnp.exp(jnp.arange(half, dtype=jnp.float32) * (-math.log(10000.0) / (half - 1)))
            e = x[:, None] * freqs[None, :]
            return jnp.concatenate([jnp.sin(e), jnp.cos(e)], axis=-1)

        def _ln(x):
            m = jnp.mean(x, axis=-1, keepdims=True)
            v = jnp.var(x, axis=-1, keepdims=True)
            return (x - m) / jnp.sqrt(v + EPS)

        def _gelu2(x):
            return x * jax.nn.sigmoid(1.702 * x)
        key = jax.random.key(seed)
        ks = jax.random.split(key, 24)
        B, S, D, F = (4, 128, D_MODEL, D_FF)
        std = 0.02
        inp = {'src': jax.random.normal(ks[0], (B, S, D), dtype=jnp.float32), 'src_mask': jax.random.randint(ks[1], (B, 1, S, S), 0, 2).astype(bool), 'timestep': jax.random.randint(ks[2], (B,), 0, 100, dtype=jnp.int32), 'attention_bias': jax.random.normal(ks[3], (B, N_HEAD, S, S), dtype=jnp.float32), 'W_ada': jax.random.normal(ks[4], (D, 2 * D), dtype=jnp.float32) * std, 'b_ada': jnp.zeros((2 * D,), dtype=jnp.float32), 'Wq': jax.random.normal(ks[5], (D, D), dtype=jnp.float32) * std, 'bq': jnp.zeros((D,), dtype=jnp.float32), 'Wk': jax.random.normal(ks[6], (D, D), dtype=jnp.float32) * std, 'bk': jnp.zeros((D,), dtype=jnp.float32), 'Wv': jax.random.normal(ks[7], (D, D), dtype=jnp.float32) * std, 'bv': jnp.zeros((D,), dtype=jnp.float32), 'Wo': jax.random.normal(ks[8], (D, D), dtype=jnp.float32) * std, 'bo': jnp.zeros((D,), dtype=jnp.float32), 'W1': jax.random.normal(ks[9], (D, F), dtype=jnp.float32) * std, 'b1': jnp.zeros((F,), dtype=jnp.float32), 'W2': jax.random.normal(ks[10], (F, D), dtype=jnp.float32) * std, 'b2': jnp.zeros((D,), dtype=jnp.float32), 'g2': jnp.ones((D,), dtype=jnp.float32), 'beta2': jnp.zeros((D,), dtype=jnp.float32)}
        return inp
    _L2_cond_all = _L2_cond_setup()
    _L2_cond_in = {k: v for k, v in _L2_cond_all.items() if k in ('W_ada', 'b_ada', 'Wq', 'bq', 'Wk', 'bk', 'Wv', 'bv', 'Wo', 'bo', 'W1', 'b1', 'W2', 'b2', 'g2', 'beta2')}
    del _L2_cond_all

    def _L3_cond_setup():
        import jax, jax.numpy as jnp
        import numpy as np
        key = jax.random.key(seed)
        k1, k2, k3 = jax.random.split(key, 3)
        B, N, D = (16, 1024, 256)
        embeddings = jax.random.normal(k1, (B, N, D), dtype=jnp.float32)
        theta = jax.random.uniform(k2, (B,), dtype=jnp.float32)
        phi = jax.random.uniform(k3, (B,), dtype=jnp.float32)
        return {'embeddings': embeddings, 'theta': theta, 'phi': phi}
    _L3_cond_all = _L3_cond_setup()
    _L3_cond_in = {k: v for k, v in _L3_cond_all.items() if k in ()}
    del _L3_cond_all
    return {'x': x, 'condB_t': condB_t, 'itok_B_0_2': itok_B_0_2, 'itok_B_34_63': itok_B_34_63, 'fside_Bx16xSxS_0': fside_Bx16xSxS_0, 'condB_theta': condB_theta, 'condB_phi': condB_phi, 'mask_Bx1xSxS_bk0': mask_Bx1xSxS_bk0, 'L0_cond_W1': _L0_cond_in['W1'], 'L0_cond_b1': _L0_cond_in['b1'], 'L0_cond_W2': _L0_cond_in['W2'], 'L0_cond_b2': _L0_cond_in['b2'], 'L0_cond_Wsc': _L0_cond_in['Wsc'], 'L0_cond_bsc': _L0_cond_in['bsc'], 'L0_cond_Wsh': _L0_cond_in['Wsh'], 'L0_cond_bsh': _L0_cond_in['bsh'], 'L0_cond_gamma': _L0_cond_in['gamma'], 'L0_cond_beta': _L0_cond_in['beta'], 'L0_cond_W_in': _L0_cond_in['W_in'], 'L0_cond_b_in': _L0_cond_in['b_in'], 'L0_cond_W_out': _L0_cond_in['W_out'], 'L0_cond_b_out': _L0_cond_in['b_out'], 'L1_cond_w1_nr': _L1_cond_in['w1_nr'], 'L1_cond_b1_nr': _L1_cond_in['b1_nr'], 'L1_cond_w2_nr': _L1_cond_in['w2_nr'], 'L1_cond_b2_nr': _L1_cond_in['b2_nr'], 'L1_cond_w1_tsr': _L1_cond_in['w1_tsr'], 'L1_cond_b1_tsr': _L1_cond_in['b1_tsr'], 'L1_cond_w2_tsr': _L1_cond_in['w2_tsr'], 'L1_cond_b2_tsr': _L1_cond_in['b2_tsr'], 'L1_cond_w1_sr': _L1_cond_in['w1_sr'], 'L1_cond_b1_sr': _L1_cond_in['b1_sr'], 'L1_cond_w2_sr': _L1_cond_in['w2_sr'], 'L1_cond_b2_sr': _L1_cond_in['b2_sr'], 'L1_cond_w3_sr': _L1_cond_in['w3_sr'], 'L1_cond_b3_sr': _L1_cond_in['b3_sr'], 'L1_cond_gamma': _L1_cond_in['gamma'], 'L1_cond_beta': _L1_cond_in['beta'], 'L2_cond_W_ada': _L2_cond_in['W_ada'], 'L2_cond_b_ada': _L2_cond_in['b_ada'], 'L2_cond_Wq': _L2_cond_in['Wq'], 'L2_cond_bq': _L2_cond_in['bq'], 'L2_cond_Wk': _L2_cond_in['Wk'], 'L2_cond_bk': _L2_cond_in['bk'], 'L2_cond_Wv': _L2_cond_in['Wv'], 'L2_cond_bv': _L2_cond_in['bv'], 'L2_cond_Wo': _L2_cond_in['Wo'], 'L2_cond_bo': _L2_cond_in['bo'], 'L2_cond_W1': _L2_cond_in['W1'], 'L2_cond_b1': _L2_cond_in['b1'], 'L2_cond_W2': _L2_cond_in['W2'], 'L2_cond_b2': _L2_cond_in['b2'], 'L2_cond_g2': _L2_cond_in['g2'], 'L2_cond_beta2': _L2_cond_in['beta2']}

def reference(x, condB_t, itok_B_0_2, itok_B_34_63, fside_Bx16xSxS_0, condB_theta, condB_phi, mask_Bx1xSxS_bk0, L0_cond_W1, L0_cond_b1, L0_cond_W2, L0_cond_b2, L0_cond_Wsc, L0_cond_bsc, L0_cond_Wsh, L0_cond_bsh, L0_cond_gamma, L0_cond_beta, L0_cond_W_in, L0_cond_b_in, L0_cond_W_out, L0_cond_b_out, L1_cond_w1_nr, L1_cond_b1_nr, L1_cond_w2_nr, L1_cond_b2_nr, L1_cond_w1_tsr, L1_cond_b1_tsr, L1_cond_w2_tsr, L1_cond_b2_tsr, L1_cond_w1_sr, L1_cond_b1_sr, L1_cond_w2_sr, L1_cond_b2_sr, L1_cond_w3_sr, L1_cond_b3_sr, L1_cond_gamma, L1_cond_beta, L2_cond_W_ada, L2_cond_b_ada, L2_cond_Wq, L2_cond_bq, L2_cond_Wk, L2_cond_bk, L2_cond_Wv, L2_cond_bv, L2_cond_Wo, L2_cond_bo, L2_cond_W1, L2_cond_b1, L2_cond_W2, L2_cond_b2, L2_cond_g2, L2_cond_beta2):
    import jax
    import jax.numpy as jnp

    def _L0_cond_ref(x, t, W1, b1, W2, b2, Wsc, bsc, Wsh, bsh, gamma, beta, W_in, b_in, W_out, b_out):
        import jax, jax.numpy as jnp
        import numpy as np
        import math
        B, S, D, E = (32, 256, 256, 128)

        def _layer_norm(x, gamma, beta, eps=1e-05):
            mean = jnp.mean(x, axis=(-2, -1), keepdims=True)
            var = jnp.mean(jnp.square(x - mean), axis=(-2, -1), keepdims=True)
            return (x - mean) * jax.lax.rsqrt(var + eps) * gamma + beta

        def _noise_encoding(t, channels):
            half = channels // 2
            freqs = jnp.exp(jnp.arange(half, dtype=jnp.float32) * (-math.log(10000.0) / (half - 1)))
            emb = 5000.0 * t[:, None] * freqs[None, :]
            return jnp.concatenate([jnp.sin(emb), jnp.cos(emb)], axis=1)
        h = _noise_encoding(t, E)
        h = jax.nn.silu(h @ W1 + b1)
        h = h @ W2 + b2
        scale = (h @ Wsc + bsc)[:, None, :]
        shift = (h @ Wsh + bsh)[:, None, :]
        out = jax.nn.silu(scale * _layer_norm(x, gamma, beta) + shift)
        out = out @ W_in + b_in
        out = jax.nn.silu(scale * _layer_norm(out, gamma, beta) + shift)
        out = out @ W_out + b_out
        return out + x

    def _L1_cond_ref(x, condition, w1_nr, b1_nr, w2_nr, b2_nr, w1_tsr, b1_tsr, w2_tsr, b2_tsr, w1_sr, b1_sr, w2_sr, b2_sr, w3_sr, b3_sr, gamma, beta):
        import jax, jax.numpy as jnp
        import numpy as np
        H = 256
        EPS = 1e-05

        def _gelu(x):
            return jax.nn.gelu(x, approximate=False)
        out_nr = _gelu(jnp.einsum('bth,hk->btk', x, w1_nr) + b1_nr)
        out_nr = jnp.einsum('bth,hk->btk', out_nr, w2_nr) + b2_nr
        out_tsr = _gelu(jnp.einsum('bth,hk->btk', x, w1_tsr) + b1_tsr)
        out_tsr = jnp.einsum('bth,hk->btk', out_tsr, w2_tsr) + b2_tsr
        h = _gelu(jnp.einsum('bth,hk->btk', x, w1_sr) + b1_sr)
        h = _gelu(jnp.einsum('bth,hk->btk', h, w2_sr) + b2_sr)
        out_sr = jnp.einsum('bth,hk->btk', h, w3_sr) + b3_sr
        c = condition[:, None, None]
        out = jnp.where(c == 0, out_nr, jnp.where(c == 1, out_tsr, jnp.where(c == 2, out_sr, jnp.zeros_like(x))))
        y = x + out
        mu = jnp.mean(y, axis=-1, keepdims=True)
        var = jnp.mean((y - mu) ** 2, axis=-1, keepdims=True)
        return (y - mu) * jax.lax.rsqrt(var + EPS) * gamma + beta

    def _L2_cond_ref(src, src_mask, timestep, attention_bias, W_ada, b_ada, Wq, bq, Wk, bk, Wv, bv, Wo, bo, W1, b1, W2, b2, g2, beta2):
        import jax, jax.numpy as jnp
        import numpy as np
        import math
        D_MODEL = 256
        N_HEAD = 16
        HEAD_DIM = D_MODEL // N_HEAD
        D_FF = 1024
        NUM_STEPS = 100.0
        RESCALE = 4000.0
        EPS = 1e-05

        def _sin_emb(t):
            half = D_MODEL // 2
            x = t.astype(jnp.float32) / NUM_STEPS * RESCALE
            freqs = jnp.exp(jnp.arange(half, dtype=jnp.float32) * (-math.log(10000.0) / (half - 1)))
            e = x[:, None] * freqs[None, :]
            return jnp.concatenate([jnp.sin(e), jnp.cos(e)], axis=-1)

        def _ln(x):
            m = jnp.mean(x, axis=-1, keepdims=True)
            v = jnp.var(x, axis=-1, keepdims=True)
            return (x - m) / jnp.sqrt(v + EPS)

        def _gelu2(x):
            return x * jax.nn.sigmoid(1.702 * x)
        B, S, D = src.shape
        emb = jax.nn.silu(_sin_emb(timestep)) @ W_ada + b_ada
        scale, shift = jnp.split(emb[:, None, :], 2, axis=-1)
        x = _ln(src) * (1.0 + scale) + shift
        q = (x @ Wq + bq).reshape(B, S, N_HEAD, HEAD_DIM).transpose(0, 2, 1, 3)
        k = (x @ Wk + bk).reshape(B, S, N_HEAD, HEAD_DIM).transpose(0, 2, 1, 3)
        v = (x @ Wv + bv).reshape(B, S, N_HEAD, HEAD_DIM).transpose(0, 2, 1, 3)
        scores = jnp.einsum('bhqd,bhkd->bhqk', q / math.sqrt(HEAD_DIM), k)
        scores = scores + attention_bias
        scores = jnp.where(src_mask, -jnp.inf, scores.astype(jnp.float32))
        probs = jax.nn.softmax(scores, axis=-1).astype(v.dtype)
        ctx = jnp.einsum('bhqk,bhkd->bhqd', probs, v)
        ctx = ctx.transpose(0, 2, 1, 3).reshape(B, S, D)
        x = x + (ctx @ Wo + bo)
        h = _ln(x) * g2 + beta2
        ff = _gelu2(h @ W1 + b1) @ W2 + b2
        return x + ff

    def _L3_cond_ref(embeddings, theta, phi):
        import jax, jax.numpy as jnp
        import numpy as np
        B, N, D = embeddings.shape
        e = embeddings.reshape(B, N, D // 4, 4)
        ct = jnp.cos(theta)[:, None, None]
        st = jnp.sin(theta)[:, None, None]
        cp = jnp.cos(phi)[:, None, None]
        sp = jnp.sin(phi)[:, None, None]
        x0, x1, x2, x3 = (e[..., 0], e[..., 1], e[..., 2], e[..., 3])
        out = jnp.stack([x0 * ct + x1 * st, -x0 * st + x1 * ct, x2 * cp + x3 * sp, -x2 * sp + x3 * cp], axis=-1)
        return out.reshape(B, N, D)
    x = _L0_cond_ref(x, condB_t, L0_cond_W1, L0_cond_b1, L0_cond_W2, L0_cond_b2, L0_cond_Wsc, L0_cond_bsc, L0_cond_Wsh, L0_cond_bsh, L0_cond_gamma, L0_cond_beta, L0_cond_W_in, L0_cond_b_in, L0_cond_W_out, L0_cond_b_out)
    x = _L1_cond_ref(x, itok_B_0_2, L1_cond_w1_nr, L1_cond_b1_nr, L1_cond_w2_nr, L1_cond_b2_nr, L1_cond_w1_tsr, L1_cond_b1_tsr, L1_cond_w2_tsr, L1_cond_b2_tsr, L1_cond_w1_sr, L1_cond_b1_sr, L1_cond_w2_sr, L1_cond_b2_sr, L1_cond_w3_sr, L1_cond_b3_sr, L1_cond_gamma, L1_cond_beta)
    x = _L2_cond_ref(x, mask_Bx1xSxS_bk0, itok_B_34_63, fside_Bx16xSxS_0, L2_cond_W_ada, L2_cond_b_ada, L2_cond_Wq, L2_cond_bq, L2_cond_Wk, L2_cond_bk, L2_cond_Wv, L2_cond_bv, L2_cond_Wo, L2_cond_bo, L2_cond_W1, L2_cond_b1, L2_cond_W2, L2_cond_b2, L2_cond_g2, L2_cond_beta2)
    x = _L3_cond_ref(x, condB_theta, condB_phi)
    return x

_drawn_inputs = setup_inputs


def setup_inputs(seed=0):
    import zlib

    import numpy as np

    out = dict(_drawn_inputs(seed))
    spreads = {'L0_cond_b1': (0.0, 0.1),
     'L0_cond_b2': (0.0, 0.1),
     'L0_cond_bsc': (0.0, 0.1),
     'L0_cond_bsh': (0.0, 0.1),
     'L0_cond_gamma': (1.0, 0.2),
     'L0_cond_beta': (0.0, 0.285),
     'L0_cond_b_in': (0.0, 0.1),
     'L0_cond_b_out': (0.0, 0.1),
     'L1_cond_b1_nr': (0.0, 0.1),
     'L1_cond_b2_nr': (0.0, 0.1),
     'L1_cond_b1_tsr': (0.0, 0.288),
     'L1_cond_b2_tsr': (0.0, 0.1),
     'L1_cond_b1_sr': (0.0, 0.448),
     'L1_cond_b2_sr': (0.0, 0.29),
     'L1_cond_b3_sr': (0.0, 0.1),
     'L1_cond_gamma': (1.0, 0.2),
     'L1_cond_beta': (0.0, 0.1),
     'L2_cond_b_ada': (0.0, 0.1),
     'L2_cond_bq': (0.0, 0.8),
     'L2_cond_bk': (0.0, 0.8),
     'L2_cond_bv': (0.0, 0.278),
     'L2_cond_bo': (0.0, 0.1),
     'L2_cond_b1': (0.0, 0.1),
     'L2_cond_b2': (0.0, 0.1),
     'L2_cond_g2': (1.0, 0.6),
     'L2_cond_beta2': (0.0, 0.773)}
    factors = {'fside_Bx16xSxS_0': 7.14, 'L2_cond_Wq': 8.0, 'L2_cond_Wk': 8.0}
    for name, (base, spread) in spreads.items():
        noise = np.random.default_rng([zlib.crc32(name.encode()), seed]).standard_normal(out[name].shape)
        drawn = base * np.exp(spread * noise) if base else spread * noise
        out[name] = jnp.asarray(drawn.astype(out[name].dtype))
    for name, factor in factors.items():
        out[name] = (out[name] * factor).astype(out[name].dtype)
    return out
```

```python
from contextlib import ExitStack

import numpy as np
import concourse.bass as bass
from concourse import mybir

F32 = mybir.dt.float32
F32R = mybir.dt.float32r
BF16 = mybir.dt.bfloat16
F16 = mybir.dt.float16
I32 = mybir.dt.int32
U8 = mybir.dt.uint8
ALU = mybir.AluOpType
ACT = mybir.ActivationFunctionType
AX = mybir.AxisListType

P = 128
B = 16
S = 256
D = 256
TC = S // P
DC = D // P
E0 = 128
EH = 4 * E0
HC = EH // P
FF = 1024
FC = FF // P
NH = 16
HD = D // NH
LANES_A = 4
LANES = 2
EPS = 1e-5
TWO_PI = 2.0 * np.pi
PI_A = 6.28125
PI_B = float(np.float32(np.floor((TWO_PI - PI_A) * 2 ** 21) / 2 ** 21))
PI_C = float(TWO_PI - PI_A - PI_B)
ROUND = float(3 * 2 ** 22)
SIN_EDGE = 3.1415925
MASKED = -float(2.0 ** 100)

VEC = {}
_at = 0
for _name, _n in (("L0_b1", HC), ("L0_b2", HC), ("L0_bsc", DC), ("L0_bsh", DC), ("L0_b_in", DC),
                  ("nr_b1", DC), ("tsr_b1", DC), ("sr_b1", 4), ("sr_b2", DC),
                  ("bq", DC), ("bk", DC), ("ff_b1", FC), ("g2", DC), ("beta2", DC)):
    VEC[_name] = _at
    _at += _n
NVEC = _at
ROWS = {n: i for i, n in enumerate(("b_out", "nr_b2", "tsr_b2", "sr_b3", "gamma1", "beta1", "bv", "bo", "ff_b2"))}


def split_shapes():
    first = [("W_in", DC, D), ("W_out", DC, D), ("nr_w1", DC, D), ("nr_w2", DC, D), ("tsr_w1", DC, D),
             ("tsr_w2", DC, D), ("sr_w1", DC, 2 * D), ("sr_w2", 4, D), ("sr_w3", DC, D)]
    second = [("Wq", DC, D), ("Wk", DC, D), ("Wv", DC, D), ("Wo", DC, D)]
    return first, second


def build_program(nc, a, out):
    with ExitStack() as whole:
        def sb(name, shape, dt=F32, ctx=whole):
            return ctx.enter_context(nc.sbuf_tensor(name, shape, dt))

        first, second = split_shapes()
        t = dict(
            w={n: sb(f"w_{n}", [P, 2, k, m], F32R) for n, k, m in second},
            x3=sb("x3", [P, B, TC, D]),
            ident=sb("ident", [P, P]),
            vecs=sb("vecs", [P, NVEC]),
            rows=sb("rows", [P, len(ROWS), D]),
            rot=sb("rot", [P, 2, B, 4]),
            halves=sb("halves", [P, 2]),
        )
        ps = whole.enter_context(nc.psum_tensor("ps", [P, 8, 512], F32))
        ada = nc.dram_tensor("ada_scratch", [B, 2 * D], F32, kind="Internal").ap()
        with ExitStack() as ctx:
            t["w"] |= {n: sb(f"w_{n}", [P, 2, k, m], F32R, ctx) for n, k, m in first}
            t |= dict(
                mean_of=sb("mean_of", [P, P], ctx=ctx),
                scale0=sb("scale0", [P, DC, B], ctx=ctx),
                shift0=sb("shift0", [P, DC, B], ctx=ctx),
                gammaT=sb("gammaT", [P, DC, S], ctx=ctx),
                betaT=sb("betaT", [P, DC, S], ctx=ctx),
                cond=sb("cond", [1, B], I32, ctx),
            )
            with nc.cleanup_on_exit():
                conditioning(nc, a, t, ps, ada, first + second)
                first_layers(nc, a, t, ps, ada)
        with ExitStack() as ctx:
            t["ff"] = sb("w_ff", [P, 2, DC * FF + FC * D], F32R, ctx)
            attention(nc, a, t, ps)
            feed_forward(nc, a, t, ps, out)


def conditioning(nc, a, t, ps, ada, first):
    w = t["w"]
    with ExitStack() as ctx:
        def sb(name, shape, dt=F32):
            return ctx.enter_context(nc.sbuf_tensor(name, shape, dt))

        def sem(name):
            return nc.alloc_semaphore(name)

        NST = 3
        stage = sb("p_stage", [P, NST, 1024])
        w1 = sb("p_w1", [P, 1, EH])
        w2 = sb("p_w2", [P, HC, EH])
        wsc = sb("p_wsc", [P, HC, D])
        wsh = sb("p_wsh", [P, HC, D])
        wada = sb("p_wada", [P, DC, 2 * D])
        vec_rows = sb("p_vec_rows", [NVEC, P])
        gb = sb("p_gb", [P, 2, TC, D])
        bada = sb("p_bada", [B, 2 * D])
        consts = sb("p_consts", [P, 4])
        tb = sb("p_tb", [P, B])
        ti = sb("p_ti", [P, B], I32)
        dv = sb("p_divide", [P, 6, B])
        NA = 7 * B
        arg = sb("p_arg", [P, NA])
        turn = sb("p_turn", [P, NA])
        red = sb("p_red", [P, NA])
        trig = sb("p_trig", [P, NA])
        silu2 = sb("p_silu2", [P, 2, B])
        h1 = sb("p_h1", [P, HC, B])
        h2 = sb("p_h2", [P, HC, B])
        ada_rows = sb("p_ada_rows", [B, 2 * D])

        consts_in = sem("p_consts_in")
        vecs_in = sem("p_vecs_in")
        rows_in = sem("p_rows_in")
        gb_in = sem("p_gb_in")
        w_in = {n: sem(f"p_in_{n}") for n in ("w1", "w2", "wsc", "wsh", "wada")}
        stage_in = [sem(f"p_stage_in{i}") for i in range(NST)]
        hi_done = sem("p_hi_done")
        lo_done = sem("p_lo_done")
        fills = sem("p_fills")
        step = sem("p_vector_step")
        args_done = sem("p_args_done")
        sin_done = sem("p_sin_done")
        silu2_done = sem("p_silu2_done")
        vecT = sem("p_vecT")
        vecs_done = sem("p_vecs_done")
        gbT = sem("p_gbT")
        gbT_done = sem("p_gbT_done")
        h1_mm, h1_done = sem("p_h1_mm"), sem("p_h1_done")
        h2_mm, h2_done = sem("p_h2_mm"), sem("p_h2_done")
        sc_mm, ada_mm, ada_done, ada_out = sem("p_sc_mm"), sem("p_ada_mm"), sem("p_ada_done"), sem("p_ada_out")

        pieces = [(n, k0, min(k, k0 + 1024 // m) - k0, m) for n, k, m in first
                  for k0 in range(0, k, 1024 // m)]

        def factor(name):
            return HD ** -0.5 if name == "Wq" else 1.0

        block = ctx.enter_context(nc.Block())

        @block.sync
        def _(sp):
            for dst, src in ((t["ident"][:, :], a["ident"]), (consts[:, :], a["consts"]),
                             (tb[:, :], a["condB_t"].partition_broadcast(P)),
                             (ti[:, :], a["itok_B_34_63"].partition_broadcast(P)),
                             (arg[:, 3 * B:4 * B], a["condB_theta"].partition_broadcast(P)),
                             (arg[:, 4 * B:5 * B], a["condB_phi"].partition_broadcast(P)),
                             (t["cond"][:, :], a["itok_B_0_2"].rearrange("(o b) -> o b", o=1)),
                             (bada[:, :], a["L2_cond_b_ada"].partition_broadcast(B))):
                sp.dma_start(dst, src).then_inc(consts_in, 16)
            sp.dma_start(vec_rows[:, :], a["vec_rows"]).then_inc(vecs_in, 16)
            sp.dma_start(w1[:, 0, :], a["L0_cond_W1"]).then_inc(w_in["w1"], 16)
            sp.dma_start(w2[:, :, :], a["L0_cond_W2"].rearrange("(k p) n -> p k n", p=P)).then_inc(w_in["w2"], 16)
            sp.dma_start(wsc[:, :, :], a["L0_cond_Wsc"].rearrange("(k p) n -> p k n", p=P)).then_inc(w_in["wsc"], 16)
            sp.dma_start(wsh[:, :, :], a["L0_cond_Wsh"].rearrange("(k p) n -> p k n", p=P)).then_inc(w_in["wsh"], 16)
            sp.dma_start(wada[:, :, :], a["L2_cond_W_ada"].rearrange("(k p) n -> p k n", p=P)).then_inc(w_in["wada"], 16)
            sp.dma_start(gb[:, 0, :, :], a["L0_cond_gamma"].rearrange("(c p) d -> p c d", p=P)).then_inc(gb_in, 16)
            sp.dma_start(gb[:, 1, :, :], a["L0_cond_beta"].rearrange("(c p) d -> p c d", p=P)).then_inc(gb_in, 16)
            sp.dma_start(t["rows"][:, :, :], a["rows"].partition_broadcast(P)).then_inc(rows_in, 16)
            sp.wait_ge(ada_done, 2)
            sp.dma_start(ada, ada_rows[:, :]).then_inc(ada_out, 16)
            sp.wait_ge(ada_out, 16)
            sp.wait_ge(rows_in, 16)

        @block.gpsimd
        def _(pool):
            pool.memset(t["mean_of"][:, :], 1.0 / P).then_inc(fills, 1)
            pool.memset(t["halves"][:, :], -0.5).then_inc(fills, 1)
            for i, (n, k0, nk, m) in enumerate(pieces):
                if i >= NST:
                    pool.wait_ge(lo_done, i - NST + 1)
                pool.dma_start(stage[:, i % NST, 0:nk * m].rearrange("p (k m) -> p k m", m=m),
                               a[n].rearrange("(k p) m -> p k m", p=P)[:, k0:k0 + nk, :]).then_inc(stage_in[i % NST], 16)

        @block.scalar
        def _(act):
            act.wait_ge(args_done, 1)
            act.activation(trig[:, :], red[:, :], ACT.Sin).then_inc(sin_done, 1)
            act.wait_ge(sin_done, 1)
            act.activation(silu2[:, :, :], trig[:, B:3 * B].rearrange("p (c b) -> p c b", c=2),
                           ACT.Silu).then_inc(silu2_done, 1)
            act.wait_ge(vecs_done, 1)
            act.wait_ge(h1_mm, 1)
            for m in range(HC):
                last = act.activation(h1[:, m, :], ps[:, 0, m * B:(m + 1) * B], ACT.Silu,
                                      bias=t["vecs"][:, VEC["L0_b1"] + m:VEC["L0_b1"] + m + 1])
            last.then_inc(h1_done, 1)
            for i, (n, k0, nk, m) in enumerate(pieces):
                act.wait_ge(stage_in[i % NST], 16 * (i // NST + 1))
                act.activation(w[n][:, 0, k0:k0 + nk, :].rearrange("p k m -> p (k m)"), stage[:, i % NST, 0:nk * m],
                               ACT.Copy, scale=factor(n)).then_inc(hi_done, 1)

        @block.vector
        def _(dve):
            n_step = [0]

            def then(ins):
                n_step[0] += 1
                ins.then_inc(step, 1)
                dve.wait_ge(step, n_step[0])

            dve.wait_ge(consts_in, 16 * 8)
            then(dve.tensor_scalar(arg[:, 0:B], tb[:, :], 5000.0, consts[:, 0:1], ALU.mult, ALU.mult))
            num, quot, big, high, low, rem = (dv[:, j, :] for j in range(6))
            then(dve.tensor_copy(num, ti[:, :]))
            then(dve.tensor_scalar(quot, num, 0.01, None, ALU.mult))
            then(dve.tensor_scalar(big, quot, 4097.0, None, ALU.mult))
            then(dve.tensor_tensor(high, big, quot, ALU.subtract))
            then(dve.tensor_tensor(high, big, high, ALU.subtract))
            then(dve.tensor_tensor(low, quot, high, ALU.subtract))
            then(dve.scalar_tensor_tensor(rem, high, -100.0, num, ALU.mult, ALU.add))
            then(dve.scalar_tensor_tensor(rem, low, -100.0, rem, ALU.mult, ALU.add))
            then(dve.scalar_tensor_tensor(arg[:, 6 * B:7 * B], rem, 0.01, quot, ALU.mult, ALU.add))
            then(dve.tensor_scalar(arg[:, B:2 * B], arg[:, 6 * B:7 * B], 4000.0, consts[:, 1:2], ALU.mult, ALU.mult))
            then(dve.tensor_copy(arg[:, 2 * B:3 * B], arg[:, B:2 * B]))
            then(dve.tensor_copy(arg[:, 5 * B:7 * B], arg[:, 3 * B:5 * B]))
            sin_part = ((0, B, consts[:, 2:3], consts[:, 3:4]), (B, 2 * B, 0.0, 0.0), (2 * B, 3 * B, 0.25, np.pi / 2),
                        (3 * B, 5 * B, 0.0, 0.0), (5 * B, 7 * B, 0.25, np.pi / 2))
            for lo, hi, turns, _angle in sin_part:
                then(dve.tensor_scalar(turn[:, lo:hi], arg[:, lo:hi], 1.0 / TWO_PI, turns, ALU.mult, ALU.add))
            then(dve.tensor_scalar(turn[:, :], turn[:, :], ROUND, None, ALU.add))
            then(dve.tensor_scalar(turn[:, :], turn[:, :], -ROUND, None, ALU.add))
            then(dve.scalar_tensor_tensor(red[:, :], turn[:, :], -PI_A, arg[:, :], ALU.mult, ALU.add))
            then(dve.scalar_tensor_tensor(red[:, :], turn[:, :], -PI_B, red[:, :], ALU.mult, ALU.add))
            then(dve.scalar_tensor_tensor(red[:, :], turn[:, :], -PI_C, red[:, :], ALU.mult, ALU.add))
            for lo, hi, _turns, angle in sin_part:
                then(dve.tensor_scalar(red[:, lo:hi], red[:, lo:hi], angle, SIN_EDGE, ALU.add, ALU.min))
            dve.tensor_scalar(red[:, :], red[:, :], -SIN_EDGE, None, ALU.max).then_inc(args_done, 1)
            dve.wait_ge(vecT, 1)
            dve.tensor_copy(t["vecs"][:, :], ps[:, 1, 0:NVEC]).then_inc(vecs_done, 1)
            dve.wait_ge(vecs_done, 1)
            dve.tensor_scalar(t["vecs"][:, VEC["bq"]:VEC["bq"] + DC], t["vecs"][:, VEC["bq"]:VEC["bq"] + DC],
                              factor("Wq"), None, ALU.mult)
            dve.wait_ge(sin_done, 1)
            for j in range(4):
                at = (j // 2) * B
                dve.tensor_copy(t["rot"][:, 0, :, j], trig[:, 5 * B + at:6 * B + at])
                dve.tensor_scalar(t["rot"][:, 1, :, j], trig[:, 3 * B + at:4 * B + at], -1.0 if j % 2 else 1.0,
                                  None, ALU.mult)
            dve.wait_ge(gbT, 1)
            for i, name in enumerate(("gammaT", "betaT")):
                dve.tensor_copy(t[name][:, :, :].rearrange("p c s -> p (c s)"), ps[:, 4 + i, :]).then_inc(gbT_done, 1)
            dve.wait_ge(h2_mm, 1)
            for m in range(HC):
                last = dve.tensor_scalar(h2[:, m, :], ps[:, 2, m * B:(m + 1) * B],
                                         t["vecs"][:, VEC["L0_b2"] + m:VEC["L0_b2"] + m + 1], None, ALU.add)
            last.then_inc(h2_done, 1)
            dve.wait_ge(ada_mm, 1)
            dve.tensor_tensor(ada_rows[:, :], ps[0:B, 6, :], bada[:, :], ALU.add).then_inc(ada_done, 1)
            dve.wait_ge(ada_done, 1)
            dve.tensor_scalar(ada_rows[:, 0:D], ada_rows[:, 0:D], 1.0, None, ALU.add).then_inc(ada_done, 1)
            dve.wait_ge(sc_mm, 1)
            for m in range(DC):
                for q, (dst, b) in enumerate((("scale0", "L0_bsc"), ("shift0", "L0_bsh"))):
                    dve.tensor_scalar(t[dst][:, m, :], ps[:, 3, (q * DC + m) * B:(q * DC + m + 1) * B],
                                      t["vecs"][:, VEC[b] + m:VEC[b] + m + 1], None, ALU.add)
            for i, (n, k0, nk, m) in enumerate(pieces):
                dve.wait_ge(hi_done, i + 1)
                dve.scalar_tensor_tensor(w[n][:, 1, k0:k0 + nk, :].rearrange("p k m -> p (k m)"),
                                         stage[:, i % NST, 0:nk * m], factor(n),
                                         w[n][:, 0, k0:k0 + nk, :].rearrange("p k m -> p (k m)").bitcast(F32),
                                         ALU.mult, ALU.subtract).then_inc(lo_done, 1)

        @block.tensor
        def _(pe):
            pe.wait_ge(consts_in, 16 * 8)
            pe.wait_ge(vecs_in, 16)
            pe.transpose(ps[:, 1, 0:NVEC], vec_rows[:, :], t["ident"][0:NVEC, 0:NVEC]).then_inc(vecT, 1)
            pe.wait_ge(w_in["w1"], 16)
            pe.wait_ge(sin_done, 1)
            for m in range(HC):
                last = pe.matmul(ps[:, 0, m * B:(m + 1) * B], w1[:, 0, m * P:(m + 1) * P], trig[:, 0:B],
                                 start=True, stop=True)
            last.then_inc(h1_mm, 1)
            pe.wait_ge(gb_in, 32)
            for q in range(2):
                for c in range(DC):
                    for s in range(TC):
                        last = pe.transpose(ps[:, 4 + q, c * S + s * P:c * S + (s + 1) * P],
                                            gb[:, q, s, c * P:(c + 1) * P], t["ident"][:, :])
            last.then_inc(gbT, 1)
            pe.wait_ge(h1_done, 1)
            pe.wait_ge(w_in["w2"], 16)
            for m in range(HC):
                for k in range(HC):
                    last = pe.matmul(ps[:, 2, m * B:(m + 1) * B], w2[:, k, m * P:(m + 1) * P], h1[:, k, :],
                                     start=(k == 0), stop=(k == HC - 1))
            last.then_inc(h2_mm, 1)
            pe.wait_ge(w_in["wada"], 16)
            pe.wait_ge(silu2_done, 1)
            for k in range(DC):
                last = pe.matmul(ps[0:B, 6, :], silu2[:, k, :], wada[:, k, :], start=(k == 0), stop=(k == DC - 1))
            last.then_inc(ada_mm, 1)
            pe.wait_ge(h2_done, 1)
            pe.wait_ge(w_in["wsc"], 16)
            pe.wait_ge(w_in["wsh"], 16)
            for q, wt in enumerate((wsc, wsh)):
                for m in range(DC):
                    for k in range(HC):
                        last = pe.matmul(ps[:, 3, (q * DC + m) * B:(q * DC + m + 1) * B], wt[:, k, m * P:(m + 1) * P],
                                         h2[:, k, :], start=(k == 0), stop=(k == HC - 1))
            last.then_inc(sc_mm, 1)


def wait_apart(eng, semaphore, count):
    eng.wait_ge(semaphore, count)
    eng.nop(nofuse=True)


def matmul3(pe, out, lhs, rhs, first, last):
    pe.matmul(out, lhs[0], rhs[0], start=first, stop=False)
    pe.matmul(out, lhs[0], rhs[1], start=False, stop=False)
    return pe.matmul(out, lhs[1], rhs[0], start=False, stop=last)


def parts(tile, k, lo, hi):
    return tile[:, 0, k, lo:hi], tile[:, 1, k, lo:hi]


def by_route(eng, route, body):
    with eng.If(route == 0):
        body(0)
    with eng.Else():
        with eng.If(route == 1):
            body(1)
        with eng.Else():
            body(2)


def flat(tile):
    return tile[:, :, :].rearrange("p c s -> p (c s)")


def first_layers(nc, a, t, ps, ada):
    w, vecs, rows = t["w"], t["vecs"], t["rows"]
    XT = MA = 0
    MB = Z = 1
    HIDDEN = (("nr_w1", "nr_b1", DC), ("tsr_w1", "tsr_b1", DC), ("sr_w1", "sr_b1", 4))
    OUTER = (("nr_w2", "nr_b2"), ("tsr_w2", "tsr_b2"), ("sr_w3", "sr_b3"))
    with ExitStack() as ctx:
        def sb(name, shape, dt=F32):
            return ctx.enter_context(nc.sbuf_tensor(name, shape, dt))

        def sem(name):
            return nc.alloc_semaphore(name)

        def per_lane(name, shape, dt=F32):
            return [sb(f"{name}{l}", shape, dt) for l in range(LANES_A)]

        x = per_lane("a_x", [P, TC, D])
        xb = per_lane("a_xb", [P, TC, D])
        f = per_lane("a_f", [P, 4, S])
        v = per_lane("a_v", [P, DC, S])
        y = per_lane("a_y", [P, DC, S])
        x1 = per_lane("a_x1", [P, TC, D])
        part = per_lane("a_part", [P, 2, 4, S], F32R)
        adab = per_lane("a_ada", [P, 2, D])
        st = per_lane("a_st", [P, 2, 8])
        bn = per_lane("a_bn", [P, TC, 6])
        mv = per_lane("a_mv", [P, 2, TC, 2])
        rs = per_lane("a_rs", [P, 2, TC])
        rv = per_lane("a_rv", [P, 2, TC])

        s = {n: sem(f"a_{n}") for n in (
            "xT", "stat_mm0", "stat_mm1", "y_mm", "out0_mm", "x1T", "g_mm", "out1_mm",
            "s0", "hi0", "y", "s1", "hi1", "hi2", "g", "hi3",
            "in0", "ve0", "v0", "lo0", "in1", "ve1", "v1", "lo1", "x1", "lo2", "lo3",
            "ve2", "t1", "ve3", "t2",
            "xb", "rstd0", "rstd1", "xb2", "rstd2", "t1g", "x2", "rstd3", "t2s", "x3")}
        own, OWN = sem("a_vector_own"), 14 * LANES_A
        r = {n: [sem(f"a_{n}_{l}") for l in range(LANES_A)] for n in ("g2_mm", "g2", "hi4", "lo4", "y1")}
        x_in = [sem(f"a_x_in{l}") for l in range(LANES_A)]
        ada_in = [sem(f"a_ada_in{l}") for l in range(LANES_A)]

        def bank(l, i):
            return ps[:, 2 * l + i, :]

        block = ctx.enter_context(nc.Block())

        @block.sync
        def _(sp):
            def load_x(b, l):
                sp.dma_start(x[l][:, :, :], a["x"][b + l].rearrange("(c p) d -> p c d", p=P)).then_inc(x_in[l], 16)

            def load_ada(b, l):
                sp.dma_start(flat(adab[l]), ada[b + l].partition_broadcast(P)).then_inc(ada_in[l], 16)

            for l in range(LANES_A):
                load_x(0, l)
                load_ada(0, l)
            with sp.Fori(1, B // LANES_A) as i:
                b = i * LANES_A
                for l in range(LANES_A):
                    sp.wait_ge(s["xT"], b + (l + 1 - LANES_A))
                    sp.wait_ge(s["in0"], b + (l + 1 - LANES_A))
                    wait_apart(sp, s["xb"], b + (l + 1 - LANES_A))
                    load_x(b, l)
                for l in range(LANES_A):
                    wait_apart(sp, s["x3"], b + (l + 1 - LANES_A))
                    load_ada(b, l)

        @block.tensor
        def _(pe):
            def transposes(l, src, done):
                for c in range(DC):
                    for q in range(TC):
                        last = pe.transpose(bank(l, XT)[:, c * S + q * P:c * S + (q + 1) * P],
                                            src[:, q, c * P:(c + 1) * P], t["ident"][:, :])
                last.then_inc(s[done], 1)

            def to_features(l, name, chunks, nk, done):
                for m in range(chunks):
                    for k in range(nk):
                        last = matmul3(pe, bank(l, (MA, MB)[m // 2])[:, (m % 2) * S:(m % 2 + 1) * S],
                                       parts(w[name], k, m * P, (m + 1) * P), parts(part[l], k, 0, S),
                                       k == 0, k == nk - 1)
                last.then_inc(done, 1)

            def to_rows(l, name, done):
                nk = 4 if name == "sr_w2" else DC
                for q in range(TC):
                    for k in range(nk):
                        last = matmul3(pe, bank(l, Z)[:, q * D:(q + 1) * D], parts(part[l], k, q * P, (q + 1) * P),
                                       parts(w[name], k, 0, D), k == 0, k == nk - 1)
                last.then_inc(s[done], 1)

            with pe.Fori(0, B // LANES_A) as i:
                b = i * LANES_A
                n = [b + (l + 1) for l in range(LANES_A)]
                for l in range(LANES_A):
                    pe.wait_ge(x_in[l], 16 * i + 16)
                    transposes(l, x[l], "xT")
                    pe.wait_ge(s["in0"], n[l])
                    pe.matmul(bank(l, Z)[:, 0:2], t["mean_of"][:, :], st[l][:, 0, 0:2], start=True,
                              stop=True).then_inc(s["stat_mm0"], 1)
                for l in range(LANES_A):
                    pe.wait_ge(s["lo0"], n[l])
                    to_features(l, "W_in", DC, DC, s["y_mm"])
                for l in range(LANES_A):
                    pe.wait_ge(s["in1"], n[l])
                    pe.matmul(bank(l, Z)[:, 0:2], t["mean_of"][:, :], st[l][:, 1, 0:2], start=True,
                              stop=True).then_inc(s["stat_mm1"], 1)
                for l in range(LANES_A):
                    pe.wait_ge(s["lo1"], n[l])
                    to_rows(l, "W_out", "out0_mm")
                for l in range(LANES_A):
                    pe.wait_ge(s["x1"], n[l])
                    transposes(l, x1[l], "x1T")
                route = [pe.value_load(t["cond"][0:1, bass.ds(b + l, 1)]) for l in range(LANES_A)]
                for l in range(LANES_A):
                    pe.wait_ge(s["lo2"], n[l])
                    by_route(pe, route[l], lambda way: to_features(l, HIDDEN[way][0], HIDDEN[way][2], DC, s["g_mm"]))
                for l in range(LANES_A):
                    pe.wait_ge(s["lo3"], n[l])
                    by_route(pe, route[l], lambda way: to_features(l, "sr_w2", DC, 4, r["g2_mm"][l]) if way == 2
                             else pe.sem_inc(r["g2_mm"][l], 1))
                for l in range(LANES_A):
                    pe.wait_ge(r["lo4"][l], i + 1)
                    by_route(pe, route[l], lambda way: to_rows(l, OUTER[way][0], "out1_mm"))

        @block.scalar
        def _(act):
            def silu_high(l, b, s_name, hi_name, n):
                for c in range(DC):
                    last = act.activation(f[l][:, c, :], v[l][:, c, :], ACT.Silu,
                                          scale=t["scale0"][:, c, bass.ds(b + l, 1)],
                                          bias=t["shift0"][:, c, bass.ds(b + l, 1)])
                last.then_inc(s[s_name], 1)
                act.wait_ge(s[s_name], n)
                act.activation(part[l][:, 0, 0:DC, :], f[l][:, 0:DC, :], ACT.Copy).then_inc(s[hi_name], 1)

            def gelus(l, bias, chunks, done):
                for m in range(chunks):
                    last = act.activation(f[l][:, m, :], bank(l, (MA, MB)[m // 2])[:, (m % 2) * S:(m % 2 + 1) * S],
                                          ACT.Gelu, bias=vecs[:, VEC[bias] + m:VEC[bias] + m + 1])
                last.then_inc(done, 1)

            def high(l, chunks, done):
                act.activation(part[l][:, 0, 0:chunks, :], f[l][:, 0:chunks, :], ACT.Copy).then_inc(done, 1)

            with act.Fori(0, B // LANES_A) as i:
                b = i * LANES_A
                n = [b + (l + 1) for l in range(LANES_A)]
                for l in range(LANES_A):
                    wait_apart(act, s["v0"], n[l])
                    silu_high(l, b, "s0", "hi0", n[l])
                for l in range(LANES_A):
                    act.wait_ge(s["y_mm"], n[l])
                    for c in range(DC):
                        last = act.activation(y[l][:, c, :], bank(l, MA)[:, c * S:(c + 1) * S], ACT.Identity,
                                              bias=vecs[:, VEC["L0_b_in"] + c:VEC["L0_b_in"] + c + 1])
                    last.then_inc(s["y"], 1)
                for l in range(LANES_A):
                    wait_apart(act, s["v1"], n[l])
                    silu_high(l, b, "s1", "hi1", n[l])
                for l in range(LANES_A):
                    act.wait_ge(s["x1T"], n[l])
                    act.activation(part[l][:, 0, 0:DC, :].rearrange("p c s -> p (c s)"), bank(l, XT),
                                   ACT.Copy).then_inc(s["hi2"], 1)
                route = [act.value_load(t["cond"][0:1, bass.ds(b + l, 1)]) for l in range(LANES_A)]
                for l in range(LANES_A):
                    wait_apart(act, s["g_mm"], n[l])
                    by_route(act, route[l], lambda way: gelus(l, HIDDEN[way][1], HIDDEN[way][2], s["g"]))
                    wait_apart(act, s["g"], n[l])
                    by_route(act, route[l], lambda way: high(l, HIDDEN[way][2], s["hi3"]))
                for l in range(LANES_A):
                    wait_apart(act, r["g2_mm"][l], i + 1)
                    by_route(act, route[l], lambda way: gelus(l, "sr_b2", DC, r["g2"][l]) if way == 2
                             else act.sem_inc(r["g2"][l], 1))
                    wait_apart(act, r["g2"][l], i + 1)
                    by_route(act, route[l], lambda way: high(l, DC, r["hi4"][l]) if way == 2 else act.sem_inc(r["hi4"][l], 1))

        @block.vector
        def _(dve):
            count = [0]

            def then(ins):
                count[0] += 1
                ins.then_inc(own, 1)
                wait_apart(dve, own, OWN * turn[0] + count[0])

            def low(l, chunks, done):
                dve.tensor_tensor(part[l][:, 1, 0:chunks, :], f[l][:, 0:chunks, :],
                                  part[l][:, 0, 0:chunks, :].bitcast(F32), ALU.subtract).then_inc(done, 1)

            def statistics(l, src, i, n):
                then(dve.bn_stats(bn[l][:, 0, :], src))
                then(dve.bn_aggr(st[l][:, i, 0:2], bn[l][:, 0, :]))
                dve.scalar_tensor_tensor(st[l][:, i, 1:2], st[l][:, i, 0:1], st[l][:, i, 0:1],
                                         st[l][:, i, 1:2], ALU.mult, ALU.add).then_inc(s[f"in{i}"], 1)

            def block_norm(l, src, i, n):
                dve.wait_ge(s[f"stat_mm{i}"], n)
                then(dve.tensor_copy(st[l][:, i, 2:4], bank(l, Z)[:, 0:2]))
                then(dve.scalar_tensor_tensor(st[l][:, i, 4:5], st[l][:, i, 2:3], st[l][:, i, 2:3], st[l][:, i, 3:4],
                                              ALU.mult, ALU.subtract))
                dve.tensor_scalar(st[l][:, i, 5:6], st[l][:, i, 4:5], -1.0, EPS, ALU.mult,
                                  ALU.add).then_inc(s[f"ve{i}"], 1)
                then(dve.scalar_tensor_tensor(flat(v[l]), src, st[l][:, i, 2:3], flat(t["gammaT"]),
                                              ALU.subtract, ALU.mult))
                dve.wait_ge(s[f"rstd{i}"], n)
                dve.scalar_tensor_tensor(flat(v[l]), flat(v[l]), st[l][:, i, 6:7], flat(t["betaT"]),
                                         ALU.mult, ALU.add).then_inc(s[f"v{i}"], 1)

            def token_statistics(l, src, i, n):
                for q in range(TC):
                    last = dve.bn_stats(bn[l][:, q, :], src[:, q, :])
                then(last)
                for q in range(TC):
                    last = dve.bn_aggr(mv[l][:, i - 2, q, :], bn[l][:, q, :])
                then(last)
                dve.tensor_scalar(rv[l][:, i - 2, :], mv[l][:, i - 2, :, 1], EPS, None, ALU.add).then_inc(s[f"ve{i}"], 1)

            def normalise(l, dst, src, i, done):
                for q in range(TC):
                    last = dve.tensor_scalar(dst[:, q, :], src[:, q, :], mv[l][:, i - 2, q, 0:1], rs[l][:, i - 2, q:q + 1],
                                             ALU.subtract, ALU.mult)
                last.then_inc(s[done], 1)

            with dve.Fori(0, B // LANES_A) as i:
                turn = [i]
                b = i * LANES_A
                n = [b + (l + 1) for l in range(LANES_A)]
                for l in range(LANES_A):
                    dve.wait_ge(x_in[l], 16 * i + 16)
                    statistics(l, flat(x[l]), 0, n[l])
                for l in range(LANES_A):
                    dve.wait_ge(s["xT"], n[l])
                    block_norm(l, bank(l, XT), 0, n[l])
                for l in range(LANES_A):
                    dve.wait_ge(s["hi0"], n[l])
                    low(l, DC, s["lo0"])
                for l in range(LANES_A):
                    dve.wait_ge(s["y"], n[l])
                    statistics(l, flat(y[l]), 1, n[l])
                for l in range(LANES_A):
                    block_norm(l, flat(y[l]), 1, n[l])
                for l in range(LANES_A):
                    dve.wait_ge(s["hi1"], n[l])
                    low(l, DC, s["lo1"])
                for l in range(LANES_A):
                    dve.wait_ge(s["out0_mm"], n[l])
                    dve.wait_ge(s["xb"], n[l])
                    dve.tensor_tensor(flat(x1[l]), bank(l, Z), flat(xb[l]), ALU.add).then_inc(s["x1"], 1)
                for l in range(LANES_A):
                    dve.wait_ge(s["hi2"], n[l])
                    dve.tensor_tensor(part[l][:, 1, 0:DC, :].rearrange("p c s -> p (c s)"), bank(l, XT),
                                      part[l][:, 0, 0:DC, :].rearrange("p c s -> p (c s)").bitcast(F32),
                                      ALU.subtract).then_inc(s["lo2"], 1)
                route = [dve.value_load(t["cond"][0:1, bass.ds(b + l, 1)]) for l in range(LANES_A)]
                for l in range(LANES_A):
                    wait_apart(dve, s["hi3"], n[l])
                    by_route(dve, route[l], lambda way: low(l, HIDDEN[way][2], s["lo3"]))
                for l in range(LANES_A):
                    wait_apart(dve, r["hi4"][l], i + 1)
                    by_route(dve, route[l], lambda way: low(l, DC, r["lo4"][l]) if way == 2 else dve.sem_inc(r["lo4"][l], 1))
                for l in range(LANES_A):
                    dve.wait_ge(s["out1_mm"], n[l])
                    wait_apart(dve, s["xb2"], n[l])

                    def add(way):
                        dve.tensor_tensor(flat(x1[l]), bank(l, Z), flat(xb[l]), ALU.add).then_inc(r["y1"][l], 1)

                    def add_or_not(way):
                        if way < 2:
                            add(way)
                            return
                        with dve.If(route[l] == 2):
                            add(way)
                        with dve.Else():
                            dve.sem_inc(r["y1"][l], 1)
                    by_route(dve, route[l], add_or_not)
                    dve.wait_ge(r["y1"][l], i + 1)
                    token_statistics(l, x1[l], 2, n[l])
                for l in range(LANES_A):
                    dve.wait_ge(s["rstd2"], n[l])
                    normalise(l, v[l], x1[l], 2, "t1")
                for l in range(LANES_A):
                    dve.wait_ge(s["x2"], n[l])
                    token_statistics(l, v[l], 3, n[l])
                for l in range(LANES_A):
                    dve.wait_ge(s["rstd3"], n[l])
                    normalise(l, y[l], v[l], 3, "t2")

        @block.gpsimd
        def _(pool):
            def rsqrt(l, dst, src, width, done):
                pool.tensor_tensor(dst, src, t["halves"][:, 0:width], ALU.pow).then_inc(s[done], 1)

            def row(name):
                return rows[:, ROWS[name]:ROWS[name] + 1, :].to_broadcast([P, TC, D])

            with pool.Fori(0, B // LANES_A) as i:
                b = i * LANES_A
                n = [b + (l + 1) for l in range(LANES_A)]
                for l in range(LANES_A):
                    pool.wait_ge(x_in[l], 16 * i + 16)
                    pool.tensor_tensor(xb[l][:, :, :], x[l][:, :, :], row("b_out"), ALU.add).then_inc(s["xb"], 1)
                for l in range(LANES_A):
                    pool.wait_ge(s["ve0"], n[l])
                    rsqrt(l, st[l][:, 0, 6:7], st[l][:, 0, 5:6], 1, "rstd0")
                for l in range(LANES_A):
                    pool.wait_ge(s["ve1"], n[l])
                    rsqrt(l, st[l][:, 1, 6:7], st[l][:, 1, 5:6], 1, "rstd1")
                route = [pool.value_load(t["cond"][0:1, bass.ds(b + l, 1)]) for l in range(LANES_A)]
                for l in range(LANES_A):
                    wait_apart(pool, s["x1"], n[l])
                    by_route(pool, route[l], lambda way: pool.tensor_tensor(
                        xb[l][:, :, :], x1[l][:, :, :], row(OUTER[way][1]), ALU.add).then_inc(s["xb2"], 1))
                for l in range(LANES_A):
                    pool.wait_ge(s["ve2"], n[l])
                    rsqrt(l, rs[l][:, 0, :], rv[l][:, 0, :], TC, "rstd2")
                for l in range(LANES_A):
                    pool.wait_ge(s["t1"], n[l])
                    pool.tensor_tensor(v[l][:, :, :], v[l][:, :, :], row("gamma1"), ALU.mult).then_inc(s["t1g"], 1)
                    pool.wait_ge(s["t1g"], n[l])
                    pool.tensor_tensor(v[l][:, :, :], v[l][:, :, :], row("beta1"), ALU.add).then_inc(s["x2"], 1)
                for l in range(LANES_A):
                    pool.wait_ge(s["ve3"], n[l])
                    rsqrt(l, rs[l][:, 1, :], rv[l][:, 1, :], TC, "rstd3")
                for l in range(LANES_A):
                    pool.wait_ge(s["t2"], n[l])
                    pool.wait_ge(ada_in[l], 16 * i + 16)
                    pool.tensor_tensor(y[l][:, :, :], y[l][:, :, :], adab[l][:, 0:1, :].to_broadcast([P, TC, D]),
                                       ALU.mult).then_inc(s["t2s"], 1)
                    pool.wait_ge(s["t2s"], n[l])
                    pool.tensor_tensor(t["x3"][:, bass.ds(b + l, 1), :, :].rearrange("p o c d -> p (o c) d"), y[l][:, :, :],
                                       adab[l][:, 1:2, :].to_broadcast([P, TC, D]), ALU.add).then_inc(s["x3"], 1)


def attention(nc, a, t, ps):
    w, vecs, rows = t["w"], t["vecs"], t["rows"]
    UNITS = NH // 2 * TC
    GH = 4
    GROUPS = NH // GH
    GU = UNITS // GROUPS
    VW = 3 * HD + 1
    SCORES, BIAS, EXPS, TURNS, PARTS = 5, 4, 3, 2, 1
    PAIRS = B // LANES
    TURN = LANES * UNITS
    SHIFT = 8
    S_BANK, T_BANK, V_BANK, X_BANK = 0, 2, 4, 6
    with ExitStack() as ctx:
        def sb(name, shape, dt=F32):
            return ctx.enter_context(nc.sbuf_tensor(name, shape, dt))

        def sem(name):
            return ctx.enter_context(nc.semaphore(name))

        x_rows = sb("b_x_rows", [P, TC, D])
        x_part = sb("b_x", [P, 2, DC, S], F32R)
        q_part = [sb(f"b_q{l}", [P, 2, DC, S], F32R) for l in range(LANES)]
        k_part = [sb(f"b_k{l}", [P, DC, 2, S], F32R) for l in range(LANES)]
        KM = 4
        k_head = sb("b_k_head", [P, KM, 2, 2, S], F32R)
        v_full = sb("b_v_full", [P, TC, D])
        v_rest = sb("b_v_rest", [P, TC, D])
        v_part = [sb(f"b_v{l}", [P, TC, NH, VW], BF16) for l in range(LANES)]
        bias = sb("b_bias", [P, GROUPS, GH, TC, S])
        mask8 = [sb(f"b_mask8{l}", [P, TC, S], U8) for l in range(LANES)]
        mask = [sb(f"b_mask{l}", [P, TC, S], BF16) for l in range(LANES)]
        masked = sb("b_masked", [P, P], BF16)
        head_rows = sb("b_head_rows", [P, 8])
        NP_ = 4
        prob = sb("b_prob", [P, NP_, 2 * S])
        lowest = sb("b_lowest", [P, NP_, 2])
        pT = sb("b_pT", [P, NP_, 2, 2 * S], F16)
        sums = sb("b_sums", [P, 2, TC * GH, HD])
        recip = sb("b_recip", [P, 2, TC * GH])
        ctx_rows = [sb(f"b_ctx{l}", [P, TC, D]) for l in range(LANES)]
        c_part = sb("b_c", [P, 2, DC, S], F32R)
        FP = (DC * FF + FC * D) // PAIRS
        ff_raw = sb("b_ff_raw", [P, FP])

        q = {n: sem(f"b_{n}") for n in (
            "x_mm", "q_mm", "k_mm", "v_mm", "c_mm", "o_mm", "x_hi", "q_hi", "k_hi", "v_hi", "v_mid", "c_hi",
            "x_lo", "q_lo", "k_lo", "v_full", "v_rest", "v_lo", "c_lo", "x4", "mask", "x3b")}
        score_mm, scored, exped = sem("b_score_mm"), sem("b_scored"), sem("b_exped")
        turned, t_hi, t_lo, applied = sem("b_turned"), sem("b_t_hi"), sem("b_t_lo"), sem("b_applied")
        group_read, normed = sem("b_group_read"), sem("b_normed")
        k_ready = sem("b_k_ready")
        bias_in = [sem(f"b_bias_in{g}") for g in range(GROUPS)]
        x_in = sem("b_x_in")
        mask_in = [sem(f"b_mask_in{l}") for l in range(LANES)]
        once_in, ff_in, once, ff_hi, ff_lo = sem("b_once_in"), sem("b_ff_in"), sem("b_once"), sem("b_ff_hi"), sem("b_ff_lo")
        FREE_KEYS = 2 * KM

        def heads(u):
            return u // TC, u % TC

        def at(i, x):
            return TURN * i + (x + 1)

        def seq(i, x):
            return LANES * i + (x // UNITS + 1)

        def run_slots(eng, slot):
            for k in range(-SCORES, SHIFT):
                slot(k, 0, range(0, B * UNITS))
            with eng.Fori(0, PAIRS - 1) as i:
                for k in range(SHIFT, SHIFT + TURN):
                    slot(k, i, range(-B * UNITS, B * UNITS))
            for k in range(SHIFT, TURN + 8):
                slot(k, PAIRS - 1, range(-B * UNITS, TURN))

        block = ctx.enter_context(nc.Block())

        @block.sync
        def _(sp):
            def load_bias(b, g):
                sp.dma_start(bias[:, g, :, :, :], a["fside_Bx16xSxS_0"][b, g * GH:(g + 1) * GH]
                             .rearrange("h (c p) k -> p h c k", p=P)).then_inc(bias_in[g], 16)

            def load_mask(b, l):
                sp.dma_start(mask8[l][:, :, :], a["mask"][b, 0].rearrange("(c p) k -> p c k", p=P)).then_inc(mask_in[l], 16)

            def copy_x(b):
                sp.dma_start(x_rows[:, :, :].rearrange("p (o c) d -> p o c d", o=1),
                             t["x3"][:, bass.ds(b, 1), :, :]).then_inc(x_in, 16)

            sp.dma_start(head_rows[:, :], a["head_rows"]).then_inc(once_in, 16)
            for l in range(LANES):
                load_mask(l, l)
            copy_x(0)
            for g in range(GROUPS):
                load_bias(0, g)
            sp.dma_start(ff_raw[:, :], a["ff"][:, 0:FP]).then_inc(ff_in, 16)

            def loads(b, more=True):
                if more:
                    wait_apart(sp, q["x_mm"], b + 1)
                    copy_x(b + 1)
                for g in range(GROUPS):
                    wait_apart(sp, scored, 2 * LANES + 2 * (UNITS * (b - 1)) + 2 * GU * (g + 1))
                    load_bias(b, g)

            sp.wait_ge(q["x_mm"], 1)
            copy_x(1)
            with sp.Fori(0, PAIRS - 1) as i:
                for l in range(LANES):
                    loads(LANES * i + (l + 1))
                    wait_apart(sp, q["mask"], LANES * i + (l + 1))
                    load_mask(LANES * i + (l + 2), l)
                wait_apart(sp, ff_lo, i + 1)
                sp.dma_start(ff_raw[:, :], a["ff"][:, bass.ds(FP * i + FP, FP)]).then_inc(ff_in, 16)
            loads(B - 1, more=False)

        @block.tensor
        def _(pe):
            def project(name, src_part, bank, done):
                for m in range(DC):
                    for k in range(DC):
                        last = matmul3(pe, ps[:, bank, m * S:(m + 1) * S], parts(w[name], k, m * P, (m + 1) * P),
                                       parts(src_part, k, 0, S), k == 0, k == DC - 1)
                last.then_inc(done, 1)

            def to_rows(name, src_part, bank, done):
                for c in range(TC):
                    for k in range(DC):
                        last = matmul3(pe, ps[:, bank, c * D:(c + 1) * D], parts(src_part, k, c * P, (c + 1) * P),
                                       parts(w[name], k, 0, D), k == 0, k == DC - 1)
                last.then_inc(done, 1)

            def turn_x(i, x):
                pe.wait_ge(x_in, 16 * seq(i, x))
                if x >= UNITS:
                    pe.wait_ge(q["v_full"], seq(i, x - UNITS))
                for c in range(DC):
                    for r in range(TC):
                        last = pe.transpose(ps[:, X_BANK + 1, c * S + r * P:c * S + (r + 1) * P],
                                            x_rows[:, r, c * P:(c + 1) * P], t["ident"][:, :])
                last.then_inc(q["x_mm"], 1)

            def queries(i, x):
                pe.wait_ge(q["x_lo"], seq(i, x))
                project("Wq", x_part, X_BANK + 1, q["q_mm"])

            def keys(i, x):
                pe.wait_ge(q["q_lo"], seq(i, x))
                project("Wk", x_part, X_BANK + 1, q["k_mm"])

            def values(i, x):
                pe.wait_ge(q["k_lo"], seq(i, x))
                to_rows("Wv", x_part, X_BANK + 1, q["v_mm"])

            def turn_ctx(i, x):
                pe.wait_ge(normed, GROUPS * seq(i, x))
                pe.wait_ge(q["x4"], seq(i, x))
                for k in range(DC):
                    for c in range(TC):
                        last = pe.transpose(ps[:, X_BANK, k * S + c * P:k * S + (c + 1) * P],
                                            ctx_rows[x // UNITS % LANES][:, c, k * P:(k + 1) * P], t["ident"][:, :])
                last.then_inc(q["c_mm"], 1)

            def output(i, x):
                pe.wait_ge(q["c_lo"], seq(i, x))
                to_rows("Wo", c_part, X_BANK, q["o_mm"])

            def scores(i, x):
                u, l = x % UNITS, x // UNITS % LANES
                pair, c = heads(u)
                slot = (x // TC) % KM
                if u == 0:
                    pe.wait_ge(q["mask"], seq(i, x))
                    pe.wait_ge(q["q_lo"], seq(i, x))
                if c == 0:
                    pe.wait_ge(k_ready, (TURN // TC) * i + (x // TC + 1))
                pe.wait_ge(scored, 2 * at(i, x))
                out_ = ps[:, S_BANK + x % 2, :]
                pe.matmul(out_, masked[:, :], mask[l][:, c:c + 1, :].to_broadcast([P, 2, S]), start=True, stop=False)
                chunk = pair // 4
                qh, ql = (q_part[l][:, h, chunk, c * P:(c + 1) * P] for h in range(2))
                kh, kl = (k_head[:, slot, h, :, :].rearrange("p j s -> p (j s)") for h in range(2))
                pe.matmul(out_, qh, kh, start=False, stop=False)
                pe.matmul(out_, qh, kl, start=False, stop=False)
                pe.matmul(out_, ql, kh, start=False, stop=True).then_inc(score_mm, 1)

            def turn(i, x):
                pe.wait_ge(exped, 2 * at(i, x))
                pe.wait_ge(t_lo, at(i, x))
                for j in range(4):
                    last = pe.transpose(ps[:, T_BANK + x % 2, j * P:(j + 1) * P], prob[:, x % NP_, j * P:(j + 1) * P],
                                        t["ident"][:, :])
                last.then_inc(turned, 1)

            def apply(i, x):
                u, l = x % UNITS, x // UNITS % LANES
                pair, c = heads(u)
                g = (x // GU) % 2
                if u == 0:
                    pe.wait_ge(q["v_lo"], seq(i, x))
                if u % GU == 0:
                    pe.wait_ge(group_read, 2 * (TURN // GU) * i + 2 * (x // GU + 1))
                pe.wait_ge(t_lo, at(i, x) + 2)
                for j in range(2):
                    head = 2 * pair + j
                    col = (c * GH + head % GH) * VW
                    for kc in range(TC):
                        for h in range(2):
                            last = pe.matmul(ps[:, V_BANK + g, col:col + VW], pT[:, x % NP_, h, (2 * j + kc) * P:(2 * j + kc + 1) * P],
                                             v_part[l][:, kc, head, :], start=(kc + h == 0), stop=(kc + h == 2))
                last.then_inc(applied, 1)

            def slot(k, i, here):
                s, first = k % UNITS, k // UNITS * UNITS
                if k >= 0 and first + UNITS in here:
                    for when, what in ((0, turn_x), (3, queries), (6, keys), (8, values)):
                        if s == when:
                            what(i, first + UNITS)
                if k >= 0 and first - UNITS in here:
                    for when, what in ((2, turn_ctx), (5, output)):
                        if s == when:
                            what(i, first - UNITS)
                if k + TURNS in here:
                    turn(i, k + TURNS)
                if k + SCORES in here:
                    scores(i, k + SCORES)
                if k in here:
                    apply(i, k)

            pe.wait_ge(once, 3)
            for what in (turn_x, queries, keys, values):
                what(0, 0)
            run_slots(pe, slot)

        @block.scalar
        def _(act):
            def high(dst, src, wait, n, done):
                act.wait_ge(wait, n)
                act.activation(dst, src, ACT.Copy).then_inc(done, 1)

            def x_high(i, x):
                high(x_part[:, 0, :, :].rearrange("p c s -> p (c s)"), ps[:, X_BANK + 1, :], q["x_mm"], seq(i, x), q["x_hi"])

            def ctx_high(i, x):
                high(c_part[:, 0, :, :].rearrange("p c s -> p (c s)"), ps[:, X_BANK, :], q["c_mm"], seq(i, x), q["c_hi"])

            def q_high(i, x):
                act.wait_ge(q["q_mm"], seq(i, x))
                for m in range(DC):
                    last = act.activation(q_part[x // UNITS % LANES][:, 0, m, :], ps[:, X_BANK + 1, m * S:(m + 1) * S],
                                          ACT.Identity, bias=vecs[:, VEC["bq"] + m:VEC["bq"] + m + 1])
                last.then_inc(q["q_hi"], 1)

            def k_high(i, x):
                act.wait_ge(q["k_mm"], seq(i, x))
                for m in range(DC):
                    last = act.activation(k_part[x // UNITS % LANES][:, m, 0, :], ps[:, X_BANK + 1, m * S:(m + 1) * S],
                                          ACT.Identity, bias=vecs[:, VEC["bk"] + m:VEC["bk"] + m + 1])
                last.then_inc(q["k_hi"], 1)

            def v_slices(l, s):
                return v_part[l][:, :, :, s * HD:(s + 1) * HD]

            def v_high(i, x):
                act.wait_ge(q["v_full"], seq(i, x))
                act.activation(v_slices(x // UNITS % LANES, 0), v_full[:, :, :].rearrange("p c (h d) -> p c h d", d=HD),
                               ACT.Copy).then_inc(q["v_hi"], 1)

            def v_middle(i, x):
                act.wait_ge(q["v_rest"], seq(i, x))
                act.activation(v_slices(x // UNITS % LANES, 1), v_rest[:, :, :].rearrange("p c (h d) -> p c h d", d=HD),
                               ACT.Copy).then_inc(q["v_mid"], 1)

            def exps(i, x):
                r = x % NP_
                for j in range(2):
                    act.wait_ge(scored, 2 * at(i, x) + (3 + j))
                    act.activation(prob[:, r, j * S:(j + 1) * S], prob[:, r, j * S:(j + 1) * S], ACT.Exp,
                                   bias=lowest[:, r, j:j + 1], scale=-1.0).then_inc(exped, 1)

            def turned_high(i, x):
                act.wait_ge(turned, at(i, x) + NP_)
                act.wait_ge(applied, at(i, x))
                act.activation(pT[:, x % NP_, 0, :], ps[:, T_BANK + x % 2, :], ACT.Copy).then_inc(t_hi, 1)

            def slot(k, i, here):
                s, first = k % UNITS, k // UNITS * UNITS
                if k + PARTS in here:
                    turned_high(i, k + PARTS)
                if k + EXPS in here:
                    exps(i, k + EXPS)
                if k >= 0 and first + UNITS in here:
                    for when, what in ((0, x_high), (3, q_high), (6, k_high), (10, v_high), (12, v_middle)):
                        if s == when:
                            what(i, first + UNITS)
                if k >= 0 and first - UNITS in here and s == 2:
                    ctx_high(i, first - UNITS)

            for what in (x_high, q_high, k_high, v_high, v_middle):
                what(0, 0)
            run_slots(act, slot)

        @block.vector
        def _(dve):
            dve.sem_inc(scored, 4)
            dve.sem_inc(t_lo, 2)
            dve.sem_inc(group_read, 4)
            dve.sem_inc(q["x4"], 1)

            def x_low(i, x):
                dve.wait_ge(q["x_hi"], seq(i, x))
                dve.tensor_tensor(x_part[:, 1, :, :].rearrange("p c s -> p (c s)"), ps[:, X_BANK + 1, :],
                                  x_part[:, 0, :, :].rearrange("p c s -> p (c s)").bitcast(F32),
                                  ALU.subtract).then_inc(q["x_lo"], 1)

            def ctx_low(i, x):
                dve.wait_ge(q["c_hi"], seq(i, x))
                dve.tensor_tensor(c_part[:, 1, :, :].rearrange("p c s -> p (c s)"), ps[:, X_BANK, :],
                                  c_part[:, 0, :, :].rearrange("p c s -> p (c s)").bitcast(F32),
                                  ALU.subtract).then_inc(q["c_lo"], 1)

            def q_low(i, x):
                dve.wait_ge(q["q_hi"], seq(i, x))
                part = q_part[x // UNITS % LANES]
                for m in range(DC):
                    last = dve.scalar_tensor_tensor(part[:, 1, m, :], ps[:, X_BANK + 1, m * S:(m + 1) * S],
                                                    vecs[:, VEC["bq"] + m:VEC["bq"] + m + 1], part[:, 0, m, :].bitcast(F32),
                                                    ALU.add, ALU.subtract)
                last.then_inc(q["q_lo"], 1)

            def k_low(i, x):
                dve.wait_ge(q["k_hi"], seq(i, x))
                part = k_part[x // UNITS % LANES]
                for m in range(DC):
                    last = dve.scalar_tensor_tensor(part[:, m, 1, :], ps[:, X_BANK + 1, m * S:(m + 1) * S],
                                                    vecs[:, VEC["bk"] + m:VEC["bk"] + m + 1], part[:, m, 0, :].bitcast(F32),
                                                    ALU.add, ALU.subtract)
                last.then_inc(q["k_lo"], 1)

            def v_whole(i, x):
                dve.wait_ge(q["v_mm"], seq(i, x))
                dve.tensor_tensor(v_full[:, :, :], ps[:, X_BANK + 1, :].rearrange("p (c d) -> p c d", c=TC),
                                  rows[:, ROWS["bv"]:ROWS["bv"] + 1, :].to_broadcast([P, TC, D]), ALU.add).then_inc(q["v_full"], 1)

            def by_head(tile):
                return tile[:, :, :].rearrange("p c (h d) -> p c h d", d=HD)

            def v_remainder(i, x):
                dve.wait_ge(q["v_hi"], seq(i, x))
                dve.tensor_tensor(by_head(v_rest), by_head(v_full), v_part[x // UNITS % LANES][:, :, :, 0:HD],
                                  ALU.subtract).then_inc(q["v_rest"], 1)

            def v_low(i, x):
                dve.wait_ge(q["v_mid"], seq(i, x))
                part = v_part[x // UNITS % LANES]
                dve.tensor_tensor(part[:, :, :, 2 * HD:3 * HD], by_head(v_rest), part[:, :, :, HD:2 * HD],
                                  ALU.subtract).then_inc(q["v_lo"], 1)

            def residual(i, x):
                dve.wait_ge(q["o_mm"], seq(i, x))
                dve.wait_ge(q["x3b"], seq(i, x))
                x4 = t["x3"][:, bass.ds(LANES * i + x // UNITS, 1), :, :].rearrange("p o c d -> p (o c) d")
                dve.tensor_tensor(x4, ps[:, X_BANK, :].rearrange("p (c d) -> p c d", c=TC), x4, ALU.add).then_inc(q["x4"], 1)

            def add_bias(i, x):
                u = x % UNITS
                pair, c = heads(u)
                r = x % NP_
                dve.wait_ge(score_mm, at(i, x) + FREE_KEYS)
                if u % GU == 0:
                    dve.wait_ge(bias_in[u // GU], 16 * seq(i, x))
                wait_apart(dve, turned, at(i, x))
                for j in range(2):
                    dve.tensor_tensor_reduce(prob[:, r, j * S:(j + 1) * S], ps[:, S_BANK + x % 2, j * S:(j + 1) * S],
                                             bias[:, u // GU, 2 * (pair % 2) + j, c, :], -1.0, 3.0e38, ALU.add, ALU.min,
                                             lowest[:, r, j:j + 1]).then_inc(scored, 1)

            def turned_low(i, x):
                dve.wait_ge(t_hi, at(i, x))
                dve.tensor_tensor(pT[:, x % NP_, 1, :], ps[:, T_BANK + x % 2, :], pT[:, x % NP_, 0, :],
                                  ALU.subtract).then_inc(t_lo, 1)

            def sum_group(i, x):
                g = (x // GU) % 2
                res = ps[:, V_BANK + g, 0:TC * GH * VW].rearrange("p (e f) -> p e f", f=VW)
                dve.wait_ge(applied, at(i, x) + NP_)
                dve.tensor_reduce(sums[:, g, :, :], res[:, :, 0:3 * HD].rearrange("p e (s d) -> p e d s", d=HD), AX.X,
                                  ALU.add).then_inc(group_read, 1)
                dve.reciprocal(recip[:, g, :], res[:, :, 3 * HD]).then_inc(group_read, 1)

            def norm_group(i, x):
                u, l, g = x % UNITS, x // UNITS % LANES, (x // GU) % 2
                dve.wait_ge(group_read, 2 * (TURN // GU) * i + (2 * (x // GU + 1) + 4))
                at_ = u // GU * GH * HD
                for c in range(TC):
                    last = dve.tensor_tensor(ctx_rows[l][:, c, at_:at_ + GH * HD].rearrange("p (h d) -> p h d", d=HD),
                                             sums[:, g, c * GH:(c + 1) * GH, :],
                                             recip[:, g, c * GH:(c + 1) * GH].rearrange("p (e o) -> p e o", o=1)
                                             .to_broadcast([P, GH, HD]), ALU.mult)
                last.then_inc(normed, 1)

            def slot(k, i, here):
                s, first = k % UNITS, k // UNITS * UNITS
                if k % GU == 0 and k - 1 in here:
                    sum_group(i, k - 1)
                if k + BIAS in here:
                    add_bias(i, k + BIAS)
                if k % GU == 0 and k - 1 in here:
                    norm_group(i, k - 1)
                if k + PARTS in here:
                    turned_low(i, k + PARTS)
                if k >= 0 and first + UNITS in here:
                    for when, what in ((1, x_low), (4, q_low), (7, k_low), (9, v_whole), (11, v_remainder), (13, v_low)):
                        if s == when:
                            what(i, first + UNITS)
                if k >= 0 and first - UNITS in here:
                    for when, what in ((3, ctx_low), (6, residual)):
                        if s == when:
                            what(i, first - UNITS)

            for what in (x_low, q_low, k_low, v_whole, v_remainder, v_low):
                what(0, 0)
            run_slots(dve, slot)

        @block.gpsimd
        def _(pool):
            pool.wait_ge(once_in, 16)
            for l in range(LANES):
                pool.memset(v_part[l][:, :, :, 3 * HD:VW], 1.0).then_inc(once, 1)
            pool.tensor_scalar(masked[:, :], t["ident"][:, :], MASKED, 0.0, ALU.mult, ALU.add).then_inc(once, 1)

            def mask_bits(i, l):
                wait_apart(pool, mask_in[l], 16 * i + 16)
                pool.tensor_copy(mask[l][:, :, :], mask8[l][:, :, :]).then_inc(q["mask"], 1)

            pool.sem_inc(score_mm, FREE_KEYS)
            pool.sem_inc(applied, NP_)
            pool.sem_inc(turned, NP_)
            with pool.Fori(0, PAIRS) as i:
                for l in range(LANES):
                    n = LANES * i + (l + 1)
                    pool.wait_ge(score_mm, TURN * i + (UNITS * (l - 1) + FREE_KEYS) if l else TURN * i + 1)
                    mask_bits(i, l)
                    pool.wait_ge(q["x_mm"], n)
                    x3 = t["x3"][:, bass.ds(LANES * i + l, 1), :, :].rearrange("p o c d -> p (o c) d")
                    pool.tensor_tensor(x3, x3, rows[:, ROWS["bo"]:ROWS["bo"] + 1, :].to_broadcast([P, TC, D]),
                                       ALU.add).then_inc(q["x3b"], 1)
                    wait_apart(pool, q["k_lo"], n)
                    for pair in range(NH // 2):
                        wait_apart(pool, score_mm, TURN * i + (UNITS * l + 2 * pair + 2))
                        for j in range(2):
                            head = (2 * pair + j) % 8
                            last = pool.tensor_scalar(k_head[:, pair % KM, :, j, :], k_part[l][:, pair // 4, :, :],
                                                      head_rows[:, head:head + 1], 0.0, ALU.mult, ALU.add)
                        last.then_inc(k_ready, 1)
                wait_apart(pool, ff_in, 16 * i + 16)
                eighth = bass.ds(FP * i, FP)
                pool.tensor_copy(t["ff"][:, 0, eighth], ff_raw[:, :]).then_inc(ff_hi, 1)
                pool.wait_ge(ff_hi, i + 1)
                pool.tensor_tensor(t["ff"][:, 1, eighth], ff_raw[:, :], t["ff"][:, 0, eighth].bitcast(F32),
                                   ALU.subtract).then_inc(ff_lo, 1)


def feed_forward(nc, a, t, ps, out):
    vecs, rows = t["vecs"], t["rows"]
    w1 = t["ff"][:, :, 0:DC * FF].rearrange("p h (k m) -> p h k m", m=FF)
    w2 = t["ff"][:, :, DC * FF:].rearrange("p h (k m) -> p h k m", m=D)
    BANKS = FC // 2
    PAIRS = B // LANES
    with ExitStack() as ctx:
        def per_lane(name, shape, dt=F32):
            return [ctx.enter_context(nc.sbuf_tensor(f"{name}{l}", shape, dt)) for l in range(LANES)]

        def sem(name):
            return ctx.enter_context(nc.semaphore(name))

        norm = per_lane("c_norm", [P, TC, D])
        h = per_lane("c_h", [P, DC, S])
        h_part = per_lane("c_h_part", [P, 2, DC, S], F32R)
        act_ = per_lane("c_act", [P, FC, S])
        a_part = per_lane("c_act_part", [P, 2, FC, S], F32R)
        x5 = per_lane("c_x5", [P, TC, D])
        rot1 = per_lane("c_rot1", [P, TC, D])
        rot2 = per_lane("c_rot2", [P, TC, D])
        bn = per_lane("c_bn", [P, TC, 6])
        mv = per_lane("c_mv", [P, TC, 2])
        rv = per_lane("c_rv", [P, TC])
        rs = per_lane("c_rs", [P, TC])
        s = {n: sem(f"c_{n}") for n in ("own", "ve", "rstd", "norm", "normT", "h", "h_hi", "h_lo", "out_mm", "x4b",
                                        "x5", "rot1", "rot2", "rotated")}
        ff_mm, ff_act, ff_hi, ff_lo = sem("c_ff_mm"), sem("c_ff_act"), sem("c_ff_hi"), sem("c_ff_lo")
        stored = [sem(f"c_stored{l}") for l in range(LANES)]

        def bank(l, j):
            return ps[:, BANKS * l + j, :]

        def x4(i, l):
            return t["x3"][:, bass.ds(LANES * i + l, 1), :, :].rearrange("p o c d -> p (o c) d")

        def turns(eng, prepare, work):
            for l in range(LANES):
                prepare(0, l)
            with eng.Fori(0, PAIRS - 1) as i:
                work(i, lambda l: prepare(i + 1, l))
            work(PAIRS - 1, lambda l: None)

        block = ctx.enter_context(nc.Block())

        @block.sync
        def _(sp):
            with sp.Fori(0, PAIRS) as i:
                for l in range(LANES):
                    wait_apart(sp, s["rotated"], LANES * i + (l + 1))
                    sp.dma_start(out[LANES * i + l].rearrange("(c p) d -> p c d", p=P), rot1[l][:, :, :]).then_inc(stored[l], 16)
            for l in range(LANES):
                sp.wait_ge(stored[l], 16 * PAIRS + 16)

        @block.tensor
        def _(pe):
            def prepare(i, l):
                pe.wait_ge(s["norm"], LANES * i + (l + 1))
                for c in range(DC):
                    for r in range(TC):
                        last = pe.transpose(bank(l, 1)[:, c * S + r * P:c * S + (r + 1) * P], norm[l][:, r, c * P:(c + 1) * P],
                                            t["ident"][:, :])
                last.then_inc(s["normT"], 1)

            def work(i, next_):
                n = [LANES * i + (l + 1) for l in range(LANES)]
                for l in range(LANES):
                    pe.wait_ge(s["h_lo"], n[l])
                    for m in range(FC):
                        for k in range(DC):
                            last = matmul3(pe, bank(l, m // 2)[:, (m % 2) * S:(m % 2 + 1) * S], parts(w1, k, m * P, (m + 1) * P),
                                           parts(h_part[l], k, 0, S), k == 0, k == DC - 1)
                        if m % 2:
                            last.then_inc(ff_mm, 1)
                for l in range(LANES):
                    for c in range(TC):
                        for k in range(FC):
                            if c == 0 and k % 2 == 0:
                                pe.wait_ge(ff_lo, BANKS * LANES * i + (BANKS * l + k // 2 + 1))
                            last = matmul3(pe, bank(l, 0)[:, c * D:(c + 1) * D], parts(a_part[l], k, c * P, (c + 1) * P),
                                           parts(w2, k, 0, D), k == 0, k == FC - 1)
                    last.then_inc(s["out_mm"], 1)
                    next_(l)
            turns(pe, prepare, work)

        @block.scalar
        def _(act):
            def prepare(i, l):
                n = LANES * i + (l + 1)
                act.wait_ge(s["normT"], n)
                for c in range(DC):
                    last = act.activation(h[l][:, c, :], bank(l, 1)[:, c * S:(c + 1) * S], ACT.Identity,
                                          bias=vecs[:, VEC["beta2"] + c:VEC["beta2"] + c + 1],
                                          scale=vecs[:, VEC["g2"] + c:VEC["g2"] + c + 1])
                last.then_inc(s["h"], 1)
                act.wait_ge(s["h"], n)
                act.activation(h_part[l][:, 0, :, :], h[l][:, :, :], ACT.Copy).then_inc(s["h_hi"], 1)

            def work(i, next_):
                for l in range(LANES):
                    for j in range(BANKS):
                        n = BANKS * LANES * i + (BANKS * l + j + 1)
                        act.wait_ge(ff_mm, n)
                        for m in (2 * j, 2 * j + 1):
                            last = act.activation(act_[l][:, m, :], bank(l, j)[:, (m % 2) * S:(m % 2 + 1) * S],
                                                  ACT.Gelu_apprx_sigmoid, bias=vecs[:, VEC["ff_b1"] + m:VEC["ff_b1"] + m + 1])
                        last.then_inc(ff_act, 1)
                        act.wait_ge(ff_act, n)
                        act.activation(a_part[l][:, 0, 2 * j:2 * j + 2, :], act_[l][:, 2 * j:2 * j + 2, :],
                                       ACT.Copy).then_inc(ff_hi, 1)
                for l in range(LANES):
                    next_(l)
            turns(act, prepare, work)

        @block.vector
        def _(dve):
            def normalised(i, l):
                n = LANES * i + (l + 1)
                for r in range(TC):
                    last = dve.bn_stats(bn[l][:, r, :], t["x3"][:, bass.ds(LANES * i + l, 1), r, :].rearrange("p o d -> p (o d)"))
                last.then_inc(s["own"], 1)
                wait_apart(dve, s["own"], 2 * LANES * i + (2 * l + 1))
                for r in range(TC):
                    last = dve.bn_aggr(mv[l][:, r, :], bn[l][:, r, :])
                last.then_inc(s["own"], 1)
                dve.wait_ge(s["own"], 2 * LANES * i + (2 * l + 2))
                dve.tensor_scalar(rv[l][:, :], mv[l][:, :, 1], EPS, None, ALU.add).then_inc(s["ve"], 1)
                dve.wait_ge(s["rstd"], n)
                for r in range(TC):
                    last = dve.tensor_scalar(norm[l][:, r, :], t["x3"][:, bass.ds(LANES * i + l, 1), r, :].rearrange("p o d -> p (o d)"),
                                             mv[l][:, r, 0:1], rs[l][:, r:r + 1], ALU.subtract, ALU.mult)
                last.then_inc(s["norm"], 1)

            def low(i, l):
                n = LANES * i + (l + 1)
                dve.wait_ge(s["h_hi"], n)
                dve.tensor_tensor(h_part[l][:, 1, :, :], h[l][:, :, :], h_part[l][:, 0, :, :].bitcast(F32),
                                  ALU.subtract).then_inc(s["h_lo"], 1)

            def prepare(i, l):
                normalised(i, l)
                if isinstance(i, int):
                    low(i, l)

            def work(i, next_):
                for l in range(LANES):
                    for j in range(BANKS):
                        dve.wait_ge(ff_hi, BANKS * LANES * i + (BANKS * l + j + 1))
                        dve.tensor_tensor(a_part[l][:, 1, 2 * j:2 * j + 2, :], act_[l][:, 2 * j:2 * j + 2, :],
                                          a_part[l][:, 0, 2 * j:2 * j + 2, :].bitcast(F32), ALU.subtract).then_inc(ff_lo, 1)
                for l in range(LANES):
                    next_(l)
                for l in range(LANES):
                    n = LANES * i + (l + 1)
                    dve.wait_ge(s["out_mm"], n)
                    dve.wait_ge(s["x4b"], n)
                    if isinstance(i, int):
                        dve.wait_ge(s["rotated"], LANES * (i - 1) + (l + 1))
                    dve.tensor_tensor(x5[l][:, :, :], bank(l, 0).rearrange("p (c d) -> p c d", c=TC), x4(i, l),
                                      ALU.add).then_inc(s["x5"], 1)
                    if not isinstance(i, int):
                        low(i + 1, l)
            turns(dve, prepare, work)

        @block.gpsimd
        def _(pool):
            def prepare(i, l):
                n = LANES * i + (l + 1)
                pool.wait_ge(s["ve"], n)
                pool.tensor_tensor(rs[l][:, :], rv[l][:, :], t["halves"][:, 0:TC], ALU.pow).then_inc(s["rstd"], 1)
                pool.wait_ge(s["norm"], n)
                pool.tensor_tensor(x4(i, l), x4(i, l), rows[:, ROWS["ff_b2"]:ROWS["ff_b2"] + 1, :].to_broadcast([P, TC, D]),
                                   ALU.add).then_inc(s["x4b"], 1)

            def work(i, next_):
                for l in range(LANES):
                    next_(l)
                for l in range(LANES):
                    n = LANES * i + (l + 1)
                    fours = [tile[:, :, :].rearrange("p c (g j) -> p (c g) j", j=4) for tile in (x5[l], rot1[l], rot2[l])]
                    pool.wait_ge(s["x5"], n)
                    pool.wait_ge(stored[l], 16 * i + 16)
                    pool.tensor_tensor(fours[1], fours[0], t["rot"][:, 0, bass.ds(LANES * i + l, 1), :]
                                       .to_broadcast([P, TC * D // 4, 4]), ALU.mult).then_inc(s["rot1"], 1)
                    for j in range(4):
                        last = pool.tensor_tensor(fours[2][:, :, j:j + 1], fours[0][:, :, (j ^ 1):(j ^ 1) + 1],
                                                  t["rot"][:, 1, bass.ds(LANES * i + l, 1), j:j + 1]
                                                  .to_broadcast([P, TC * D // 4, 1]), ALU.mult)
                    last.then_inc(s["rot2"], 1)
                    pool.wait_ge(s["rot1"], n)
                    pool.wait_ge(s["rot2"], n)
                    pool.tensor_tensor(rot1[l][:, :, :], rot1[l][:, :, :], rot2[l][:, :, :], ALU.add).then_inc(s["rotated"], 1)
            for l in range(LANES):
                pool.sem_inc(stored[l], 16)
            turns(pool, prepare, work)


_VEC_ORDER = ("L0_cond_b1", "L0_cond_b2", "L0_cond_bsc", "L0_cond_bsh", "L0_cond_b_in", "L1_cond_b1_nr", "L1_cond_b1_tsr",
              "L1_cond_b1_sr", "L1_cond_b2_sr", "L2_cond_bq", "L2_cond_bk", "L2_cond_b1", "L2_cond_g2", "L2_cond_beta2")
_ROW_ORDER = ("L0_cond_b_out", "L1_cond_b2_nr", "L1_cond_b2_tsr", "L1_cond_b3_sr", "L1_cond_gamma", "L1_cond_beta",
              "L2_cond_bv", "L2_cond_bo", "L2_cond_b2")
_WEIGHTS = {"W_in": "L0_cond_W_in", "W_out": "L0_cond_W_out", "nr_w1": "L1_cond_w1_nr", "nr_w2": "L1_cond_w2_nr",
            "tsr_w1": "L1_cond_w1_tsr", "tsr_w2": "L1_cond_w2_tsr", "sr_w1": "L1_cond_w1_sr", "sr_w2": "L1_cond_w2_sr",
            "sr_w3": "L1_cond_w3_sr", "Wq": "L2_cond_Wq", "Wk": "L2_cond_Wk", "Wv": "L2_cond_Wv", "Wo": "L2_cond_Wo"}
_AS_THEY_ARE = ("x", "condB_t", "itok_B_0_2", "itok_B_34_63", "fside_Bx16xSxS_0", "condB_theta", "condB_phi",
                "L0_cond_W1", "L0_cond_W2", "L0_cond_Wsc", "L0_cond_Wsh", "L0_cond_gamma", "L0_cond_beta",
                "L2_cond_W_ada", "L2_cond_b_ada")


def constants():
    def freqs(half):
        return np.exp(np.arange(half, dtype=np.float32) * np.float32(-np.log(10000.0) / (half - 1)))
    consts = np.zeros((P, 4), np.float32)
    consts[:, 0] = np.tile(freqs(E0 // 2), 2)
    consts[:, 1] = freqs(D // 2)
    consts[E0 // 2:, 2] = 0.25
    consts[E0 // 2:, 3] = np.pi / 2
    odd = np.zeros((P, 8), np.float32)
    for head in range(8):
        odd[head * HD:(head + 1) * HD, head] = 1.0
    return {"ident": np.eye(P, dtype=np.float32), "consts": consts, "head_rows": odd}


def by_partition(weight):
    k, m = weight.shape
    return weight.reshape(k // P, P, m).transpose(1, 0, 2).reshape(P, k // P * m)


def laid_out(inputs):
    arrays = {n: np.ascontiguousarray(inputs[n]) for n in _AS_THEY_ARE}
    arrays |= {n: np.ascontiguousarray(inputs[src]) for n, src in _WEIGHTS.items()}
    arrays["vec_rows"] = np.concatenate([np.asarray(inputs[n]) for n in _VEC_ORDER]).reshape(-1, P)
    arrays["rows"] = np.concatenate([np.asarray(inputs[n]) for n in _ROW_ORDER])
    arrays["mask"] = np.ascontiguousarray(inputs["mask_Bx1xSxS_bk0"])
    arrays["ff"] = np.concatenate([by_partition(np.asarray(inputs[n])) for n in ("L2_cond_W1", "L2_cond_W2")], axis=1)
    return arrays | constants()


def kernel(**inputs):
    import concourse.bacc as bacc
    from concourse.bass_utils import run_bass_kernel_spmd as run

    arrays = laid_out(inputs)
    nc = bacc.Bacc("TRN2", target_bir_lowering=False, num_devices=1)
    a = {n: nc.dram_tensor(f"in_{n}", v.shape, mybir.dt.from_np(v.dtype), kind="ExternalInput").ap()
         for n, v in arrays.items()}
    out = nc.dram_tensor("out", (B, S, D), F32, kind="ExternalOutput").ap()
    build_program(nc, a, out)
    r = run(nc, [{f"in_{n}": v for n, v in arrays.items()}], core_ids=[0])
    return r.results[0]["out"]
```

```python
from contextlib import ExitStack

import numpy as np
import concourse.bass as bass
from concourse import mybir

F32 = mybir.dt.float32
F32R = mybir.dt.float32r
BF16 = mybir.dt.bfloat16
F16 = mybir.dt.float16
I32 = mybir.dt.int32
U8 = mybir.dt.uint8
ALU = mybir.AluOpType
ACT = mybir.ActivationFunctionType
AX = mybir.AxisListType

P = 128
B = 16
S = 256
D = 256
TC = S // P
DC = D // P
E0 = 128
EH = 4 * E0
HC = EH // P
FF = 1024
FC = FF // P
NH = 16
HD = D // NH
LANES_A = 4
TURN_SLOTS = 60
SLOT = (0, 0, 2, 7, 12, 13, 16, 18, 18, 23, 24, 24, 34, 35, 38, 40, 44, 49, 50, 53, 54, 55, 55, 55, 56)
LANES = 2
EPS = 1e-5
TWO_PI = 2.0 * np.pi
PI_A = 6.28125
PI_B = float(np.float32(np.floor((TWO_PI - PI_A) * 2 ** 21) / 2 ** 21))
PI_C = float(TWO_PI - PI_A - PI_B)
ROUND = float(3 * 2 ** 22)
SIN_EDGE = 3.1415925
MASKED = -float(2.0 ** 100)

VEC = {}
_at = 0
for _name, _n in (("L0_b1", HC), ("L0_b2", HC), ("L0_bsc", DC), ("L0_bsh", DC), ("L0_b_in", DC),
                  ("nr_b1", DC), ("tsr_b1", DC), ("sr_b1", 4), ("sr_b2", DC),
                  ("bq", DC), ("bk", DC), ("ff_b1", FC), ("g2", DC), ("beta2", DC)):
    VEC[_name] = _at
    _at += _n
NVEC = _at
ROWS = {n: i for i, n in enumerate(("b_out", "nr_b2", "tsr_b2", "sr_b3", "gamma1", "beta1", "bv", "bo", "ff_b2"))}


def weight_shapes():
    first = [("W_in", DC, D), ("W_out", DC, D), ("nr_w1", DC, D), ("nr_w2", DC, D), ("tsr_w1", DC, D),
             ("tsr_w2", DC, D), ("sr_w1", DC, 2 * D), ("sr_w2", 4, D), ("sr_w3", DC, D)]
    second = [("Wq", DC, D), ("Wk", DC, D), ("Wv", DC, D), ("Wo", DC, D)]
    return first, second


def build_program(nc, a, out):
    with ExitStack() as whole:
        def sb(name, shape, dt=F32, ctx=whole):
            return ctx.enter_context(nc.sbuf_tensor(name, shape, dt))

        first, second = weight_shapes()
        t = dict(
            w={n: sb(f"w_{n}", [P, 2, k, m], F32R) for n, k, m in second},
            x3=sb("x3", [P, B, TC, D]),
            ident=sb("ident", [P, P]),
            vecs=sb("vecs", [P, NVEC]),
            rows=sb("rows", [P, len(ROWS), D]),
            rot=sb("rot", [P, 2, B, 4]),
            halves=sb("halves", [P, 2]),
        )
        ps = whole.enter_context(nc.psum_tensor("ps", [P, 8, 512], F32))
        ada = nc.dram_tensor("ada_scratch", [B, 2 * D], F32, kind="Internal").ap()
        with ExitStack() as ctx:
            t["w"] |= {n: sb(f"w_{n}", [P, k, m], ctx=ctx) for n, k, m in first}
            t |= dict(
                mean_of=sb("mean_of", [P, P], ctx=ctx),
                scale0=sb("scale0", [P, DC, B], ctx=ctx),
                shift0=sb("shift0", [P, DC, B], ctx=ctx),
                gammaT=sb("gammaT", [P, DC, S], ctx=ctx),
                betaT=sb("betaT", [P, DC, S], ctx=ctx),
                cond=sb("cond", [1, B], I32, ctx),
            )
            with nc.cleanup_on_exit():
                conditioning(nc, a, t, ps, ada, second, first)
            with nc.cleanup_on_exit():
                first_layers(nc, a, t, ps, ada)
        with ExitStack() as ctx:
            t["ff"] = sb("w_ff", [P, 2, DC * FF + FC * D], F32R, ctx)
            attention(nc, a, t, ps)
            feed_forward(nc, a, t, ps, out)


def conditioning(nc, a, t, ps, ada, split, whole):
    w = t["w"]
    with ExitStack() as ctx:
        def sb(name, shape, dt=F32):
            return ctx.enter_context(nc.sbuf_tensor(name, shape, dt))

        def sem(name):
            return nc.alloc_semaphore(name)

        NST = 4
        stage = sb("p_stage", [P, NST, 1024])
        w1 = sb("p_w1", [P, 1, EH])
        w2 = sb("p_w2", [P, HC, EH])
        wsc = sb("p_wsc", [P, HC, D])
        wsh = sb("p_wsh", [P, HC, D])
        wada = sb("p_wada", [P, DC, 2 * D])
        vec_rows = sb("p_vec_rows", [NVEC, P])
        gb = sb("p_gb", [P, 2, TC, D])
        bada = sb("p_bada", [B, 2 * D])
        consts = sb("p_consts", [P, 4])
        tb = sb("p_tb", [P, B])
        ti = sb("p_ti", [P, B], I32)
        dv = sb("p_divide", [P, 6, B])
        NA = 7 * B
        arg = sb("p_arg", [P, NA])
        turn = sb("p_turn", [P, NA])
        red = sb("p_red", [P, NA])
        trig = sb("p_trig", [P, NA])
        silu2 = sb("p_silu2", [P, 2, B])
        h1 = sb("p_h1", [P, HC, B])
        h2 = sb("p_h2", [P, HC, B])
        ada_rows = sb("p_ada_rows", [B, 2 * D])

        consts_in = sem("p_consts_in")
        vecs_in = sem("p_vecs_in")
        rows_in = sem("p_rows_in")
        whole_in = sem("p_whole_in")
        gb_in = sem("p_gb_in")
        w_in = {n: sem(f"p_in_{n}") for n in ("w1", "w2", "wsc", "wsh", "wada")}
        stage_in = [sem(f"p_stage_in{i}") for i in range(NST)]
        hi_done = sem("p_hi_done")
        lo_done = sem("p_lo_done")
        fills = sem("p_fills")
        step = sem("p_vector_step")
        args_done = sem("p_args_done")
        sin_done = sem("p_sin_done")
        silu2_done = sem("p_silu2_done")
        vecT = sem("p_vecT")
        vecs_done = sem("p_vecs_done")
        gbT = sem("p_gbT")
        gbT_done = sem("p_gbT_done")
        h1_mm, h1_done = sem("p_h1_mm"), sem("p_h1_done")
        h2_mm, h2_done = sem("p_h2_mm"), sem("p_h2_done")
        sc_mm, ada_mm, ada_done, ada_out = sem("p_sc_mm"), sem("p_ada_mm"), sem("p_ada_done"), sem("p_ada_out")

        pieces = [(n, k0, min(k, k0 + 1024 // m) - k0, m) for n, k, m in split
                  for k0 in range(0, k, 1024 // m)]

        def factor(name):
            return HD ** -0.5 if name == "Wq" else 1.0

        block = ctx.enter_context(nc.Block())

        @block.sync
        def _(sp):
            for dst, src in ((t["ident"][:, :], a["ident"]), (consts[:, :], a["consts"]),
                             (tb[:, :], a["condB_t"].partition_broadcast(P)),
                             (ti[:, :], a["itok_B_34_63"].partition_broadcast(P)),
                             (arg[:, 3 * B:4 * B], a["condB_theta"].partition_broadcast(P)),
                             (arg[:, 4 * B:5 * B], a["condB_phi"].partition_broadcast(P)),
                             (t["cond"][:, :], a["itok_B_0_2"].rearrange("(o b) -> o b", o=1)),
                             (bada[:, :], a["L2_cond_b_ada"].partition_broadcast(B))):
                sp.dma_start(dst, src).then_inc(consts_in, 16)
            sp.dma_start(vec_rows[:, :], a["vec_rows"]).then_inc(vecs_in, 16)
            sp.dma_start(w1[:, 0, :], a["L0_cond_W1"]).then_inc(w_in["w1"], 16)
            sp.dma_start(w2[:, :, :], a["L0_cond_W2"].rearrange("(k p) n -> p k n", p=P)).then_inc(w_in["w2"], 16)
            sp.dma_start(wsc[:, :, :], a["L0_cond_Wsc"].rearrange("(k p) n -> p k n", p=P)).then_inc(w_in["wsc"], 16)
            sp.dma_start(wsh[:, :, :], a["L0_cond_Wsh"].rearrange("(k p) n -> p k n", p=P)).then_inc(w_in["wsh"], 16)
            sp.dma_start(wada[:, :, :], a["L2_cond_W_ada"].rearrange("(k p) n -> p k n", p=P)).then_inc(w_in["wada"], 16)
            sp.dma_start(gb[:, 0, :, :], a["L0_cond_gamma"].rearrange("(c p) d -> p c d", p=P)).then_inc(gb_in, 16)
            sp.dma_start(gb[:, 1, :, :], a["L0_cond_beta"].rearrange("(c p) d -> p c d", p=P)).then_inc(gb_in, 16)
            sp.dma_start(t["rows"][:, :, :], a["rows"].partition_broadcast(P)).then_inc(rows_in, 16)
            for n, _k, _m in whole:
                sp.dma_start(w[n][:, :, :], a[n].rearrange("(k p) m -> p k m", p=P)).then_inc(whole_in, 16)
            sp.wait_ge(ada_done, 2)
            sp.dma_start(ada, ada_rows[:, :]).then_inc(ada_out, 16)
            sp.wait_ge(ada_out, 16)
            sp.wait_ge(rows_in, 16)
            sp.wait_ge(whole_in, 16 * len(whole))

        @block.gpsimd
        def _(pool):
            pool.memset(t["mean_of"][:, :], 1.0 / P).then_inc(fills, 1)
            pool.memset(t["halves"][:, :], -0.5).then_inc(fills, 1)
            for i, (n, k0, nk, m) in enumerate(pieces):
                if i >= NST:
                    pool.wait_ge(lo_done, i - NST + 1)
                pool.dma_start(stage[:, i % NST, 0:nk * m].rearrange("p (k m) -> p k m", m=m),
                               a[n].rearrange("(k p) m -> p k m", p=P)[:, k0:k0 + nk, :]).then_inc(stage_in[i % NST], 16)

        @block.scalar
        def _(act):
            act.wait_ge(args_done, 1)
            act.activation(trig[:, :], red[:, :], ACT.Sin).then_inc(sin_done, 1)
            act.wait_ge(sin_done, 1)
            act.activation(silu2[:, :, :], trig[:, B:3 * B].rearrange("p (c b) -> p c b", c=2),
                           ACT.Silu).then_inc(silu2_done, 1)
            act.wait_ge(vecs_done, 1)
            act.wait_ge(h1_mm, 1)
            for m in range(HC):
                last = act.activation(h1[:, m, :], ps[:, 0, m * B:(m + 1) * B], ACT.Silu,
                                      bias=t["vecs"][:, VEC["L0_b1"] + m:VEC["L0_b1"] + m + 1])
            last.then_inc(h1_done, 1)
            for i, (n, k0, nk, m) in enumerate(pieces):
                act.wait_ge(stage_in[i % NST], 16 * (i // NST + 1))
                act.activation(w[n][:, 0, k0:k0 + nk, :].rearrange("p k m -> p (k m)"), stage[:, i % NST, 0:nk * m],
                               ACT.Copy, scale=factor(n)).then_inc(hi_done, 1)

        @block.vector
        def _(dve):
            n_step = [0]

            def then(ins):
                n_step[0] += 1
                ins.then_inc(step, 1)
                dve.wait_ge(step, n_step[0])

            dve.wait_ge(consts_in, 16 * 8)
            then(dve.tensor_scalar(arg[:, 0:B], tb[:, :], 5000.0, consts[:, 0:1], ALU.mult, ALU.mult))
            num, quot, big, high, low, rem = (dv[:, j, :] for j in range(6))
            then(dve.tensor_copy(num, ti[:, :]))
            then(dve.tensor_scalar(quot, num, 0.01, None, ALU.mult))
            then(dve.tensor_scalar(big, quot, 4097.0, None, ALU.mult))
            then(dve.tensor_tensor(high, big, quot, ALU.subtract))
            then(dve.tensor_tensor(high, big, high, ALU.subtract))
            then(dve.tensor_tensor(low, quot, high, ALU.subtract))
            then(dve.scalar_tensor_tensor(rem, high, -100.0, num, ALU.mult, ALU.add))
            then(dve.scalar_tensor_tensor(rem, low, -100.0, rem, ALU.mult, ALU.add))
            then(dve.scalar_tensor_tensor(arg[:, 6 * B:7 * B], rem, 0.01, quot, ALU.mult, ALU.add))
            then(dve.tensor_scalar(arg[:, B:2 * B], arg[:, 6 * B:7 * B], 4000.0, consts[:, 1:2], ALU.mult, ALU.mult))
            then(dve.tensor_copy(arg[:, 2 * B:3 * B], arg[:, B:2 * B]))
            then(dve.tensor_copy(arg[:, 5 * B:7 * B], arg[:, 3 * B:5 * B]))
            sin_part = ((0, B, consts[:, 2:3], consts[:, 3:4]), (B, 2 * B, 0.0, 0.0), (2 * B, 3 * B, 0.25, np.pi / 2),
                        (3 * B, 5 * B, 0.0, 0.0), (5 * B, 7 * B, 0.25, np.pi / 2))
            for lo, hi, turns, _angle in sin_part:
                then(dve.tensor_scalar(turn[:, lo:hi], arg[:, lo:hi], 1.0 / TWO_PI, turns, ALU.mult, ALU.add))
            then(dve.tensor_scalar(turn[:, :], turn[:, :], ROUND, None, ALU.add))
            then(dve.tensor_scalar(turn[:, :], turn[:, :], -ROUND, None, ALU.add))
            then(dve.scalar_tensor_tensor(red[:, :], turn[:, :], -PI_A, arg[:, :], ALU.mult, ALU.add))
            then(dve.scalar_tensor_tensor(red[:, :], turn[:, :], -PI_B, red[:, :], ALU.mult, ALU.add))
            then(dve.scalar_tensor_tensor(red[:, :], turn[:, :], -PI_C, red[:, :], ALU.mult, ALU.add))
            for lo, hi, _turns, angle in sin_part:
                then(dve.tensor_scalar(red[:, lo:hi], red[:, lo:hi], angle, SIN_EDGE, ALU.add, ALU.min))
            dve.tensor_scalar(red[:, :], red[:, :], -SIN_EDGE, None, ALU.max).then_inc(args_done, 1)
            dve.wait_ge(vecT, 1)
            dve.tensor_copy(t["vecs"][:, :], ps[:, 1, 0:NVEC]).then_inc(vecs_done, 1)
            dve.wait_ge(vecs_done, 1)
            dve.tensor_scalar(t["vecs"][:, VEC["bq"]:VEC["bq"] + DC], t["vecs"][:, VEC["bq"]:VEC["bq"] + DC],
                              factor("Wq"), None, ALU.mult)
            dve.wait_ge(sin_done, 1)
            for j in range(4):
                at = (j // 2) * B
                dve.tensor_copy(t["rot"][:, 0, :, j], trig[:, 5 * B + at:6 * B + at])
                dve.tensor_scalar(t["rot"][:, 1, :, j], trig[:, 3 * B + at:4 * B + at], -1.0 if j % 2 else 1.0,
                                  None, ALU.mult)
            dve.wait_ge(gbT, 1)
            for i, name in enumerate(("gammaT", "betaT")):
                dve.tensor_copy(t[name][:, :, :].rearrange("p c s -> p (c s)"), ps[:, 4 + i, :]).then_inc(gbT_done, 1)
            for i, (n, k0, nk, m) in enumerate(pieces):
                dve.wait_ge(hi_done, i + 1)
                dve.scalar_tensor_tensor(w[n][:, 1, k0:k0 + nk, :].rearrange("p k m -> p (k m)"),
                                         stage[:, i % NST, 0:nk * m], factor(n),
                                         w[n][:, 0, k0:k0 + nk, :].rearrange("p k m -> p (k m)").bitcast(F32),
                                         ALU.mult, ALU.subtract).then_inc(lo_done, 1)
            dve.wait_ge(h2_mm, 1)
            for m in range(HC):
                last = dve.tensor_scalar(h2[:, m, :], ps[:, 2, m * B:(m + 1) * B],
                                         t["vecs"][:, VEC["L0_b2"] + m:VEC["L0_b2"] + m + 1], None, ALU.add)
            last.then_inc(h2_done, 1)
            dve.wait_ge(ada_mm, 1)
            dve.tensor_tensor(ada_rows[:, :], ps[0:B, 6, :], bada[:, :], ALU.add).then_inc(ada_done, 1)
            dve.wait_ge(ada_done, 1)
            dve.tensor_scalar(ada_rows[:, 0:D], ada_rows[:, 0:D], 1.0, None, ALU.add).then_inc(ada_done, 1)
            dve.wait_ge(sc_mm, 1)
            for m in range(DC):
                for q, (dst, b) in enumerate((("scale0", "L0_bsc"), ("shift0", "L0_bsh"))):
                    dve.tensor_scalar(t[dst][:, m, :], ps[:, 3, (q * DC + m) * B:(q * DC + m + 1) * B],
                                      t["vecs"][:, VEC[b] + m:VEC[b] + m + 1], None, ALU.add)

        @block.tensor
        def _(pe):
            pe.wait_ge(consts_in, 16 * 8)
            pe.wait_ge(vecs_in, 16)
            pe.transpose(ps[:, 1, 0:NVEC], vec_rows[:, :], t["ident"][0:NVEC, 0:NVEC]).then_inc(vecT, 1)
            pe.wait_ge(w_in["w1"], 16)
            pe.wait_ge(sin_done, 1)
            for m in range(HC):
                last = pe.matmul(ps[:, 0, m * B:(m + 1) * B], w1[:, 0, m * P:(m + 1) * P], trig[:, 0:B],
                                 start=True, stop=True)
            last.then_inc(h1_mm, 1)
            pe.wait_ge(gb_in, 32)
            for q in range(2):
                for c in range(DC):
                    for s in range(TC):
                        last = pe.transpose(ps[:, 4 + q, c * S + s * P:c * S + (s + 1) * P],
                                            gb[:, q, s, c * P:(c + 1) * P], t["ident"][:, :])
            last.then_inc(gbT, 1)
            pe.wait_ge(h1_done, 1)
            pe.wait_ge(w_in["w2"], 16)
            for m in range(HC):
                for k in range(HC):
                    last = pe.matmul(ps[:, 2, m * B:(m + 1) * B], w2[:, k, m * P:(m + 1) * P], h1[:, k, :],
                                     start=(k == 0), stop=(k == HC - 1))
            last.then_inc(h2_mm, 1)
            pe.wait_ge(w_in["wada"], 16)
            pe.wait_ge(silu2_done, 1)
            for k in range(DC):
                last = pe.matmul(ps[0:B, 6, :], silu2[:, k, :], wada[:, k, :], start=(k == 0), stop=(k == DC - 1))
            last.then_inc(ada_mm, 1)
            pe.wait_ge(h2_done, 1)
            pe.wait_ge(w_in["wsc"], 16)
            pe.wait_ge(w_in["wsh"], 16)
            for q, wt in enumerate((wsc, wsh)):
                for m in range(DC):
                    for k in range(HC):
                        last = pe.matmul(ps[:, 3, (q * DC + m) * B:(q * DC + m + 1) * B], wt[:, k, m * P:(m + 1) * P],
                                         h2[:, k, :], start=(k == 0), stop=(k == HC - 1))
            last.then_inc(sc_mm, 1)


def wait_apart(eng, semaphore, count):
    eng.wait_ge(semaphore, count)
    eng.nop(nofuse=True)


def matmul3(pe, out, lhs, rhs, first, last):
    pe.matmul(out, lhs[0], rhs[0], start=first, stop=False)
    pe.matmul(out, lhs[0], rhs[1], start=False, stop=False)
    return pe.matmul(out, lhs[1], rhs[0], start=False, stop=last)


def parts(tile, k, lo, hi):
    return tile[:, 0, k, lo:hi], tile[:, 1, k, lo:hi]


def by_route(eng, route, body):
    with eng.If(route == 0):
        body(0)
    with eng.Else():
        with eng.If(route == 1):
            body(1)
        with eng.Else():
            body(2)


def flat(tile):
    return tile[:, :, :].rearrange("p c s -> p (c s)")


def first_layers(nc, a, t, ps, ada):
    w, vecs, rows = t["w"], t["vecs"], t["rows"]
    XT = MA = 0
    MB = Z = 1
    HIDDEN = (("nr_w1", "nr_b1", DC), ("tsr_w1", "tsr_b1", DC), ("sr_w1", "sr_b1", 4))
    OUTER = (("nr_w2", "nr_b2"), ("tsr_w2", "tsr_b2"), ("sr_w3", "sr_b3"))
    (X_IN, X_MEAN, NORM0, SILU0, Y_MM, Y, Y_STATS, Y_MEAN, NORM1, SILU1, OUT0, X1, X1_T, X1_COPY, HIDDEN_MM, GELU,
     HIDDEN2_MM, GELU2, OUT1, SUM, RSTD2, X2, STATS3, RSTD3, X3) = range(len(SLOT))
    TURNS = B // LANES_A

    def run_stages(eng, stage):
        apart = TURN_SLOTS // LANES_A
        first = apart * (LANES_A - 1)

        def slot(k, i, last):
            for l in range(LANES_A):
                turn, k_lane = divmod(k - apart * l, TURN_SLOTS)
                if turn < 0 or last and turn > 0:
                    continue
                for s in range(len(SLOT)):
                    if SLOT[s] == k_lane:
                        stage(s, i + turn if turn else i, l)

        for k in range(first):
            slot(k, 0, False)
        with eng.Fori(0, TURNS - 1) as i:
            for k in range(first, first + TURN_SLOTS):
                slot(k, i, False)
        for k in range(first, first + TURN_SLOTS):
            slot(k, TURNS - 1, True)

    with ExitStack() as ctx:
        def sb(name, shape, dt=F32):
            return ctx.enter_context(nc.sbuf_tensor(name, shape, dt))

        def sem(name):
            return nc.alloc_semaphore(name)

        def per_lane(name, shape, dt=F32):
            return [sb(f"{name}{l}", shape, dt) for l in range(LANES_A)]

        x = per_lane("a_x", [P, TC, D])
        xb = per_lane("a_xb", [P, TC, D])
        f = per_lane("a_f", [P, 4, S])
        v = per_lane("a_v", [P, DC, S])
        y = per_lane("a_y", [P, DC, S])
        x1 = per_lane("a_x1", [P, TC, D])
        adab = per_lane("a_ada", [P, 2, D])
        st = per_lane("a_st", [P, 2, 8])
        bn = per_lane("a_bn", [P, TC, 6])
        mv = per_lane("a_mv", [P, 2, TC, 2])
        rs = per_lane("a_rs", [P, 2, TC])
        rv = per_lane("a_rv", [P, 2, TC])

        s = {n: sem(f"a_{n}") for n in (
            "xT", "stat_mm0", "stat_mm1", "y_mm", "out0_mm", "x1T", "g_mm", "out1_mm",
            "s0", "y", "s1", "x1_copy", "g",
            "in0", "ve0", "v0", "in1", "ve1", "v1", "x1",
            "ve2", "t1", "ve3", "t2",
            "xb", "rstd0", "rstd1", "xb2", "rstd2", "x2", "rstd3", "t2s", "x3")}
        own, OWN = [sem(f"a_vector_own{l}") for l in range(LANES_A)], 14
        r = {n: [sem(f"a_{n}_{l}") for l in range(LANES_A)] for n in ("g2_mm", "g2", "y1")}
        x_in = [sem(f"a_x_in{l}") for l in range(LANES_A)]
        ada_in = [sem(f"a_ada_in{l}") for l in range(LANES_A)]

        def bank(l, i):
            return ps[:, 2 * l + i, :]

        block = ctx.enter_context(nc.Block())

        @block.sync
        def _(sp):
            def load_x(b, l):
                sp.dma_start(x[l][:, :, :], a["x"][b + l].rearrange("(c p) d -> p c d", p=P)).then_inc(x_in[l], 16)

            def load_ada(b, l):
                sp.dma_start(flat(adab[l]), ada[b + l].partition_broadcast(P)).then_inc(ada_in[l], 16)

            for l in range(LANES_A):
                load_x(0, l)
                load_ada(0, l)
            with sp.Fori(1, B // LANES_A) as i:
                b = i * LANES_A
                for l in range(LANES_A):
                    sp.wait_ge(s["xT"], b + (l + 1 - LANES_A))
                    sp.wait_ge(s["in0"], b + (l + 1 - LANES_A))
                    wait_apart(sp, s["xb"], b + (l + 1 - LANES_A))
                    load_x(b, l)
                for l in range(LANES_A):
                    wait_apart(sp, s["x3"], b + (l + 1 - LANES_A))
                    load_ada(b, l)

        @block.tensor
        def _(pe):
            def transposes(l, src, done):
                for c in range(DC):
                    for q in range(TC):
                        last = pe.transpose(bank(l, XT)[:, c * S + q * P:c * S + (q + 1) * P],
                                            src[:, q, c * P:(c + 1) * P], t["ident"][:, :])
                last.then_inc(s[done], 1)

            def to_features(l, name, chunks, nk, done):
                for m in range(chunks):
                    for k in range(nk):
                        last = pe.matmul(bank(l, (MA, MB)[m // 2])[:, (m % 2) * S:(m % 2 + 1) * S],
                                         w[name][:, k, m * P:(m + 1) * P], f[l][:, k, :], start=(k == 0), stop=(k == nk - 1))
                last.then_inc(done, 1)

            def to_rows(l, name, done):
                nk = 4 if name == "sr_w2" else DC
                for q in range(TC):
                    for k in range(nk):
                        last = pe.matmul(bank(l, Z)[:, q * D:(q + 1) * D], f[l][:, k, q * P:(q + 1) * P], w[name][:, k, :],
                                         start=(k == 0), stop=(k == nk - 1))
                last.then_inc(s[done], 1)

            def stage(st_, i, l):
                n = LANES_A * i + (l + 1)

                if st_ in (HIDDEN_MM, HIDDEN2_MM, OUT1):
                    route = pe.value_load(t["cond"][0:1, bass.ds(LANES_A * i + l, 1)])
                if st_ == X_IN:
                    pe.wait_ge(x_in[l], 16 * i + 16)
                    transposes(l, x[l], "xT")
                elif st_ in (X_MEAN, Y_MEAN):
                    j = 0 if st_ == X_MEAN else 1
                    pe.wait_ge(s[f"in{j}"], n)
                    pe.matmul(bank(l, Z)[:, 0:2], t["mean_of"][:, :], st[l][:, j, 0:2], start=True,
                              stop=True).then_inc(s[f"stat_mm{j}"], 1)
                elif st_ == Y_MM:
                    pe.wait_ge(s["s0"], n)
                    to_features(l, "W_in", DC, DC, s["y_mm"])
                elif st_ == OUT0:
                    pe.wait_ge(s["s1"], n)
                    to_rows(l, "W_out", "out0_mm")
                elif st_ == X1_T:
                    pe.wait_ge(s["x1"], n)
                    transposes(l, x1[l], "x1T")
                elif st_ == HIDDEN_MM:
                    def product(way):
                        pe.wait_ge(s["x1_copy"], n)
                        to_features(l, HIDDEN[way][0], HIDDEN[way][2], DC, s["g_mm"])
                    by_route(pe, route, product)
                elif st_ == HIDDEN2_MM:
                    def product(way):
                        pe.wait_ge(s["g"], n)
                        if way == 2:
                            to_features(l, "sr_w2", DC, 4, r["g2_mm"][l])
                        else:
                            pe.sem_inc(r["g2_mm"][l], 1)
                    by_route(pe, route, product)
                elif st_ == OUT1:
                    def product(way):
                        pe.wait_ge(r["g2"][l], i + 1)
                        to_rows(l, OUTER[way][0], "out1_mm")
                    by_route(pe, route, product)

            run_stages(pe, stage)

        @block.scalar
        def _(act):
            def silu(l, i, done):
                for c in range(DC):
                    last = act.activation(f[l][:, c, :], v[l][:, c, :], ACT.Silu,
                                          scale=t["scale0"][:, c, bass.ds(LANES_A * i + l, 1)],
                                          bias=t["shift0"][:, c, bass.ds(LANES_A * i + l, 1)])
                last.then_inc(s[done], 1)

            def gelus(l, bias, chunks, done):
                for m in range(chunks):
                    last = act.activation(f[l][:, m, :], bank(l, (MA, MB)[m // 2])[:, (m % 2) * S:(m % 2 + 1) * S],
                                          ACT.Gelu, bias=vecs[:, VEC[bias] + m:VEC[bias] + m + 1])
                last.then_inc(done, 1)

            def stage(st_, i, l):
                n = LANES_A * i + (l + 1)

                if st_ in (SILU0, SILU1):
                    j = 0 if st_ == SILU0 else 1
                    wait_apart(act, s[f"v{j}"], n)
                    silu(l, i, f"s{j}")
                elif st_ == Y:
                    act.wait_ge(s["y_mm"], n)
                    for c in range(DC):
                        last = act.activation(y[l][:, c, :], bank(l, MA)[:, c * S:(c + 1) * S], ACT.Identity,
                                              bias=vecs[:, VEC["L0_b_in"] + c:VEC["L0_b_in"] + c + 1])
                    last.then_inc(s["y"], 1)
                elif st_ == X1_COPY:
                    act.wait_ge(s["x1T"], n)
                    act.activation(f[l][:, 0:DC, :].rearrange("p c s -> p (c s)"), bank(l, XT),
                                   ACT.Copy).then_inc(s["x1_copy"], 1)
                elif st_ == GELU:
                    def hidden(way):
                        act.wait_ge(s["g_mm"], n)
                        gelus(l, HIDDEN[way][1], HIDDEN[way][2], s["g"])
                    by_route(act, act.value_load(t["cond"][0:1, bass.ds(LANES_A * i + l, 1)]), hidden)
                elif st_ == GELU2:
                    def hidden2(way):
                        act.wait_ge(r["g2_mm"][l], i + 1)
                        if way == 2:
                            gelus(l, "sr_b2", DC, r["g2"][l])
                        else:
                            act.sem_inc(r["g2"][l], 1)
                    by_route(act, act.value_load(t["cond"][0:1, bass.ds(LANES_A * i + l, 1)]), hidden2)

            run_stages(act, stage)

        @block.vector
        def _(dve):
            def then(l, i, j, ins):
                ins.then_inc(own[l], 1)
                wait_apart(dve, own[l], OWN * i + j)

            def statistics(l, src, i, turn, n):
                then(l, turn, 5 * i + 1, dve.bn_stats(bn[l][:, 0, :], src))
                then(l, turn, 5 * i + 2, dve.bn_aggr(st[l][:, i, 0:2], bn[l][:, 0, :]))
                dve.scalar_tensor_tensor(st[l][:, i, 1:2], st[l][:, i, 0:1], st[l][:, i, 0:1],
                                         st[l][:, i, 1:2], ALU.mult, ALU.add).then_inc(s[f"in{i}"], 1)

            def block_norm(l, src, i, turn, n):
                dve.wait_ge(s[f"stat_mm{i}"], n)
                then(l, turn, 5 * i + 3, dve.tensor_copy(st[l][:, i, 2:4], bank(l, Z)[:, 0:2]))
                then(l, turn, 5 * i + 4, dve.scalar_tensor_tensor(
                    st[l][:, i, 4:5], st[l][:, i, 2:3], st[l][:, i, 2:3], st[l][:, i, 3:4], ALU.mult, ALU.subtract))
                dve.tensor_scalar(st[l][:, i, 5:6], st[l][:, i, 4:5], -1.0, EPS, ALU.mult,
                                  ALU.add).then_inc(s[f"ve{i}"], 1)
                then(l, turn, 5 * i + 5, dve.scalar_tensor_tensor(flat(v[l]), src, st[l][:, i, 2:3], flat(t["gammaT"]),
                                                                  ALU.subtract, ALU.mult))
                dve.wait_ge(s[f"rstd{i}"], n)
                dve.scalar_tensor_tensor(flat(v[l]), flat(v[l]), st[l][:, i, 6:7], flat(t["betaT"]),
                                         ALU.mult, ALU.add).then_inc(s[f"v{i}"], 1)

            def token_statistics(l, src, i, turn):
                for q in range(TC):
                    last = dve.bn_stats(bn[l][:, q, :], src[:, q, :])
                then(l, turn, 2 * i + 7, last)
                for q in range(TC):
                    last = dve.bn_aggr(mv[l][:, i - 2, q, :], bn[l][:, q, :])
                then(l, turn, 2 * i + 8, last)
                dve.tensor_scalar(rv[l][:, i - 2, :], mv[l][:, i - 2, :, 1], EPS, None, ALU.add).then_inc(s[f"ve{i}"], 1)

            def centre(l, dst, src, factor, i, done):
                for q in range(TC):
                    last = dve.scalar_tensor_tensor(dst[:, q, :], src[:, q, :], mv[l][:, i - 2, q, 0:1], factor,
                                                    ALU.subtract, ALU.mult)
                last.then_inc(s[done], 1)

            def stage(st_, i, l):
                n = LANES_A * i + (l + 1)

                if st_ == X_IN:
                    dve.wait_ge(x_in[l], 16 * i + 16)
                    statistics(l, flat(x[l]), 0, i, n)
                elif st_ == NORM0:
                    dve.wait_ge(s["xT"], n)
                    block_norm(l, bank(l, XT), 0, i, n)
                elif st_ == Y_STATS:
                    dve.wait_ge(s["y"], n)
                    statistics(l, flat(y[l]), 1, i, n)
                elif st_ == NORM1:
                    block_norm(l, flat(y[l]), 1, i, n)
                elif st_ == X1:
                    dve.wait_ge(s["out0_mm"], n)
                    dve.wait_ge(s["xb"], n)
                    dve.tensor_tensor(flat(x1[l]), bank(l, Z), flat(xb[l]), ALU.add).then_inc(s["x1"], 1)
                elif st_ == SUM:
                    route = dve.value_load(t["cond"][0:1, bass.ds(LANES_A * i + l, 1)])

                    def add():
                        dve.wait_ge(s["out1_mm"], n)
                        dve.wait_ge(s["xb2"], n)
                        dve.tensor_tensor(flat(x1[l]), bank(l, Z), flat(xb[l]), ALU.add).then_inc(r["y1"][l], 1)

                    def add_or_not(way):
                        if way < 2:
                            add()
                            return
                        with dve.If(route == 2):
                            add()
                        with dve.Else():
                            dve.wait_ge(s["out1_mm"], n)
                            dve.sem_inc(r["y1"][l], 1)
                    by_route(dve, route, add_or_not)
                    dve.wait_ge(r["y1"][l], i + 1)
                    token_statistics(l, x1[l], 2, i)
                    centre(l, v[l], x1[l], rows[:, ROWS["gamma1"], :], 2, "t1")
                elif st_ == X2:
                    dve.wait_ge(s["t1"], n)
                    dve.wait_ge(s["rstd2"], n)
                    for q in range(TC):
                        last = dve.scalar_tensor_tensor(v[l][:, q, :], v[l][:, q, :], rs[l][:, 0, q:q + 1],
                                                        rows[:, ROWS["beta1"], :], ALU.mult, ALU.add)
                    last.then_inc(s["x2"], 1)
                elif st_ == STATS3:
                    dve.wait_ge(s["x2"], n)
                    token_statistics(l, v[l], 3, i)
                    dve.wait_ge(ada_in[l], 16 * i + 16)
                    centre(l, y[l], v[l], adab[l][:, 0, :], 3, "t2")

            run_stages(dve, stage)

        @block.gpsimd
        def _(pool):
            def rsqrt(l, dst, src, width, done):
                pool.tensor_tensor(dst, src, t["halves"][:, 0:width], ALU.pow).then_inc(s[done], 1)

            def row(name):
                return rows[:, ROWS[name]:ROWS[name] + 1, :].to_broadcast([P, TC, D])

            def stage(st_, i, l):
                n = LANES_A * i + (l + 1)

                if st_ == X_IN:
                    pool.wait_ge(x_in[l], 16 * i + 16)
                    pool.tensor_tensor(xb[l][:, :, :], x[l][:, :, :], row("b_out"), ALU.add).then_inc(s["xb"], 1)
                elif st_ in (NORM0, NORM1):
                    j = 0 if st_ == NORM0 else 1
                    pool.wait_ge(s[f"ve{j}"], n)
                    rsqrt(l, st[l][:, j, 6:7], st[l][:, j, 5:6], 1, f"rstd{j}")
                elif st_ == X1_T:
                    route = pool.value_load(t["cond"][0:1, bass.ds(LANES_A * i + l, 1)])

                    def add_bias(way):
                        pool.wait_ge(s["x1"], n)
                        pool.tensor_tensor(xb[l][:, :, :], x1[l][:, :, :], row(OUTER[way][1]), ALU.add).then_inc(s["xb2"], 1)
                    by_route(pool, route, add_bias)
                elif st_ in (RSTD2, RSTD3):
                    j = 0 if st_ == RSTD2 else 1
                    pool.wait_ge(s[f"ve{j + 2}"], n)
                    rsqrt(l, rs[l][:, j, :], rv[l][:, j, :], TC, f"rstd{j + 2}")
                elif st_ == X3:
                    pool.wait_ge(s["t2"], n)
                    wait_apart(pool, s["rstd3"], n)
                    for q in range(TC):
                        last = pool.tensor_scalar(y[l][:, q, :], y[l][:, q, :], rs[l][:, 1, q:q + 1], 0.0, ALU.mult, ALU.add)
                    last.then_inc(s["t2s"], 1)
                    pool.wait_ge(s["t2s"], n)
                    pool.tensor_tensor(t["x3"][:, bass.ds(LANES_A * i + l, 1), :, :].rearrange("p o c d -> p (o c) d"),
                                       y[l][:, :, :], adab[l][:, 1:2, :].to_broadcast([P, TC, D]),
                                       ALU.add).then_inc(s["x3"], 1)

            run_stages(pool, stage)


def attention(nc, a, t, ps):
    w, vecs, rows = t["w"], t["vecs"], t["rows"]
    UNITS = NH // 2 * TC
    GH = 4
    GROUPS = NH // GH
    GU = UNITS // GROUPS
    VW = 3 * HD + 1
    SCORES, BIAS, EXPS, TURNS, PARTS = 5, 4, 3, 2, 1
    PAIRS = B // LANES
    TURN = LANES * UNITS
    SHIFT = 8
    S_BANK, T_BANK, V_BANK, X_BANK = 0, 2, 4, 6
    with ExitStack() as ctx:
        def sb(name, shape, dt=F32):
            return ctx.enter_context(nc.sbuf_tensor(name, shape, dt))

        def sem(name):
            return ctx.enter_context(nc.semaphore(name))

        x_rows = sb("b_x_rows", [P, TC, D])
        x_part = sb("b_x", [P, 2, DC, S], F32R)
        q_part = [sb(f"b_q{l}", [P, 2, DC, S], F32R) for l in range(LANES)]
        k_part = [sb(f"b_k{l}", [P, DC, 2, S], F32R) for l in range(LANES)]
        KM = 4
        k_head = sb("b_k_head", [P, KM, 2, 2, S], F32R)
        v_full = sb("b_v_full", [P, TC, D])
        v_rest = sb("b_v_rest", [P, TC, D])
        v_part = [sb(f"b_v{l}", [P, TC, NH, VW], BF16) for l in range(LANES)]
        bias = sb("b_bias", [P, GROUPS, GH, TC, S])
        mask8 = [sb(f"b_mask8{l}", [P, TC, S], U8) for l in range(LANES)]
        mask = [sb(f"b_mask{l}", [P, TC, S], BF16) for l in range(LANES)]
        masked = sb("b_masked", [P, P], BF16)
        head_rows = sb("b_head_rows", [P, 8])
        NP_ = 4
        prob = sb("b_prob", [P, NP_, 2 * S])
        lowest = sb("b_lowest", [P, NP_, 2])
        pT = sb("b_pT", [P, NP_, 2, 2 * S], F16)
        sums = sb("b_sums", [P, 2, TC * GH, HD])
        recip = sb("b_recip", [P, 2, TC * GH])
        ctx_rows = [sb(f"b_ctx{l}", [P, TC, D]) for l in range(LANES)]
        c_part = sb("b_c", [P, 2, DC, S], F32R)
        FP = (DC * FF + FC * D) // PAIRS
        ff_raw = sb("b_ff_raw", [P, FP])

        q = {n: sem(f"b_{n}") for n in (
            "x_mm", "q_mm", "k_mm", "v_mm", "c_mm", "o_mm", "x_hi", "q_hi", "k_hi", "v_hi", "v_mid", "c_hi",
            "x_lo", "q_lo", "k_lo", "v_full", "v_rest", "v_lo", "c_lo", "x4", "mask", "x3b")}
        score_mm, scored, exped = sem("b_score_mm"), sem("b_scored"), sem("b_exped")
        turned, t_hi, t_lo, applied = sem("b_turned"), sem("b_t_hi"), sem("b_t_lo"), sem("b_applied")
        group_read, normed = sem("b_group_read"), sem("b_normed")
        k_ready = sem("b_k_ready")
        bias_in = [sem(f"b_bias_in{g}") for g in range(GROUPS)]
        x_in = sem("b_x_in")
        mask_in = [sem(f"b_mask_in{l}") for l in range(LANES)]
        once_in, ff_in, once, ff_hi, ff_lo = sem("b_once_in"), sem("b_ff_in"), sem("b_once"), sem("b_ff_hi"), sem("b_ff_lo")
        FREE_KEYS = 2 * KM

        def heads(u):
            return u // TC, u % TC

        def at(i, x):
            return TURN * i + (x + 1)

        def seq(i, x):
            return LANES * i + (x // UNITS + 1)

        def run_slots(eng, slot):
            for k in range(-SCORES, SHIFT):
                slot(k, 0, range(0, B * UNITS))
            with eng.Fori(0, PAIRS - 1) as i:
                for k in range(SHIFT, SHIFT + TURN):
                    slot(k, i, range(-B * UNITS, B * UNITS))
            for k in range(SHIFT, TURN + 8):
                slot(k, PAIRS - 1, range(-B * UNITS, TURN))

        block = ctx.enter_context(nc.Block())

        @block.sync
        def _(sp):
            def load_bias(b, g):
                sp.dma_start(bias[:, g, :, :, :], a["fside_Bx16xSxS_0"][b, g * GH:(g + 1) * GH]
                             .rearrange("h (c p) k -> p h c k", p=P)).then_inc(bias_in[g], 16)

            def load_mask(b, l):
                sp.dma_start(mask8[l][:, :, :], a["mask"][b, 0].rearrange("(c p) k -> p c k", p=P)).then_inc(mask_in[l], 16)

            def copy_x(b):
                sp.dma_start(x_rows[:, :, :].rearrange("p (o c) d -> p o c d", o=1),
                             t["x3"][:, bass.ds(b, 1), :, :]).then_inc(x_in, 16)

            sp.dma_start(head_rows[:, :], a["head_rows"]).then_inc(once_in, 16)
            for l in range(LANES):
                load_mask(l, l)
            copy_x(0)
            for g in range(GROUPS):
                load_bias(0, g)
            sp.dma_start(ff_raw[:, :], a["ff"][:, 0:FP]).then_inc(ff_in, 16)

            def loads(b, more=True):
                if more:
                    wait_apart(sp, q["x_mm"], b + 1)
                    copy_x(b + 1)
                for g in range(GROUPS):
                    wait_apart(sp, scored, 2 * LANES + 2 * (UNITS * (b - 1)) + 2 * GU * (g + 1))
                    load_bias(b, g)

            sp.wait_ge(q["x_mm"], 1)
            copy_x(1)
            with sp.Fori(0, PAIRS - 1) as i:
                for l in range(LANES):
                    loads(LANES * i + (l + 1))
                    wait_apart(sp, q["mask"], LANES * i + (l + 1))
                    load_mask(LANES * i + (l + 2), l)
                wait_apart(sp, ff_lo, i + 1)
                sp.dma_start(ff_raw[:, :], a["ff"][:, bass.ds(FP * i + FP, FP)]).then_inc(ff_in, 16)
            loads(B - 1, more=False)

        @block.tensor
        def _(pe):
            def project(name, src_part, bank, done):
                for m in range(DC):
                    for k in range(DC):
                        last = matmul3(pe, ps[:, bank, m * S:(m + 1) * S], parts(w[name], k, m * P, (m + 1) * P),
                                       parts(src_part, k, 0, S), k == 0, k == DC - 1)
                last.then_inc(done, 1)

            def to_rows(name, src_part, bank, done):
                for c in range(TC):
                    for k in range(DC):
                        last = matmul3(pe, ps[:, bank, c * D:(c + 1) * D], parts(src_part, k, c * P, (c + 1) * P),
                                       parts(w[name], k, 0, D), k == 0, k == DC - 1)
                last.then_inc(done, 1)

            def turn_x(i, x):
                pe.wait_ge(x_in, 16 * seq(i, x))
                if x >= UNITS:
                    pe.wait_ge(q["v_full"], seq(i, x - UNITS))
                for c in range(DC):
                    for r in range(TC):
                        last = pe.transpose(ps[:, X_BANK + 1, c * S + r * P:c * S + (r + 1) * P],
                                            x_rows[:, r, c * P:(c + 1) * P], t["ident"][:, :])
                last.then_inc(q["x_mm"], 1)

            def queries(i, x):
                pe.wait_ge(q["x_lo"], seq(i, x))
                project("Wq", x_part, X_BANK + 1, q["q_mm"])

            def keys(i, x):
                pe.wait_ge(q["q_lo"], seq(i, x))
                project("Wk", x_part, X_BANK + 1, q["k_mm"])

            def values(i, x):
                pe.wait_ge(q["k_lo"], seq(i, x))
                to_rows("Wv", x_part, X_BANK + 1, q["v_mm"])

            def turn_ctx(i, x):
                pe.wait_ge(normed, GROUPS * seq(i, x))
                pe.wait_ge(q["x4"], seq(i, x))
                for k in range(DC):
                    for c in range(TC):
                        last = pe.transpose(ps[:, X_BANK, k * S + c * P:k * S + (c + 1) * P],
                                            ctx_rows[x // UNITS % LANES][:, c, k * P:(k + 1) * P], t["ident"][:, :])
                last.then_inc(q["c_mm"], 1)

            def output(i, x):
                pe.wait_ge(q["c_lo"], seq(i, x))
                to_rows("Wo", c_part, X_BANK, q["o_mm"])

            def scores(i, x):
                u, l = x % UNITS, x // UNITS % LANES
                pair, c = heads(u)
                slot = (x // TC) % KM
                if u == 0:
                    pe.wait_ge(q["mask"], seq(i, x))
                    pe.wait_ge(q["q_lo"], seq(i, x))
                if c == 0:
                    pe.wait_ge(k_ready, (TURN // TC) * i + (x // TC + 1))
                pe.wait_ge(scored, 2 * at(i, x))
                out_ = ps[:, S_BANK + x % 2, :]
                pe.matmul(out_, masked[:, :], mask[l][:, c:c + 1, :].to_broadcast([P, 2, S]), start=True, stop=False)
                chunk = pair // 4
                qh, ql = (q_part[l][:, h, chunk, c * P:(c + 1) * P] for h in range(2))
                kh, kl = (k_head[:, slot, h, :, :].rearrange("p j s -> p (j s)") for h in range(2))
                pe.matmul(out_, qh, kh, start=False, stop=False)
                pe.matmul(out_, qh, kl, start=False, stop=False)
                pe.matmul(out_, ql, kh, start=False, stop=True).then_inc(score_mm, 1)

            def turn(i, x):
                pe.wait_ge(exped, 2 * at(i, x))
                pe.wait_ge(t_lo, at(i, x))
                for j in range(4):
                    last = pe.transpose(ps[:, T_BANK + x % 2, j * P:(j + 1) * P], prob[:, x % NP_, j * P:(j + 1) * P],
                                        t["ident"][:, :])
                last.then_inc(turned, 1)

            def apply(i, x):
                u, l = x % UNITS, x // UNITS % LANES
                pair, c = heads(u)
                g = (x // GU) % 2
                if u == 0:
                    pe.wait_ge(q["v_lo"], seq(i, x))
                if u % GU == 0:
                    pe.wait_ge(group_read, 2 * (TURN // GU) * i + 2 * (x // GU + 1))
                pe.wait_ge(t_lo, at(i, x) + 2)
                for j in range(2):
                    head = 2 * pair + j
                    col = (c * GH + head % GH) * VW
                    for kc in range(TC):
                        for h in range(2):
                            last = pe.matmul(ps[:, V_BANK + g, col:col + VW], pT[:, x % NP_, h, (2 * j + kc) * P:(2 * j + kc + 1) * P],
                                             v_part[l][:, kc, head, :], start=(kc + h == 0), stop=(kc + h == 2))
                last.then_inc(applied, 1)

            def slot(k, i, here):
                s, first = k % UNITS, k // UNITS * UNITS
                if k >= 0 and first + UNITS in here:
                    for when, what in ((0, turn_x), (3, queries), (6, keys), (8, values)):
                        if s == when:
                            what(i, first + UNITS)
                if k >= 0 and first - UNITS in here:
                    for when, what in ((2, turn_ctx), (5, output)):
                        if s == when:
                            what(i, first - UNITS)
                if k + TURNS in here:
                    turn(i, k + TURNS)
                if k + SCORES in here:
                    scores(i, k + SCORES)
                if k in here:
                    apply(i, k)

            pe.wait_ge(once, 3)
            for what in (turn_x, queries, keys, values):
                what(0, 0)
            run_slots(pe, slot)

        @block.scalar
        def _(act):
            def high(dst, src, wait, n, done):
                act.wait_ge(wait, n)
                act.activation(dst, src, ACT.Copy).then_inc(done, 1)

            def x_high(i, x):
                high(x_part[:, 0, :, :].rearrange("p c s -> p (c s)"), ps[:, X_BANK + 1, :], q["x_mm"], seq(i, x), q["x_hi"])

            def ctx_high(i, x):
                high(c_part[:, 0, :, :].rearrange("p c s -> p (c s)"), ps[:, X_BANK, :], q["c_mm"], seq(i, x), q["c_hi"])

            def q_high(i, x):
                act.wait_ge(q["q_mm"], seq(i, x))
                for m in range(DC):
                    last = act.activation(q_part[x // UNITS % LANES][:, 0, m, :], ps[:, X_BANK + 1, m * S:(m + 1) * S],
                                          ACT.Identity, bias=vecs[:, VEC["bq"] + m:VEC["bq"] + m + 1])
                last.then_inc(q["q_hi"], 1)

            def k_high(i, x):
                act.wait_ge(q["k_mm"], seq(i, x))
                for m in range(DC):
                    last = act.activation(k_part[x // UNITS % LANES][:, m, 0, :], ps[:, X_BANK + 1, m * S:(m + 1) * S],
                                          ACT.Identity, bias=vecs[:, VEC["bk"] + m:VEC["bk"] + m + 1])
                last.then_inc(q["k_hi"], 1)

            def v_slices(l, s):
                return v_part[l][:, :, :, s * HD:(s + 1) * HD]

            def v_high(i, x):
                act.wait_ge(q["v_full"], seq(i, x))
                act.activation(v_slices(x // UNITS % LANES, 0), v_full[:, :, :].rearrange("p c (h d) -> p c h d", d=HD),
                               ACT.Copy).then_inc(q["v_hi"], 1)

            def v_middle(i, x):
                act.wait_ge(q["v_rest"], seq(i, x))
                act.activation(v_slices(x // UNITS % LANES, 1), v_rest[:, :, :].rearrange("p c (h d) -> p c h d", d=HD),
                               ACT.Copy).then_inc(q["v_mid"], 1)

            def exps(i, x):
                r = x % NP_
                for j in range(2):
                    act.wait_ge(scored, 2 * at(i, x) + (3 + j))
                    act.activation(prob[:, r, j * S:(j + 1) * S], prob[:, r, j * S:(j + 1) * S], ACT.Exp,
                                   bias=lowest[:, r, j:j + 1], scale=-1.0).then_inc(exped, 1)

            def turned_high(i, x):
                act.wait_ge(turned, at(i, x) + NP_)
                act.wait_ge(applied, at(i, x))
                act.activation(pT[:, x % NP_, 0, :], ps[:, T_BANK + x % 2, :], ACT.Copy).then_inc(t_hi, 1)

            def slot(k, i, here):
                s, first = k % UNITS, k // UNITS * UNITS
                if k + PARTS in here:
                    turned_high(i, k + PARTS)
                if k + EXPS in here:
                    exps(i, k + EXPS)
                if k >= 0 and first + UNITS in here:
                    for when, what in ((0, x_high), (3, q_high), (6, k_high), (10, v_high), (12, v_middle)):
                        if s == when:
                            what(i, first + UNITS)
                if k >= 0 and first - UNITS in here and s == 2:
                    ctx_high(i, first - UNITS)

            for what in (x_high, q_high, k_high, v_high, v_middle):
                what(0, 0)
            run_slots(act, slot)

        @block.vector
        def _(dve):
            dve.sem_inc(scored, 4)
            dve.sem_inc(t_lo, 2)
            dve.sem_inc(group_read, 4)
            dve.sem_inc(q["x4"], 1)

            def x_low(i, x):
                dve.wait_ge(q["x_hi"], seq(i, x))
                dve.tensor_tensor(x_part[:, 1, :, :].rearrange("p c s -> p (c s)"), ps[:, X_BANK + 1, :],
                                  x_part[:, 0, :, :].rearrange("p c s -> p (c s)").bitcast(F32),
                                  ALU.subtract).then_inc(q["x_lo"], 1)

            def ctx_low(i, x):
                dve.wait_ge(q["c_hi"], seq(i, x))
                dve.tensor_tensor(c_part[:, 1, :, :].rearrange("p c s -> p (c s)"), ps[:, X_BANK, :],
                                  c_part[:, 0, :, :].rearrange("p c s -> p (c s)").bitcast(F32),
                                  ALU.subtract).then_inc(q["c_lo"], 1)

            def q_low(i, x):
                dve.wait_ge(q["q_hi"], seq(i, x))
                part = q_part[x // UNITS % LANES]
                for m in range(DC):
                    last = dve.scalar_tensor_tensor(part[:, 1, m, :], ps[:, X_BANK + 1, m * S:(m + 1) * S],
                                                    vecs[:, VEC["bq"] + m:VEC["bq"] + m + 1], part[:, 0, m, :].bitcast(F32),
                                                    ALU.add, ALU.subtract)
                last.then_inc(q["q_lo"], 1)

            def k_low(i, x):
                dve.wait_ge(q["k_hi"], seq(i, x))
                part = k_part[x // UNITS % LANES]
                for m in range(DC):
                    last = dve.scalar_tensor_tensor(part[:, m, 1, :], ps[:, X_BANK + 1, m * S:(m + 1) * S],
                                                    vecs[:, VEC["bk"] + m:VEC["bk"] + m + 1], part[:, m, 0, :].bitcast(F32),
                                                    ALU.add, ALU.subtract)
                last.then_inc(q["k_lo"], 1)

            def v_whole(i, x):
                dve.wait_ge(q["v_mm"], seq(i, x))
                dve.tensor_tensor(v_full[:, :, :], ps[:, X_BANK + 1, :].rearrange("p (c d) -> p c d", c=TC),
                                  rows[:, ROWS["bv"]:ROWS["bv"] + 1, :].to_broadcast([P, TC, D]), ALU.add).then_inc(q["v_full"], 1)

            def by_head(tile):
                return tile[:, :, :].rearrange("p c (h d) -> p c h d", d=HD)

            def v_remainder(i, x):
                dve.wait_ge(q["v_hi"], seq(i, x))
                dve.tensor_tensor(by_head(v_rest), by_head(v_full), v_part[x // UNITS % LANES][:, :, :, 0:HD],
                                  ALU.subtract).then_inc(q["v_rest"], 1)

            def v_low(i, x):
                dve.wait_ge(q["v_mid"], seq(i, x))
                part = v_part[x // UNITS % LANES]
                dve.tensor_tensor(part[:, :, :, 2 * HD:3 * HD], by_head(v_rest), part[:, :, :, HD:2 * HD],
                                  ALU.subtract).then_inc(q["v_lo"], 1)

            def residual(i, x):
                dve.wait_ge(q["o_mm"], seq(i, x))
                dve.wait_ge(q["x3b"], seq(i, x))
                x4 = t["x3"][:, bass.ds(LANES * i + x // UNITS, 1), :, :].rearrange("p o c d -> p (o c) d")
                dve.tensor_tensor(x4, ps[:, X_BANK, :].rearrange("p (c d) -> p c d", c=TC), x4, ALU.add).then_inc(q["x4"], 1)

            def add_bias(i, x):
                u = x % UNITS
                pair, c = heads(u)
                r = x % NP_
                dve.wait_ge(score_mm, at(i, x) + FREE_KEYS)
                if u % GU == 0:
                    dve.wait_ge(bias_in[u // GU], 16 * seq(i, x))
                wait_apart(dve, turned, at(i, x))
                for j in range(2):
                    dve.tensor_tensor_reduce(prob[:, r, j * S:(j + 1) * S], ps[:, S_BANK + x % 2, j * S:(j + 1) * S],
                                             bias[:, u // GU, 2 * (pair % 2) + j, c, :], -1.0, 3.0e38, ALU.add, ALU.min,
                                             lowest[:, r, j:j + 1]).then_inc(scored, 1)

            def turned_low(i, x):
                dve.wait_ge(t_hi, at(i, x))
                dve.tensor_tensor(pT[:, x % NP_, 1, :], ps[:, T_BANK + x % 2, :], pT[:, x % NP_, 0, :],
                                  ALU.subtract).then_inc(t_lo, 1)

            def sum_group(i, x):
                g = (x // GU) % 2
                res = ps[:, V_BANK + g, 0:TC * GH * VW].rearrange("p (e f) -> p e f", f=VW)
                dve.wait_ge(applied, at(i, x) + NP_)
                dve.tensor_reduce(sums[:, g, :, :], res[:, :, 0:3 * HD].rearrange("p e (s d) -> p e d s", d=HD), AX.X,
                                  ALU.add).then_inc(group_read, 1)
                dve.reciprocal(recip[:, g, :], res[:, :, 3 * HD]).then_inc(group_read, 1)

            def norm_group(i, x):
                u, l, g = x % UNITS, x // UNITS % LANES, (x // GU) % 2
                dve.wait_ge(group_read, 2 * (TURN // GU) * i + (2 * (x // GU + 1) + 4))
                at_ = u // GU * GH * HD
                for c in range(TC):
                    last = dve.tensor_tensor(ctx_rows[l][:, c, at_:at_ + GH * HD].rearrange("p (h d) -> p h d", d=HD),
                                             sums[:, g, c * GH:(c + 1) * GH, :],
                                             recip[:, g, c * GH:(c + 1) * GH].rearrange("p (e o) -> p e o", o=1)
                                             .to_broadcast([P, GH, HD]), ALU.mult)
                last.then_inc(normed, 1)

            def slot(k, i, here):
                s, first = k % UNITS, k // UNITS * UNITS
                if k % GU == 0 and k - 1 in here:
                    sum_group(i, k - 1)
                if k + BIAS in here:
                    add_bias(i, k + BIAS)
                if k % GU == 0 and k - 1 in here:
                    norm_group(i, k - 1)
                if k + PARTS in here:
                    turned_low(i, k + PARTS)
                if k >= 0 and first + UNITS in here:
                    for when, what in ((1, x_low), (4, q_low), (7, k_low), (9, v_whole), (11, v_remainder), (13, v_low)):
                        if s == when:
                            what(i, first + UNITS)
                if k >= 0 and first - UNITS in here:
                    for when, what in ((3, ctx_low), (6, residual)):
                        if s == when:
                            what(i, first - UNITS)

            for what in (x_low, q_low, k_low, v_whole, v_remainder, v_low):
                what(0, 0)
            run_slots(dve, slot)

        @block.gpsimd
        def _(pool):
            pool.wait_ge(once_in, 16)
            for l in range(LANES):
                pool.memset(v_part[l][:, :, :, 3 * HD:VW], 1.0).then_inc(once, 1)
            pool.tensor_scalar(masked[:, :], t["ident"][:, :], MASKED, 0.0, ALU.mult, ALU.add).then_inc(once, 1)

            def mask_bits(i, l):
                wait_apart(pool, mask_in[l], 16 * i + 16)
                pool.tensor_copy(mask[l][:, :, :], mask8[l][:, :, :]).then_inc(q["mask"], 1)

            pool.sem_inc(score_mm, FREE_KEYS)
            pool.sem_inc(applied, NP_)
            pool.sem_inc(turned, NP_)
            with pool.Fori(0, PAIRS) as i:
                for l in range(LANES):
                    n = LANES * i + (l + 1)
                    pool.wait_ge(score_mm, TURN * i + (UNITS * (l - 1) + FREE_KEYS) if l else TURN * i + 1)
                    mask_bits(i, l)
                    pool.wait_ge(q["x_mm"], n)
                    x3 = t["x3"][:, bass.ds(LANES * i + l, 1), :, :].rearrange("p o c d -> p (o c) d")
                    pool.tensor_tensor(x3, x3, rows[:, ROWS["bo"]:ROWS["bo"] + 1, :].to_broadcast([P, TC, D]),
                                       ALU.add).then_inc(q["x3b"], 1)
                    wait_apart(pool, q["k_lo"], n)
                    for pair in range(NH // 2):
                        wait_apart(pool, score_mm, TURN * i + (UNITS * l + 2 * pair + 2))
                        for j in range(2):
                            head = (2 * pair + j) % 8
                            last = pool.tensor_scalar(k_head[:, pair % KM, :, j, :], k_part[l][:, pair // 4, :, :],
                                                      head_rows[:, head:head + 1], 0.0, ALU.mult, ALU.add)
                        last.then_inc(k_ready, 1)
                wait_apart(pool, ff_in, 16 * i + 16)
                eighth = bass.ds(FP * i, FP)
                pool.tensor_copy(t["ff"][:, 0, eighth], ff_raw[:, :]).then_inc(ff_hi, 1)
                pool.wait_ge(ff_hi, i + 1)
                pool.tensor_tensor(t["ff"][:, 1, eighth], ff_raw[:, :], t["ff"][:, 0, eighth].bitcast(F32),
                                   ALU.subtract).then_inc(ff_lo, 1)


def feed_forward(nc, a, t, ps, out):
    vecs, rows = t["vecs"], t["rows"]
    w1 = t["ff"][:, :, 0:DC * FF].rearrange("p h (k m) -> p h k m", m=FF)
    w2 = t["ff"][:, :, DC * FF:].rearrange("p h (k m) -> p h k m", m=D)
    BANKS = FC // 2
    PAIRS = B // LANES
    with ExitStack() as ctx:
        def per_lane(name, shape, dt=F32):
            return [ctx.enter_context(nc.sbuf_tensor(f"{name}{l}", shape, dt)) for l in range(LANES)]

        def sem(name):
            return ctx.enter_context(nc.semaphore(name))

        norm = per_lane("c_norm", [P, TC, D])
        h = per_lane("c_h", [P, DC, S])
        h_part = per_lane("c_h_part", [P, 2, DC, S], F32R)
        act_ = per_lane("c_act", [P, FC, S])
        a_part = per_lane("c_act_part", [P, 2, FC, S], F32R)
        x5 = per_lane("c_x5", [P, TC, D])
        rot1 = per_lane("c_rot1", [P, TC, D])
        rot2 = per_lane("c_rot2", [P, TC, D])
        bn = per_lane("c_bn", [P, TC, 6])
        mv = per_lane("c_mv", [P, TC, 2])
        rv = per_lane("c_rv", [P, TC])
        rs = per_lane("c_rs", [P, TC])
        s = {n: sem(f"c_{n}") for n in ("own", "ve", "rstd", "norm", "normT", "h", "h_hi", "h_lo", "out_mm", "x4b",
                                        "x5", "rot1", "rot2", "rotated")}
        ff_mm, ff_act, ff_hi, ff_lo = sem("c_ff_mm"), sem("c_ff_act"), sem("c_ff_hi"), sem("c_ff_lo")
        stored = [sem(f"c_stored{l}") for l in range(LANES)]

        def bank(l, j):
            return ps[:, BANKS * l + j, :]

        def x4(i, l):
            return t["x3"][:, bass.ds(LANES * i + l, 1), :, :].rearrange("p o c d -> p (o c) d")

        def turns(eng, prepare, work):
            for l in range(LANES):
                prepare(0, l)
            with eng.Fori(0, PAIRS - 1) as i:
                work(i, lambda l: prepare(i + 1, l))
            work(PAIRS - 1, lambda l: None)

        block = ctx.enter_context(nc.Block())

        @block.sync
        def _(sp):
            with sp.Fori(0, PAIRS) as i:
                for l in range(LANES):
                    wait_apart(sp, s["rotated"], LANES * i + (l + 1))
                    sp.dma_start(out[LANES * i + l].rearrange("(c p) d -> p c d", p=P), rot1[l][:, :, :]).then_inc(stored[l], 16)
            for l in range(LANES):
                sp.wait_ge(stored[l], 16 * PAIRS + 16)

        @block.tensor
        def _(pe):
            def prepare(i, l):
                pe.wait_ge(s["norm"], LANES * i + (l + 1))
                for c in range(DC):
                    for r in range(TC):
                        last = pe.transpose(bank(l, 1)[:, c * S + r * P:c * S + (r + 1) * P], norm[l][:, r, c * P:(c + 1) * P],
                                            t["ident"][:, :])
                last.then_inc(s["normT"], 1)

            def work(i, next_):
                n = [LANES * i + (l + 1) for l in range(LANES)]
                for l in range(LANES):
                    pe.wait_ge(s["h_lo"], n[l])
                    for m in range(FC):
                        for k in range(DC):
                            last = matmul3(pe, bank(l, m // 2)[:, (m % 2) * S:(m % 2 + 1) * S], parts(w1, k, m * P, (m + 1) * P),
                                           parts(h_part[l], k, 0, S), k == 0, k == DC - 1)
                        if m % 2:
                            last.then_inc(ff_mm, 1)
                for l in range(LANES):
                    for c in range(TC):
                        for k in range(FC):
                            if c == 0 and k % 2 == 0:
                                pe.wait_ge(ff_lo, BANKS * LANES * i + (BANKS * l + k // 2 + 1))
                            last = matmul3(pe, bank(l, 0)[:, c * D:(c + 1) * D], parts(a_part[l], k, c * P, (c + 1) * P),
                                           parts(w2, k, 0, D), k == 0, k == FC - 1)
                    last.then_inc(s["out_mm"], 1)
                    next_(l)
            turns(pe, prepare, work)

        @block.scalar
        def _(act):
            def prepare(i, l):
                n = LANES * i + (l + 1)
                act.wait_ge(s["normT"], n)
                for c in range(DC):
                    last = act.activation(h[l][:, c, :], bank(l, 1)[:, c * S:(c + 1) * S], ACT.Identity,
                                          bias=vecs[:, VEC["beta2"] + c:VEC["beta2"] + c + 1],
                                          scale=vecs[:, VEC["g2"] + c:VEC["g2"] + c + 1])
                last.then_inc(s["h"], 1)
                act.wait_ge(s["h"], n)
                act.activation(h_part[l][:, 0, :, :], h[l][:, :, :], ACT.Copy).then_inc(s["h_hi"], 1)

            def work(i, next_):
                for l in range(LANES):
                    for j in range(BANKS):
                        n = BANKS * LANES * i + (BANKS * l + j + 1)
                        act.wait_ge(ff_mm, n)
                        for m in (2 * j, 2 * j + 1):
                            last = act.activation(act_[l][:, m, :], bank(l, j)[:, (m % 2) * S:(m % 2 + 1) * S],
                                                  ACT.Gelu_apprx_sigmoid, bias=vecs[:, VEC["ff_b1"] + m:VEC["ff_b1"] + m + 1])
                        last.then_inc(ff_act, 1)
                        act.wait_ge(ff_act, n)
                        act.activation(a_part[l][:, 0, 2 * j:2 * j + 2, :], act_[l][:, 2 * j:2 * j + 2, :],
                                       ACT.Copy).then_inc(ff_hi, 1)
                for l in range(LANES):
                    next_(l)
            turns(act, prepare, work)

        @block.vector
        def _(dve):
            def normalised(i, l):
                n = LANES * i + (l + 1)
                for r in range(TC):
                    last = dve.bn_stats(bn[l][:, r, :], t["x3"][:, bass.ds(LANES * i + l, 1), r, :].rearrange("p o d -> p (o d)"))
                last.then_inc(s["own"], 1)
                wait_apart(dve, s["own"], 2 * LANES * i + (2 * l + 1))
                for r in range(TC):
                    last = dve.bn_aggr(mv[l][:, r, :], bn[l][:, r, :])
                last.then_inc(s["own"], 1)
                dve.wait_ge(s["own"], 2 * LANES * i + (2 * l + 2))
                dve.tensor_scalar(rv[l][:, :], mv[l][:, :, 1], EPS, None, ALU.add).then_inc(s["ve"], 1)
                dve.wait_ge(s["rstd"], n)
                for r in range(TC):
                    last = dve.tensor_scalar(norm[l][:, r, :], t["x3"][:, bass.ds(LANES * i + l, 1), r, :].rearrange("p o d -> p (o d)"),
                                             mv[l][:, r, 0:1], rs[l][:, r:r + 1], ALU.subtract, ALU.mult)
                last.then_inc(s["norm"], 1)

            def low(i, l):
                n = LANES * i + (l + 1)
                dve.wait_ge(s["h_hi"], n)
                dve.tensor_tensor(h_part[l][:, 1, :, :], h[l][:, :, :], h_part[l][:, 0, :, :].bitcast(F32),
                                  ALU.subtract).then_inc(s["h_lo"], 1)

            def prepare(i, l):
                normalised(i, l)
                if isinstance(i, int):
                    low(i, l)

            def work(i, next_):
                for l in range(LANES):
                    for j in range(BANKS):
                        dve.wait_ge(ff_hi, BANKS * LANES * i + (BANKS * l + j + 1))
                        dve.tensor_tensor(a_part[l][:, 1, 2 * j:2 * j + 2, :], act_[l][:, 2 * j:2 * j + 2, :],
                                          a_part[l][:, 0, 2 * j:2 * j + 2, :].bitcast(F32), ALU.subtract).then_inc(ff_lo, 1)
                for l in range(LANES):
                    next_(l)
                for l in range(LANES):
                    n = LANES * i + (l + 1)
                    dve.wait_ge(s["out_mm"], n)
                    dve.wait_ge(s["x4b"], n)
                    if isinstance(i, int):
                        dve.wait_ge(s["rotated"], LANES * (i - 1) + (l + 1))
                    dve.tensor_tensor(x5[l][:, :, :], bank(l, 0).rearrange("p (c d) -> p c d", c=TC), x4(i, l),
                                      ALU.add).then_inc(s["x5"], 1)
                    if not isinstance(i, int):
                        low(i + 1, l)
            turns(dve, prepare, work)

        @block.gpsimd
        def _(pool):
            def prepare(i, l):
                n = LANES * i + (l + 1)
                pool.wait_ge(s["ve"], n)
                pool.tensor_tensor(rs[l][:, :], rv[l][:, :], t["halves"][:, 0:TC], ALU.pow).then_inc(s["rstd"], 1)
                pool.wait_ge(s["norm"], n)
                pool.tensor_tensor(x4(i, l), x4(i, l), rows[:, ROWS["ff_b2"]:ROWS["ff_b2"] + 1, :].to_broadcast([P, TC, D]),
                                   ALU.add).then_inc(s["x4b"], 1)

            def work(i, next_):
                for l in range(LANES):
                    next_(l)
                for l in range(LANES):
                    n = LANES * i + (l + 1)
                    fours = [tile[:, :, :].rearrange("p c (g j) -> p (c g) j", j=4) for tile in (x5[l], rot1[l], rot2[l])]
                    pool.wait_ge(s["x5"], n)
                    pool.wait_ge(stored[l], 16 * i + 16)
                    pool.tensor_tensor(fours[1], fours[0], t["rot"][:, 0, bass.ds(LANES * i + l, 1), :]
                                       .to_broadcast([P, TC * D // 4, 4]), ALU.mult).then_inc(s["rot1"], 1)
                    for j in range(4):
                        last = pool.tensor_tensor(fours[2][:, :, j:j + 1], fours[0][:, :, (j ^ 1):(j ^ 1) + 1],
                                                  t["rot"][:, 1, bass.ds(LANES * i + l, 1), j:j + 1]
                                                  .to_broadcast([P, TC * D // 4, 1]), ALU.mult)
                    last.then_inc(s["rot2"], 1)
                    pool.wait_ge(s["rot1"], n)
                    pool.wait_ge(s["rot2"], n)
                    pool.tensor_tensor(rot1[l][:, :, :], rot1[l][:, :, :], rot2[l][:, :, :], ALU.add).then_inc(s["rotated"], 1)
            for l in range(LANES):
                pool.sem_inc(stored[l], 16)
            turns(pool, prepare, work)


_VEC_ORDER = ("L0_cond_b1", "L0_cond_b2", "L0_cond_bsc", "L0_cond_bsh", "L0_cond_b_in", "L1_cond_b1_nr", "L1_cond_b1_tsr",
              "L1_cond_b1_sr", "L1_cond_b2_sr", "L2_cond_bq", "L2_cond_bk", "L2_cond_b1", "L2_cond_g2", "L2_cond_beta2")
_ROW_ORDER = ("L0_cond_b_out", "L1_cond_b2_nr", "L1_cond_b2_tsr", "L1_cond_b3_sr", "L1_cond_gamma", "L1_cond_beta",
              "L2_cond_bv", "L2_cond_bo", "L2_cond_b2")
_WEIGHTS = {"W_in": "L0_cond_W_in", "W_out": "L0_cond_W_out", "nr_w1": "L1_cond_w1_nr", "nr_w2": "L1_cond_w2_nr",
            "tsr_w1": "L1_cond_w1_tsr", "tsr_w2": "L1_cond_w2_tsr", "sr_w1": "L1_cond_w1_sr", "sr_w2": "L1_cond_w2_sr",
            "sr_w3": "L1_cond_w3_sr", "Wq": "L2_cond_Wq", "Wk": "L2_cond_Wk", "Wv": "L2_cond_Wv", "Wo": "L2_cond_Wo"}
_AS_THEY_ARE = ("x", "condB_t", "itok_B_0_2", "itok_B_34_63", "fside_Bx16xSxS_0", "condB_theta", "condB_phi",
                "L0_cond_W1", "L0_cond_W2", "L0_cond_Wsc", "L0_cond_Wsh", "L0_cond_gamma", "L0_cond_beta",
                "L2_cond_W_ada", "L2_cond_b_ada")


def constants():
    def freqs(half):
        return np.exp(np.arange(half, dtype=np.float32) * np.float32(-np.log(10000.0) / (half - 1)))
    consts = np.zeros((P, 4), np.float32)
    consts[:, 0] = np.tile(freqs(E0 // 2), 2)
    consts[:, 1] = freqs(D // 2)
    consts[E0 // 2:, 2] = 0.25
    consts[E0 // 2:, 3] = np.pi / 2
    odd = np.zeros((P, 8), np.float32)
    for head in range(8):
        odd[head * HD:(head + 1) * HD, head] = 1.0
    return {"ident": np.eye(P, dtype=np.float32), "consts": consts, "head_rows": odd}


def by_partition(weight):
    k, m = weight.shape
    return weight.reshape(k // P, P, m).transpose(1, 0, 2).reshape(P, k // P * m)


def laid_out(inputs):
    arrays = {n: np.ascontiguousarray(inputs[n]) for n in _AS_THEY_ARE}
    arrays |= {n: np.ascontiguousarray(inputs[src]) for n, src in _WEIGHTS.items()}
    arrays["vec_rows"] = np.concatenate([np.asarray(inputs[n]) for n in _VEC_ORDER]).reshape(-1, P)
    arrays["rows"] = np.concatenate([np.asarray(inputs[n]) for n in _ROW_ORDER])
    arrays["mask"] = np.ascontiguousarray(inputs["mask_Bx1xSxS_bk0"])
    arrays["ff"] = np.concatenate([by_partition(np.asarray(inputs[n])) for n in ("L2_cond_W1", "L2_cond_W2")], axis=1)
    return arrays | constants()


def kernel(**inputs):
    import concourse.bacc as bacc
    from concourse.bass_utils import run_bass_kernel_spmd as run

    arrays = laid_out(inputs)
    nc = bacc.Bacc("TRN2", target_bir_lowering=False, num_devices=1)
    a = {n: nc.dram_tensor(f"in_{n}", v.shape, mybir.dt.from_np(v.dtype), kind="ExternalInput").ap()
         for n, v in arrays.items()}
    out = nc.dram_tensor("out", (B, S, D), F32, kind="ExternalOutput").ap()
    build_program(nc, a, out)
    r = run(nc, [{f"in_{n}": v for n, v in arrays.items()}], core_ids=[0])
    return r.results[0]["out"]
```

```python
from contextlib import ExitStack

import numpy as np
import concourse.bass as bass
from concourse import mybir

F32 = mybir.dt.float32
F32R = mybir.dt.float32r
BF16 = mybir.dt.bfloat16
F16 = mybir.dt.float16
I32 = mybir.dt.int32
U8 = mybir.dt.uint8
ALU = mybir.AluOpType
ACT = mybir.ActivationFunctionType
AX = mybir.AxisListType

P = 128
B = 16
S = 256
D = 256
TC = S // P
DC = D // P
E0 = 128
EH = 4 * E0
HC = EH // P
FF = 1024
FC = FF // P
NH = 16
HD = D // NH
LANES = 2
LANES_A = 4
TURN_SLOTS = 44
SLOT = (0, 1, 1, 2, 2, 3, 5, 7, 7, 10, 14, 14, 14, 15, 17, 18, 18, 19, 20, 20, 22, 24, 26, 28, 30, 33, 36,
        37, 40, 43, 44, 45, 49, 51, 51, 52, 53, 54, 55, 56, 63)
EPS = 1e-5
TWO_PI = 2.0 * np.pi
PI_A = 6.28125
PI_B = float(np.float32(np.floor((TWO_PI - PI_A) * 2 ** 21) / 2 ** 21))
PI_C = float(TWO_PI - PI_A - PI_B)
ROUND = float(3 * 2 ** 22)
SIN_EDGE = 3.1415925
MASKED = -float(2.0 ** 100)

VEC = {}
_at = 0
for _name, _n in (("L0_b1", HC), ("L0_b2", HC), ("L0_bsc", DC), ("L0_bsh", DC), ("L0_b_in", DC),
                  ("nr_b1", DC), ("tsr_b1", DC), ("sr_b1", 4), ("sr_b2", DC),
                  ("bq", DC), ("bk", DC), ("ff_b1", FC), ("g2", DC), ("beta2", DC)):
    VEC[_name] = _at
    _at += _n
NVEC = _at
ROWS = {n: i for i, n in enumerate(("b_out", "nr_b2", "tsr_b2", "sr_b3", "gamma1", "beta1", "bv", "bo", "ff_b2"))}


def weight_shapes():
    first = [("W_in", DC, D), ("W_out", DC, D), ("nr_w1", DC, D), ("nr_w2", DC, D), ("tsr_w1", DC, D),
             ("tsr_w2", DC, D), ("sr_w1", DC, 2 * D), ("sr_w2", 4, D), ("sr_w3", DC, D)]
    second = [("Wq", DC, D), ("Wk", DC, D), ("Wv", DC, D), ("Wo", DC, D)]
    return first, second


def build_program(nc, a, out):
    with ExitStack() as whole:
        def sb(name, shape, dt=F32, ctx=whole):
            return ctx.enter_context(nc.sbuf_tensor(name, shape, dt))

        first, second = weight_shapes()
        t = dict(
            w={n: sb(f"w_{n}", [P, 2, k, m], F32R) for n, k, m in second},
            x3=sb("x3", [P, B, TC, D]),
            ident=sb("ident", [P, P]),
            vecs=sb("vecs", [P, NVEC]),
            rows=sb("rows", [P, len(ROWS), D]),
            rot=sb("rot", [P, 2, B, 4]),
            halves=sb("halves", [P, 2]),
        )
        ps = whole.enter_context(nc.psum_tensor("ps", [P, 8, 512], F32))
        ada = nc.dram_tensor("ada_scratch", [B, 2 * D], F32, kind="Internal").ap()
        with ExitStack() as ctx:
            t["w"] |= {n: sb(f"w_{n}", [P, k, m], ctx=ctx) for n, k, m in first}
            t |= dict(
                mean_of=sb("mean_of", [P, P], ctx=ctx),
                scale0=sb("scale0", [P, DC, B], ctx=ctx),
                shift0=sb("shift0", [P, DC, B], ctx=ctx),
                gammaT=sb("gammaT", [P, DC, S], ctx=ctx),
                betaT=sb("betaT", [P, DC, S], ctx=ctx),
                cond=sb("cond", [1, B], I32, ctx),
                x=[sb(f"x_lane{l}", [P, TC, D], ctx=ctx) for l in range(LANES_A)],
                x_in=[ctx.enter_context(nc.semaphore(f"x_in{l}")) for l in range(LANES_A)],
            )
            with nc.cleanup_on_exit():
                conditioning(nc, a, t, ps, ada, second, first)
            with nc.cleanup_on_exit():
                first_layers(nc, a, t, ps, ada)
        with ExitStack() as ctx:
            t["ff"] = sb("w_ff", [P, 2, DC * FF + FC * D], F32R, ctx)
            attention(nc, a, t, ps)
            feed_forward(nc, a, t, ps, out)


def load_x(sp, a, t, b, l):
    sp.dma_start(t["x"][l][:, :, :], a["x"][b].rearrange("(c p) d -> p c d", p=P)).then_inc(t["x_in"][l], 16)


def conditioning(nc, a, t, ps, ada, split, whole):
    w = t["w"]
    with ExitStack() as ctx:
        def sb(name, shape, dt=F32):
            return ctx.enter_context(nc.sbuf_tensor(name, shape, dt))

        def sem(name):
            return nc.alloc_semaphore(name)

        NST = 4
        stage = sb("p_stage", [P, NST, 1024])
        w1 = sb("p_w1", [P, 1, EH])
        w2 = sb("p_w2", [P, HC, EH])
        wsc = sb("p_wsc", [P, HC, D])
        wsh = sb("p_wsh", [P, HC, D])
        wada = sb("p_wada", [P, DC, 2 * D])
        vec_rows = sb("p_vec_rows", [NVEC, P])
        gb = sb("p_gb", [P, 2, TC, D])
        bada = sb("p_bada", [B, 2 * D])
        consts = sb("p_consts", [P, 4])
        tb = sb("p_tb", [P, B])
        ti = sb("p_ti", [P, B], I32)
        dv = sb("p_divide", [P, 6, B])
        NA = 7 * B
        arg = sb("p_arg", [P, NA])
        turn = sb("p_turn", [P, NA])
        red = sb("p_red", [P, NA])
        trig = sb("p_trig", [P, NA])
        silu2 = sb("p_silu2", [P, 2, B])
        h1 = sb("p_h1", [P, HC, B])
        h2 = sb("p_h2", [P, HC, B])
        ada_rows = sb("p_ada_rows", [B, 2 * D])

        consts_in = sem("p_consts_in")
        vecs_in = sem("p_vecs_in")
        rows_in = sem("p_rows_in")
        whole_in = sem("p_whole_in")
        gb_in = sem("p_gb_in")
        w_in = {n: sem(f"p_in_{n}") for n in ("w1", "w2", "wsc", "wsh", "wada")}
        stage_in = [sem(f"p_stage_in{i}") for i in range(NST)]
        hi_done = sem("p_hi_done")
        lo_done = sem("p_lo_done")
        fills = sem("p_fills")
        step = sem("p_vector_step")
        args_done = sem("p_args_done")
        sin_done = sem("p_sin_done")
        silu2_done = sem("p_silu2_done")
        vecT = sem("p_vecT")
        vecs_done = sem("p_vecs_done")
        gbT = sem("p_gbT")
        gbT_done = sem("p_gbT_done")
        h1_mm, h1_done = sem("p_h1_mm"), sem("p_h1_done")
        h2_mm, h2_done = sem("p_h2_mm"), sem("p_h2_done")
        sc_mm, ada_mm, ada_done, ada_out = sem("p_sc_mm"), sem("p_ada_mm"), sem("p_ada_done"), sem("p_ada_out")

        pieces = [(n, k0, min(k, k0 + 1024 // m) - k0, m) for n, k, m in split
                  for k0 in range(0, k, 1024 // m)]

        def factor(name):
            return HD ** -0.5 if name == "Wq" else 1.0

        block = ctx.enter_context(nc.Block())

        @block.sync
        def _(sp):
            for dst, src in ((t["ident"][:, :], a["ident"]), (consts[:, :], a["consts"]),
                             (tb[:, :], a["condB_t"].partition_broadcast(P)),
                             (ti[:, :], a["itok_B_34_63"].partition_broadcast(P)),
                             (arg[:, 3 * B:4 * B], a["condB_theta"].partition_broadcast(P)),
                             (arg[:, 4 * B:5 * B], a["condB_phi"].partition_broadcast(P)),
                             (t["cond"][:, :], a["itok_B_0_2"].rearrange("(o b) -> o b", o=1)),
                             (bada[:, :], a["L2_cond_b_ada"].partition_broadcast(B))):
                sp.dma_start(dst, src).then_inc(consts_in, 16)
            sp.dma_start(vec_rows[:, :], a["vec_rows"]).then_inc(vecs_in, 16)
            sp.dma_start(gb[:, 0, :, :], a["L0_cond_gamma"].rearrange("(c p) d -> p c d", p=P)).then_inc(gb_in, 16)
            sp.dma_start(gb[:, 1, :, :], a["L0_cond_beta"].rearrange("(c p) d -> p c d", p=P)).then_inc(gb_in, 16)
            sp.dma_start(w1[:, 0, :], a["L0_cond_W1"]).then_inc(w_in["w1"], 16)
            sp.dma_start(wada[:, :, :], a["L2_cond_W_ada"].rearrange("(k p) n -> p k n", p=P)).then_inc(w_in["wada"], 16)
            sp.dma_start(w2[:, :, :], a["L0_cond_W2"].rearrange("(k p) n -> p k n", p=P)).then_inc(w_in["w2"], 16)
            sp.dma_start(wsc[:, :, :], a["L0_cond_Wsc"].rearrange("(k p) n -> p k n", p=P)).then_inc(w_in["wsc"], 16)
            sp.dma_start(wsh[:, :, :], a["L0_cond_Wsh"].rearrange("(k p) n -> p k n", p=P)).then_inc(w_in["wsh"], 16)
            sp.dma_start(t["rows"][:, :, :], a["rows"].partition_broadcast(P)).then_inc(rows_in, 16)
            for l in range(LANES_A):
                load_x(sp, a, t, l, l)
            for n, _k, _m in whole:
                sp.dma_start(w[n][:, :, :], a[n].rearrange("(k p) m -> p k m", p=P)).then_inc(whole_in, 16)
            sp.wait_ge(ada_done, 2)
            sp.dma_start(ada, ada_rows[:, :]).then_inc(ada_out, 16)
            sp.wait_ge(ada_out, 16)
            sp.wait_ge(rows_in, 16)
            sp.wait_ge(whole_in, 16 * len(whole))

        @block.gpsimd
        def _(pool):
            pool.memset(t["mean_of"][:, :], 1.0 / P).then_inc(fills, 1)
            pool.memset(t["halves"][:, :], -0.5).then_inc(fills, 1)
            for i, (n, k0, nk, m) in enumerate(pieces):
                if i >= NST:
                    pool.wait_ge(lo_done, i - NST + 1)
                pool.dma_start(stage[:, i % NST, 0:nk * m].rearrange("p (k m) -> p k m", m=m),
                               a[n].rearrange("(k p) m -> p k m", p=P)[:, k0:k0 + nk, :]).then_inc(stage_in[i % NST], 16)

        @block.scalar
        def _(act):
            act.wait_ge(args_done, 1)
            act.activation(trig[:, :], red[:, :], ACT.Sin).then_inc(sin_done, 1)
            act.wait_ge(sin_done, 1)
            act.activation(silu2[:, :, :], trig[:, B:3 * B].rearrange("p (c b) -> p c b", c=2),
                           ACT.Silu).then_inc(silu2_done, 1)
            act.wait_ge(vecs_done, 1)
            act.wait_ge(h1_mm, 1)
            for m in range(HC):
                last = act.activation(h1[:, m, :], ps[:, 0, m * B:(m + 1) * B], ACT.Silu,
                                      bias=t["vecs"][:, VEC["L0_b1"] + m:VEC["L0_b1"] + m + 1])
            last.then_inc(h1_done, 1)
            for i, (n, k0, nk, m) in enumerate(pieces):
                act.wait_ge(stage_in[i % NST], 16 * (i // NST + 1))
                act.activation(w[n][:, 0, k0:k0 + nk, :].rearrange("p k m -> p (k m)"), stage[:, i % NST, 0:nk * m],
                               ACT.Copy, scale=factor(n)).then_inc(hi_done, 1)

        @block.vector
        def _(dve):
            n_step = [0]

            def then(ins):
                n_step[0] += 1
                ins.then_inc(step, 1)
                dve.wait_ge(step, n_step[0])

            dve.wait_ge(consts_in, 16 * 8)
            then(dve.tensor_scalar(arg[:, 0:B], tb[:, :], 5000.0, consts[:, 0:1], ALU.mult, ALU.mult))
            num, quot, big, high, low, rem = (dv[:, j, :] for j in range(6))
            then(dve.tensor_copy(num, ti[:, :]))
            then(dve.tensor_scalar(quot, num, 0.01, None, ALU.mult))
            then(dve.tensor_scalar(big, quot, 4097.0, None, ALU.mult))
            then(dve.tensor_tensor(high, big, quot, ALU.subtract))
            then(dve.tensor_tensor(high, big, high, ALU.subtract))
            then(dve.tensor_tensor(low, quot, high, ALU.subtract))
            then(dve.scalar_tensor_tensor(rem, high, -100.0, num, ALU.mult, ALU.add))
            then(dve.scalar_tensor_tensor(rem, low, -100.0, rem, ALU.mult, ALU.add))
            then(dve.scalar_tensor_tensor(arg[:, 6 * B:7 * B], rem, 0.01, quot, ALU.mult, ALU.add))
            then(dve.tensor_scalar(arg[:, B:2 * B], arg[:, 6 * B:7 * B], 4000.0, consts[:, 1:2], ALU.mult, ALU.mult))
            then(dve.tensor_copy(arg[:, 2 * B:3 * B], arg[:, B:2 * B]))
            then(dve.tensor_copy(arg[:, 5 * B:7 * B], arg[:, 3 * B:5 * B]))
            sin_part = ((0, B, consts[:, 2:3], consts[:, 3:4]), (B, 2 * B, 0.0, 0.0), (2 * B, 3 * B, 0.25, np.pi / 2),
                        (3 * B, 5 * B, 0.0, 0.0), (5 * B, 7 * B, 0.25, np.pi / 2))
            for lo, hi, turns, _angle in sin_part:
                then(dve.tensor_scalar(turn[:, lo:hi], arg[:, lo:hi], 1.0 / TWO_PI, turns, ALU.mult, ALU.add))
            then(dve.tensor_scalar(turn[:, :], turn[:, :], ROUND, None, ALU.add))
            then(dve.tensor_scalar(turn[:, :], turn[:, :], -ROUND, None, ALU.add))
            then(dve.scalar_tensor_tensor(red[:, :], turn[:, :], -PI_A, arg[:, :], ALU.mult, ALU.add))
            then(dve.scalar_tensor_tensor(red[:, :], turn[:, :], -PI_B, red[:, :], ALU.mult, ALU.add))
            then(dve.scalar_tensor_tensor(red[:, :], turn[:, :], -PI_C, red[:, :], ALU.mult, ALU.add))
            for lo, hi, _turns, angle in sin_part:
                then(dve.tensor_scalar(red[:, lo:hi], red[:, lo:hi], angle, SIN_EDGE, ALU.add, ALU.min))
            dve.tensor_scalar(red[:, :], red[:, :], -SIN_EDGE, None, ALU.max).then_inc(args_done, 1)
            dve.wait_ge(vecT, 1)
            dve.tensor_copy(t["vecs"][:, :], ps[:, 1, 0:NVEC]).then_inc(vecs_done, 1)
            dve.wait_ge(vecs_done, 1)
            dve.tensor_scalar(t["vecs"][:, VEC["bq"]:VEC["bq"] + DC], t["vecs"][:, VEC["bq"]:VEC["bq"] + DC],
                              factor("Wq"), None, ALU.mult)
            dve.wait_ge(sin_done, 1)
            for j in range(4):
                at = (j // 2) * B
                dve.tensor_copy(t["rot"][:, 0, :, j], trig[:, 5 * B + at:6 * B + at])
                dve.tensor_scalar(t["rot"][:, 1, :, j], trig[:, 3 * B + at:4 * B + at], -1.0 if j % 2 else 1.0,
                                  None, ALU.mult)
            dve.wait_ge(gbT, 1)
            for i, name in enumerate(("gammaT", "betaT")):
                dve.tensor_copy(t[name][:, :, :].rearrange("p c s -> p (c s)"), ps[:, 4 + i, :]).then_inc(gbT_done, 1)
            for i, (n, k0, nk, m) in enumerate(pieces):
                dve.wait_ge(hi_done, i + 1)
                dve.scalar_tensor_tensor(w[n][:, 1, k0:k0 + nk, :].rearrange("p k m -> p (k m)"),
                                         stage[:, i % NST, 0:nk * m], factor(n),
                                         w[n][:, 0, k0:k0 + nk, :].rearrange("p k m -> p (k m)").bitcast(F32),
                                         ALU.mult, ALU.subtract).then_inc(lo_done, 1)
            dve.wait_ge(h2_mm, 1)
            for m in range(HC):
                last = dve.tensor_scalar(h2[:, m, :], ps[:, 2, m * B:(m + 1) * B],
                                         t["vecs"][:, VEC["L0_b2"] + m:VEC["L0_b2"] + m + 1], None, ALU.add)
            last.then_inc(h2_done, 1)
            dve.wait_ge(ada_mm, 1)
            dve.tensor_tensor(ada_rows[:, :], ps[0:B, 6, :], bada[:, :], ALU.add).then_inc(ada_done, 1)
            dve.wait_ge(ada_done, 1)
            dve.tensor_scalar(ada_rows[:, 0:D], ada_rows[:, 0:D], 1.0, None, ALU.add).then_inc(ada_done, 1)
            dve.wait_ge(sc_mm, 1)
            for m in range(DC):
                for q, (dst, b) in enumerate((("scale0", "L0_bsc"), ("shift0", "L0_bsh"))):
                    dve.tensor_scalar(t[dst][:, m, :], ps[:, 3, (q * DC + m) * B:(q * DC + m + 1) * B],
                                      t["vecs"][:, VEC[b] + m:VEC[b] + m + 1], None, ALU.add)

        @block.tensor
        def _(pe):
            pe.wait_ge(consts_in, 16 * 8)
            pe.wait_ge(vecs_in, 16)
            pe.transpose(ps[:, 1, 0:NVEC], vec_rows[:, :], t["ident"][0:NVEC, 0:NVEC]).then_inc(vecT, 1)
            pe.wait_ge(gb_in, 32)
            for q in range(2):
                for c in range(DC):
                    for s in range(TC):
                        last = pe.transpose(ps[:, 4 + q, c * S + s * P:c * S + (s + 1) * P],
                                            gb[:, q, s, c * P:(c + 1) * P], t["ident"][:, :])
            last.then_inc(gbT, 1)
            pe.wait_ge(w_in["w1"], 16)
            pe.wait_ge(sin_done, 1)
            for m in range(HC):
                last = pe.matmul(ps[:, 0, m * B:(m + 1) * B], w1[:, 0, m * P:(m + 1) * P], trig[:, 0:B],
                                 start=True, stop=True)
            last.then_inc(h1_mm, 1)
            pe.wait_ge(w_in["wada"], 16)
            pe.wait_ge(silu2_done, 1)
            for k in range(DC):
                last = pe.matmul(ps[0:B, 6, :], silu2[:, k, :], wada[:, k, :], start=(k == 0), stop=(k == DC - 1))
            last.then_inc(ada_mm, 1)
            pe.wait_ge(h1_done, 1)
            pe.wait_ge(w_in["w2"], 16)
            for m in range(HC):
                for k in range(HC):
                    last = pe.matmul(ps[:, 2, m * B:(m + 1) * B], w2[:, k, m * P:(m + 1) * P], h1[:, k, :],
                                     start=(k == 0), stop=(k == HC - 1))
            last.then_inc(h2_mm, 1)
            pe.wait_ge(h2_done, 1)
            pe.wait_ge(w_in["wsc"], 16)
            pe.wait_ge(w_in["wsh"], 16)
            for q, wt in enumerate((wsc, wsh)):
                for m in range(DC):
                    for k in range(HC):
                        last = pe.matmul(ps[:, 3, (q * DC + m) * B:(q * DC + m + 1) * B], wt[:, k, m * P:(m + 1) * P],
                                         h2[:, k, :], start=(k == 0), stop=(k == HC - 1))
            last.then_inc(sc_mm, 1)


def wait_apart(eng, semaphore, count):
    eng.wait_ge(semaphore, count)
    eng.nop(nofuse=True)


def matmul3(pe, out, lhs, rhs, first, last):
    pe.matmul(out, lhs[0], rhs[0], start=first, stop=False)
    pe.matmul(out, lhs[0], rhs[1], start=False, stop=False)
    return pe.matmul(out, lhs[1], rhs[0], start=False, stop=last)


def parts(tile, k, lo, hi):
    return tile[:, 0, k, lo:hi], tile[:, 1, k, lo:hi]


def by_route(eng, route, body):
    with eng.If(route == 0):
        body(0)
    with eng.Else():
        with eng.If(route == 1):
            body(1)
        with eng.Else():
            body(2)


def flat(tile):
    return tile[:, :, :].rearrange("p c s -> p (c s)")


def first_layers(nc, a, t, ps, ada):
    w, vecs, rows = t["w"], t["vecs"], t["rows"]
    XT = MA = 0
    MB = Z = 1
    HIDDEN = (("nr_w1", "nr_b1", DC), ("tsr_w1", "tsr_b1", DC), ("sr_w1", "sr_b1", 4))
    OUTER = (("nr_w2", "nr_b2"), ("tsr_w2", "tsr_b2"), ("sr_w3", "sr_b3"))
    (X_IN, X_AGGR, X_SQUARE, X_MEAN, NORM0, NORM0_VAR, NORM0_U, NORM0_V, SILU0, Y_MM, Y, Y_STATS, Y_AGGR, Y_SQUARE,
     Y_MEAN, NORM1, NORM1_VAR, NORM1_U, NORM1_V, SILU1, OUT0, X1, X1_T, X1_COPY, HIDDEN_MM, GELU, HIDDEN2_MM,
     GELU2, OUT1, SUM, SUM_STATS, SUM_AGGR, SUM_VAR, RSTD2, X2, STATS3, AGGR3, VAR3, RSTD3, X3, NEXT_ADA) = range(len(SLOT))
    TURNS = B // LANES_A

    def run_stages(eng, stage):
        apart = TURN_SLOTS // LANES_A
        last = apart * (LANES_A - 1) + SLOT[-1]
        first = last - TURN_SLOTS + 1
        ahead = (first + TURN_SLOTS - 1) // TURN_SLOTS

        def slot(k, i, turns):
            for l in range(LANES_A):
                for s in range(len(SLOT)):
                    turn, rest = divmod(k - apart * l - SLOT[s], TURN_SLOTS)
                    if rest == 0 and turn in turns:
                        stage(s, i + turn if turn else i, l)

        for k in range(first):
            slot(k, 0, range(TURNS))
        with eng.Fori(0, TURNS - ahead) as i:
            for k in range(first, first + TURN_SLOTS):
                slot(k, i, range(ahead + 1))
        for k in range(first + TURN_SLOTS * (TURNS - ahead), last + TURN_SLOTS * (TURNS - 1) + 1):
            slot(k, 0, range(TURNS))

    with ExitStack() as ctx:
        def sb(name, shape, dt=F32):
            return ctx.enter_context(nc.sbuf_tensor(name, shape, dt))

        def sem(name):
            return nc.alloc_semaphore(name)

        def per_lane(name, shape, dt=F32):
            return [sb(f"{name}{l}", shape, dt) for l in range(LANES_A)]

        x = t["x"]
        xb = per_lane("a_xb", [P, TC, D])
        f = per_lane("a_f", [P, 4, S])
        v = per_lane("a_v", [P, DC, S])
        y = per_lane("a_y", [P, DC, S])
        x2 = per_lane("a_x2", [P, TC, D])
        z = per_lane("a_z", [P, TC, D])
        xs = per_lane("a_xs", [P, TC, D])
        x1 = per_lane("a_x1", [P, TC, D])
        adab = per_lane("a_ada", [P, 2, D])
        st = per_lane("a_st", [P, 2, 8])
        bn = per_lane("a_bn", [P, TC, 6])
        bt = per_lane("a_bt", [P, TC, 6])
        mv = per_lane("a_mv", [P, 2, TC, 2])
        rs = per_lane("a_rs", [P, 2, TC])
        rv = per_lane("a_rv", [P, 2, TC])

        s = {n: sem(f"a_{n}") for n in (
            "xT", "stat_mm0", "stat_mm1", "y_mm", "out0_mm", "x1T", "g_mm", "out1_mm",
            "s0", "y", "s1", "x1_copy", "g",
            "in0", "ve0", "v0", "in1", "ve1", "v1", "x1",
            "ve2", "t1", "ve3", "t2",
            "xb", "rstd0", "rstd1", "xb2", "rstd2", "x2", "rstd3", "t2s", "x3")}
        own, OWN = [sem(f"a_vector_own{l}") for l in range(LANES_A)], 10
        own_t, OWN_T = [sem(f"a_vector_own_t{l}") for l in range(LANES_A)], 4
        r = {n: [sem(f"a_{n}_{l}") for l in range(LANES_A)] for n in ("g2_mm", "g2", "y1")}
        x_in = t["x_in"]
        ada_in = [sem(f"a_ada_in{l}") for l in range(LANES_A)]

        def bank(l, i):
            return ps[:, 2 * l + i, :]

        block = ctx.enter_context(nc.Block())

        @block.sync
        def _(sp):
            for l in range(LANES_A):
                sp.dma_start(flat(adab[l]), ada[l].partition_broadcast(P)).then_inc(ada_in[l], 16)
            with sp.Fori(1, B // LANES_A) as i:
                b = i * LANES_A
                for l in range(LANES_A):
                    sp.wait_ge(s["xT"], b + (l + 1 - LANES_A))
                    sp.wait_ge(s["in0"], b + (l + 1 - LANES_A))
                    wait_apart(sp, s["xb"], b + (l + 1 - LANES_A))
                    load_x(sp, a, t, b + l, l)

        @block.tensor
        def _(pe):
            def transposes(l, src, done):
                for c in range(DC):
                    for q in range(TC):
                        last = pe.transpose(bank(l, XT)[:, c * S + q * P:c * S + (q + 1) * P],
                                            src[:, q, c * P:(c + 1) * P], t["ident"][:, :])
                last.then_inc(s[done], 1)

            def to_features(l, name, chunks, nk, done):
                for m in range(chunks):
                    for k in range(nk):
                        last = pe.matmul(bank(l, (MA, MB)[m // 2])[:, (m % 2) * S:(m % 2 + 1) * S],
                                         w[name][:, k, m * P:(m + 1) * P], f[l][:, k, :], start=(k == 0), stop=(k == nk - 1))
                last.then_inc(done, 1)

            def to_rows(l, name, done):
                nk = 4 if name == "sr_w2" else DC
                for q in range(TC):
                    for k in range(nk):
                        last = pe.matmul(bank(l, Z)[:, q * D:(q + 1) * D], f[l][:, k, q * P:(q + 1) * P], w[name][:, k, :],
                                         start=(k == 0), stop=(k == nk - 1))
                last.then_inc(s[done], 1)

            def stage(st_, i, l):
                n = LANES_A * i + (l + 1)

                if st_ in (HIDDEN_MM, HIDDEN2_MM, OUT1):
                    route = pe.value_load(t["cond"][0:1, bass.ds(LANES_A * i + l, 1)])
                if st_ == X_IN:
                    pe.wait_ge(x_in[l], 16 * i + 16)
                    transposes(l, x[l], "xT")
                elif st_ in (X_MEAN, Y_MEAN):
                    j = 0 if st_ == X_MEAN else 1
                    pe.wait_ge(s[f"in{j}"], n)
                    pe.matmul(bank(l, Z)[:, 0:2], t["mean_of"][:, :], st[l][:, j, 0:2], start=True,
                              stop=True).then_inc(s[f"stat_mm{j}"], 1)
                elif st_ == Y_MM:
                    pe.wait_ge(s["s0"], n)
                    to_features(l, "W_in", DC, DC, s["y_mm"])
                elif st_ == OUT0:
                    pe.wait_ge(s["s1"], n)
                    to_rows(l, "W_out", "out0_mm")
                elif st_ == X1_T:
                    pe.wait_ge(s["x1"], n)
                    transposes(l, x1[l], "x1T")
                elif st_ == HIDDEN_MM:
                    def product(way):
                        pe.wait_ge(s["x1_copy"], n)
                        to_features(l, HIDDEN[way][0], HIDDEN[way][2], DC, s["g_mm"])
                    by_route(pe, route, product)
                elif st_ == HIDDEN2_MM:
                    def product(way):
                        pe.wait_ge(s["g"], n)
                        if way == 2:
                            to_features(l, "sr_w2", DC, 4, r["g2_mm"][l])
                        else:
                            pe.sem_inc(r["g2_mm"][l], 1)
                    by_route(pe, route, product)
                elif st_ == OUT1:
                    def product(way):
                        pe.wait_ge(r["g2"][l], i + 1)
                        to_rows(l, OUTER[way][0], "out1_mm")
                    by_route(pe, route, product)

            run_stages(pe, stage)

        @block.scalar
        def _(act):
            def silu(l, i, done):
                for c in range(DC):
                    last = act.activation(f[l][:, c, :], v[l][:, c, :], ACT.Silu,
                                          scale=t["scale0"][:, c, bass.ds(LANES_A * i + l, 1)],
                                          bias=t["shift0"][:, c, bass.ds(LANES_A * i + l, 1)])
                last.then_inc(s[done], 1)

            def gelus(l, bias, chunks, done):
                for m in range(chunks):
                    last = act.activation(f[l][:, m, :], bank(l, (MA, MB)[m // 2])[:, (m % 2) * S:(m % 2 + 1) * S],
                                          ACT.Gelu, bias=vecs[:, VEC[bias] + m:VEC[bias] + m + 1])
                last.then_inc(done, 1)

            def stage(st_, i, l):
                n = LANES_A * i + (l + 1)

                if st_ in (SILU0, SILU1):
                    j = 0 if st_ == SILU0 else 1
                    wait_apart(act, s[f"v{j}"], n)
                    silu(l, i, f"s{j}")
                elif st_ == Y:
                    act.wait_ge(s["y_mm"], n)
                    for c in range(DC):
                        last = act.activation(y[l][:, c, :], bank(l, MA)[:, c * S:(c + 1) * S], ACT.Identity,
                                              bias=vecs[:, VEC["L0_b_in"] + c:VEC["L0_b_in"] + c + 1])
                    last.then_inc(s["y"], 1)
                elif st_ == X1_COPY:
                    act.wait_ge(s["x1T"], n)
                    act.activation(f[l][:, 0:DC, :].rearrange("p c s -> p (c s)"), bank(l, XT),
                                   ACT.Copy).then_inc(s["x1_copy"], 1)
                elif st_ == GELU:
                    def hidden(way):
                        act.wait_ge(s["g_mm"], n)
                        gelus(l, HIDDEN[way][1], HIDDEN[way][2], s["g"])
                    by_route(act, act.value_load(t["cond"][0:1, bass.ds(LANES_A * i + l, 1)]), hidden)
                elif st_ == GELU2:
                    def hidden2(way):
                        act.wait_ge(r["g2_mm"][l], i + 1)
                        if way == 2:
                            gelus(l, "sr_b2", DC, r["g2"][l])
                        else:
                            act.sem_inc(r["g2"][l], 1)
                    by_route(act, act.value_load(t["cond"][0:1, bass.ds(LANES_A * i + l, 1)]), hidden2)

                elif st_ == NEXT_ADA:
                    if not isinstance(i, int) or i + 1 < TURNS:
                        wait_apart(act, s["x3"], n)
                        act.dma_start(flat(adab[l]), ada[LANES_A * i + (l + LANES_A)].partition_broadcast(P)).then_inc(ada_in[l], 16)

            run_stages(act, stage)

        @block.vector
        def _(dve):
            def after(l, i, j):
                wait_apart(dve, own[l], OWN * i + j)

            def centre(l, dst, src, factor, j, done):
                for q in range(TC):
                    last = dve.scalar_tensor_tensor(dst[:, q, :], src[:, q, :], mv[l][:, j, q, 0:1], factor,
                                                    ALU.subtract, ALU.mult)
                last.then_inc(s[done], 1)

            def token_stats(l, src):
                for q in range(TC):
                    last = dve.bn_stats(bt[l][:, q, :], src[:, q, :])
                last.then_inc(own_t[l], 1)

            def token_mean(l, i, j):
                wait_apart(dve, own_t[l], OWN_T * i + (2 * j + 1))
                for q in range(TC):
                    last = dve.bn_aggr(mv[l][:, j, q, :], bt[l][:, q, :])
                last.then_inc(own_t[l], 1)

            def token_variance(l, i, j):
                wait_apart(dve, own_t[l], OWN_T * i + (2 * j + 2))
                dve.tensor_scalar(rv[l][:, j, :], mv[l][:, j, :, 1], EPS, None, ALU.add).then_inc(s[f"ve{j + 2}"], 1)

            def stage(st_, i, l):
                n = LANES_A * i + (l + 1)

                if st_ in (X_IN, Y_STATS):
                    if st_ == X_IN:
                        dve.wait_ge(x_in[l], 16 * i + 16)
                    else:
                        dve.wait_ge(s["y"], n)
                    dve.bn_stats(bn[l][:, 0, :], flat(x[l]) if st_ == X_IN else flat(y[l])).then_inc(own[l], 1)
                elif st_ in (X_AGGR, Y_AGGR):
                    j = 0 if st_ == X_AGGR else 1
                    after(l, i, 5 * j + 1)
                    dve.bn_aggr(st[l][:, j, 0:2], bn[l][:, 0, :]).then_inc(own[l], 1)
                elif st_ in (X_SQUARE, Y_SQUARE):
                    j = 0 if st_ == X_SQUARE else 1
                    after(l, i, 5 * j + 2)
                    dve.scalar_tensor_tensor(st[l][:, j, 1:2], st[l][:, j, 0:1], st[l][:, j, 0:1],
                                             st[l][:, j, 1:2], ALU.mult, ALU.add).then_inc(s[f"in{j}"], 1)
                elif st_ in (NORM0, NORM1):
                    j = 0 if st_ == NORM0 else 1
                    dve.wait_ge(s[f"stat_mm{j}"], n)
                    dve.tensor_copy(st[l][:, j, 2:4], bank(l, Z)[:, 0:2]).then_inc(own[l], 1)
                elif st_ in (NORM0_VAR, NORM1_VAR):
                    j = 0 if st_ == NORM0_VAR else 1
                    after(l, i, 5 * j + 3)
                    dve.scalar_tensor_tensor(st[l][:, j, 4:5], st[l][:, j, 2:3], st[l][:, j, 2:3], st[l][:, j, 3:4],
                                             ALU.mult, ALU.subtract).then_inc(own[l], 1)
                elif st_ in (NORM0_U, NORM1_U):
                    j = 0 if st_ == NORM0_U else 1
                    after(l, i, 5 * j + 4)
                    dve.tensor_scalar(st[l][:, j, 5:6], st[l][:, j, 4:5], -1.0, EPS, ALU.mult, ALU.add).then_inc(s[f"ve{j}"], 1)
                    if j == 0:
                        dve.wait_ge(s["xT"], n)
                    dve.scalar_tensor_tensor(flat(v[l]), flat(y[l]) if j else bank(l, XT), st[l][:, j, 2:3],
                                             flat(t["gammaT"]), ALU.subtract, ALU.mult).then_inc(own[l], 1)
                elif st_ in (NORM0_V, NORM1_V):
                    j = 0 if st_ == NORM0_V else 1
                    after(l, i, 5 * j + 5)
                    dve.wait_ge(s[f"rstd{j}"], n)
                    dve.scalar_tensor_tensor(flat(v[l]), flat(v[l]), st[l][:, j, 6:7], flat(t["betaT"]),
                                             ALU.mult, ALU.add).then_inc(s[f"v{j}"], 1)
                elif st_ == X1:
                    dve.wait_ge(s["out0_mm"], n)
                    dve.wait_ge(s["xb"], n)
                    dve.tensor_tensor(flat(x1[l]), bank(l, Z), flat(xb[l]), ALU.add).then_inc(s["x1"], 1)
                elif st_ == SUM:
                    route = dve.value_load(t["cond"][0:1, bass.ds(LANES_A * i + l, 1)])

                    def add():
                        dve.wait_ge(s["out1_mm"], n)
                        dve.wait_ge(s["xb2"], n)
                        dve.tensor_tensor(flat(x1[l]), bank(l, Z), flat(xs[l]), ALU.add).then_inc(r["y1"][l], 1)

                    def add_or_not(way):
                        if way < 2:
                            add()
                            return
                        with dve.If(route == 2):
                            add()
                        with dve.Else():
                            dve.wait_ge(s["out1_mm"], n)
                            dve.sem_inc(r["y1"][l], 1)
                    by_route(dve, route, add_or_not)
                elif st_ == SUM_STATS:
                    dve.wait_ge(r["y1"][l], i + 1)
                    token_stats(l, x1[l])
                elif st_ == SUM_AGGR:
                    token_mean(l, i, 0)
                elif st_ == SUM_VAR:
                    token_variance(l, i, 0)
                    centre(l, x2[l], x1[l], rows[:, ROWS["gamma1"], :], 0, "t1")
                elif st_ == X2:
                    dve.wait_ge(s["t1"], n)
                    dve.wait_ge(s["rstd2"], n)
                    for q in range(TC):
                        last = dve.scalar_tensor_tensor(x2[l][:, q, :], x2[l][:, q, :], rs[l][:, 0, q:q + 1],
                                                        rows[:, ROWS["beta1"], :], ALU.mult, ALU.add)
                    last.then_inc(s["x2"], 1)
                elif st_ == STATS3:
                    dve.wait_ge(s["x2"], n)
                    token_stats(l, x2[l])
                elif st_ == AGGR3:
                    token_mean(l, i, 1)
                elif st_ == VAR3:
                    token_variance(l, i, 1)
                    dve.wait_ge(ada_in[l], 16 * i + 16)
                    centre(l, z[l], x2[l], adab[l][:, 0, :], 1, "t2")

            run_stages(dve, stage)

        @block.gpsimd
        def _(pool):
            def rsqrt(l, dst, src, width, done):
                pool.tensor_tensor(dst, src, t["halves"][:, 0:width], ALU.pow).then_inc(s[done], 1)

            def row(name):
                return rows[:, ROWS[name]:ROWS[name] + 1, :].to_broadcast([P, TC, D])

            def stage(st_, i, l):
                n = LANES_A * i + (l + 1)

                if st_ == X_IN:
                    pool.wait_ge(x_in[l], 16 * i + 16)
                    pool.tensor_tensor(xb[l][:, :, :], x[l][:, :, :], row("b_out"), ALU.add).then_inc(s["xb"], 1)
                elif st_ in (NORM0_U, NORM1_U):
                    j = 0 if st_ == NORM0_U else 1
                    pool.wait_ge(s[f"ve{j}"], n)
                    rsqrt(l, st[l][:, j, 6:7], st[l][:, j, 5:6], 1, f"rstd{j}")
                elif st_ == X1_T:
                    route = pool.value_load(t["cond"][0:1, bass.ds(LANES_A * i + l, 1)])

                    def add_bias(way):
                        pool.wait_ge(s["x1"], n)
                        pool.tensor_tensor(xs[l][:, :, :], x1[l][:, :, :], row(OUTER[way][1]), ALU.add).then_inc(s["xb2"], 1)
                    by_route(pool, route, add_bias)
                elif st_ in (RSTD2, RSTD3):
                    j = 0 if st_ == RSTD2 else 1
                    pool.wait_ge(s[f"ve{j + 2}"], n)
                    rsqrt(l, rs[l][:, j, :], rv[l][:, j, :], TC, f"rstd{j + 2}")
                elif st_ == X3:
                    pool.wait_ge(s["t2"], n)
                    wait_apart(pool, s["rstd3"], n)
                    for q in range(TC):
                        last = pool.tensor_scalar(z[l][:, q, :], z[l][:, q, :], rs[l][:, 1, q:q + 1], 0.0, ALU.mult, ALU.add)
                    last.then_inc(s["t2s"], 1)
                    pool.wait_ge(s["t2s"], n)
                    pool.tensor_tensor(t["x3"][:, bass.ds(LANES_A * i + l, 1), :, :].rearrange("p o c d -> p (o c) d"),
                                       z[l][:, :, :], adab[l][:, 1:2, :].to_broadcast([P, TC, D]),
                                       ALU.add).then_inc(s["x3"], 1)

            run_stages(pool, stage)


def attention(nc, a, t, ps):
    w, vecs, rows = t["w"], t["vecs"], t["rows"]
    UNITS = NH // 2 * TC
    GH = 4
    GROUPS = NH // GH
    GU = UNITS // GROUPS
    VW = 3 * HD + 1
    SCORES, BIAS, EXPS, TURNS, PARTS = 5, 4, 3, 2, 1
    PAIRS = B // LANES
    TURN = LANES * UNITS
    SHIFT = 8
    S_BANK, T_BANK, V_BANK, X_BANK = 0, 2, 4, 6
    with ExitStack() as ctx:
        def sb(name, shape, dt=F32):
            return ctx.enter_context(nc.sbuf_tensor(name, shape, dt))

        def sem(name):
            return ctx.enter_context(nc.semaphore(name))

        x_rows = sb("b_x_rows", [P, TC, D])
        x_part = sb("b_x", [P, 2, DC, S], F32R)
        q_part = [sb(f"b_q{l}", [P, 2, DC, S], F32R) for l in range(LANES)]
        k_part = [sb(f"b_k{l}", [P, DC, 2, S], F32R) for l in range(LANES)]
        KM = 4
        k_head = sb("b_k_head", [P, KM, 2, 2, S], F32R)
        v_full = sb("b_v_full", [P, TC, D])
        v_rest = sb("b_v_rest", [P, TC, D])
        v_part = [sb(f"b_v{l}", [P, TC, NH, VW], BF16) for l in range(LANES)]
        bias = sb("b_bias", [P, GROUPS, GH, TC, S])
        mask8 = [sb(f"b_mask8{l}", [P, TC, S], U8) for l in range(LANES)]
        mask = [sb(f"b_mask{l}", [P, S], BF16) for l in range(LANES)]
        mask_sum = [sb(f"b_mask_sum{l}", [P, S]) for l in range(LANES)]
        masked = sb("b_masked", [P, P], BF16)
        head_rows = sb("b_head_rows", [P, 8])
        NP_ = 4
        prob = sb("b_prob", [P, NP_, 2 * S])
        lowest = sb("b_lowest", [P, NP_, 2])
        pT = sb("b_pT", [P, NP_, 2, 2 * S], F16)
        sums = sb("b_sums", [P, 2, TC * GH, HD])
        recip = sb("b_recip", [P, 2, TC * GH])
        ctx_rows = [sb(f"b_ctx{l}", [P, TC, D]) for l in range(LANES)]
        c_part = sb("b_c", [P, 2, DC, S], F32R)
        FP = (DC * FF + FC * D) // PAIRS
        ff_raw = sb("b_ff_raw", [P, FP])

        q = {n: sem(f"b_{n}") for n in (
            "x_mm", "q_mm", "k_mm", "v_mm", "c_mm", "o_mm", "x_hi", "q_hi", "k_hi", "v_hi", "v_mid", "c_hi",
            "x_lo", "q_lo", "k_lo", "v_full", "v_rest", "v_lo", "c_lo", "x4", "mask", "x3b")}
        score_mm, scored, exped = sem("b_score_mm"), sem("b_scored"), sem("b_exped")
        turned, t_hi, t_lo, applied = sem("b_turned"), sem("b_t_hi"), sem("b_t_lo"), sem("b_applied")
        group_read, normed = sem("b_group_read"), sem("b_normed")
        bias_masked = sem("b_bias_masked")
        k_ready = sem("b_k_ready")
        bias_in = [sem(f"b_bias_in{g}") for g in range(GROUPS)]
        x_in = sem("b_x_in")
        mask_in = [sem(f"b_mask_in{l}") for l in range(LANES)]
        once_in, ff_in, once, ff_hi, ff_lo = sem("b_once_in"), sem("b_ff_in"), sem("b_once"), sem("b_ff_hi"), sem("b_ff_lo")
        FREE_KEYS = 2 * KM

        def heads(u):
            return u // TC, u % TC

        def at(i, x):
            return TURN * i + (x + 1)

        def seq(i, x):
            return LANES * i + (x // UNITS + 1)

        def bank_of(i, x, at_first):
            return at_first if isinstance(i, int) and LANES * i + x == 0 else X_BANK + 1

        def run_slots(eng, slot):
            for k in range(-SCORES, SHIFT):
                slot(k, 0, range(0, B * UNITS))
            with eng.Fori(0, PAIRS - 1) as i:
                for k in range(SHIFT, SHIFT + TURN):
                    slot(k, i, range(-B * UNITS, B * UNITS))
            for k in range(SHIFT, TURN + 8):
                slot(k, PAIRS - 1, range(-B * UNITS, TURN))

        block = ctx.enter_context(nc.Block())

        @block.sync
        def _(sp):
            def load_bias(b, g):
                sp.dma_start(bias[:, g, :, :, :], a["fside_Bx16xSxS_0"][b, g * GH:(g + 1) * GH]
                             .rearrange("h (c p) k -> p h c k", p=P)).then_inc(bias_in[g], 16)

            def load_mask(b, l):
                sp.dma_start(mask8[l][:, :, :], a["mask"][b, 0].rearrange("(c p) k -> p c k", p=P)).then_inc(mask_in[l], 16)

            def copy_x(b):
                sp.dma_start(x_rows[:, :, :].rearrange("p (o c) d -> p o c d", o=1),
                             t["x3"][:, bass.ds(b, 1), :, :]).then_inc(x_in, 16)

            copy_x(1)
            sp.dma_start(head_rows[:, :], a["head_rows"]).then_inc(once_in, 16)
            for l in range(LANES):
                load_mask(l, l)
            for g in range(GROUPS):
                load_bias(0, g)
            sp.dma_start(ff_raw[:, :], a["ff"][:, 0:FP]).then_inc(ff_in, 16)

            def loads(b, more=True):
                if more:
                    wait_apart(sp, q["x_mm"], b + 1)
                    copy_x(b + 1)
                for g in range(GROUPS):
                    wait_apart(sp, scored, 2 * LANES + 2 * (UNITS * (b - 1)) + 2 * GU * (g + 1))
                    load_bias(b, g)

            with sp.Fori(0, PAIRS - 1) as i:
                for l in range(LANES):
                    loads(LANES * i + (l + 1))
                    wait_apart(sp, q["mask"], LANES * i + (l + 1))
                    load_mask(LANES * i + (l + 2), l)
                wait_apart(sp, ff_lo, i + 1)
                sp.dma_start(ff_raw[:, :], a["ff"][:, bass.ds(FP * i + FP, FP)]).then_inc(ff_in, 16)
            loads(B - 1, more=False)

        @block.tensor
        def _(pe):
            def project(name, src_part, bank, done):
                for m in range(DC):
                    for k in range(DC):
                        last = matmul3(pe, ps[:, bank, m * S:(m + 1) * S], parts(w[name], k, m * P, (m + 1) * P),
                                       parts(src_part, k, 0, S), k == 0, k == DC - 1)
                last.then_inc(done, 1)

            def to_rows(name, src_part, bank, done):
                for c in range(TC):
                    for k in range(DC):
                        last = matmul3(pe, ps[:, bank, c * D:(c + 1) * D], parts(src_part, k, c * P, (c + 1) * P),
                                       parts(w[name], k, 0, D), k == 0, k == DC - 1)
                last.then_inc(done, 1)

            def turn_x(i, x):
                if isinstance(i, int) and LANES * i + x == 0:
                    src = t["x3"][:, 0, :, :]
                else:
                    src = x_rows[:, :, :]
                    pe.wait_ge(x_in, 16 * (LANES * i + x // UNITS))
                    pe.wait_ge(q["v_full"], seq(i, x - UNITS))
                for c in range(DC):
                    for r in range(TC):
                        last = pe.transpose(ps[:, X_BANK + 1, c * S + r * P:c * S + (r + 1) * P],
                                            src[:, r, c * P:(c + 1) * P], t["ident"][:, :])
                last.then_inc(q["x_mm"], 1)

            def queries(i, x):
                pe.wait_ge(q["x_lo"], seq(i, x))
                project("Wq", x_part, X_BANK + 1, q["q_mm"])

            def keys(i, x):
                if bank_of(i, x, T_BANK) == X_BANK + 1:
                    pe.wait_ge(q["q_lo"], seq(i, x))
                project("Wk", x_part, bank_of(i, x, T_BANK), q["k_mm"])

            def values(i, x):
                if bank_of(i, x, V_BANK) == X_BANK + 1:
                    pe.wait_ge(q["k_lo"], seq(i, x))
                to_rows("Wv", x_part, bank_of(i, x, V_BANK), q["v_mm"])

            def turn_ctx(i, x):
                pe.wait_ge(normed, GROUPS * seq(i, x))
                pe.wait_ge(q["x4"], seq(i, x))
                for k in range(DC):
                    for c in range(TC):
                        last = pe.transpose(ps[:, X_BANK, k * S + c * P:k * S + (c + 1) * P],
                                            ctx_rows[x // UNITS % LANES][:, c, k * P:(k + 1) * P], t["ident"][:, :])
                last.then_inc(q["c_mm"], 1)

            def output(i, x):
                pe.wait_ge(q["c_lo"], seq(i, x))
                to_rows("Wo", c_part, X_BANK, q["o_mm"])

            def scores(i, x):
                u, l = x % UNITS, x // UNITS % LANES
                pair, c = heads(u)
                slot = (x // TC) % KM
                if u == 0:
                    pe.wait_ge(q["mask"], seq(i, x))
                    pe.wait_ge(q["q_lo"], seq(i, x))
                if c == 0:
                    pe.wait_ge(k_ready, (TURN // TC) * i + (x // TC + 1))
                pe.wait_ge(scored, 2 * at(i, x))
                out_ = ps[:, S_BANK + x % 2, :]
                if c == 0:
                    pe.matmul(out_, masked[:, :], mask[l][:, :].rearrange("p (o s) -> p o s", o=1).to_broadcast([P, 2, S]),
                              start=True, stop=False)
                chunk = pair // 4
                qh, ql = (q_part[l][:, h, chunk, c * P:(c + 1) * P] for h in range(2))
                kh, kl = (k_head[:, slot, h, :, :].rearrange("p j s -> p (j s)") for h in range(2))
                pe.matmul(out_, qh, kh, start=(c != 0), stop=False)
                pe.matmul(out_, qh, kl, start=False, stop=False)
                pe.matmul(out_, ql, kh, start=False, stop=True).then_inc(score_mm, 1)

            def turn(i, x):
                pe.wait_ge(exped, 2 * at(i, x))
                pe.wait_ge(t_lo, at(i, x))
                for j in range(4):
                    last = pe.transpose(ps[:, T_BANK + x % 2, j * P:(j + 1) * P], prob[:, x % NP_, j * P:(j + 1) * P],
                                        t["ident"][:, :])
                last.then_inc(turned, 1)

            def apply(i, x):
                u, l = x % UNITS, x // UNITS % LANES
                pair, c = heads(u)
                g = (x // GU) % 2
                if u == 0:
                    pe.wait_ge(q["v_lo"], seq(i, x))
                if u % GU == 0:
                    pe.wait_ge(group_read, 2 * (TURN // GU) * i + 2 * (x // GU + 1))
                pe.wait_ge(t_lo, at(i, x) + 2)
                for j in range(2):
                    head = 2 * pair + j
                    col = (c * GH + head % GH) * VW
                    for kc in range(TC):
                        for h in range(2):
                            last = pe.matmul(ps[:, V_BANK + g, col:col + VW], pT[:, x % NP_, h, (2 * j + kc) * P:(2 * j + kc + 1) * P],
                                             v_part[l][:, kc, head, :], start=(kc + h == 0), stop=(kc + h == 2))
                last.then_inc(applied, 1)

            def slot(k, i, here):
                s, first = k % UNITS, k // UNITS * UNITS
                if k >= 0 and first + UNITS in here:
                    for when, what in ((0, turn_x), (3, queries), (6, keys), (9, values)):
                        if s == when:
                            what(i, first + UNITS)
                if k >= 0 and first - UNITS in here:
                    for when, what in ((2, turn_ctx), (5, output)):
                        if s == when:
                            what(i, first - UNITS)
                if k + SCORES in here:
                    scores(i, k + SCORES)
                if k + TURNS in here:
                    turn(i, k + TURNS)
                if k in here:
                    apply(i, k)

            for what in (turn_x, queries, keys, values):
                what(0, 0)
            pe.wait_ge(once, 3)
            run_slots(pe, slot)

        @block.scalar
        def _(act):
            def high(dst, src, wait, n, done):
                act.wait_ge(wait, n)
                act.activation(dst, src, ACT.Copy).then_inc(done, 1)

            def x_high(i, x):
                high(x_part[:, 0, :, :].rearrange("p c s -> p (c s)"), ps[:, X_BANK + 1, :], q["x_mm"], seq(i, x), q["x_hi"])

            def ctx_high(i, x):
                high(c_part[:, 0, :, :].rearrange("p c s -> p (c s)"), ps[:, X_BANK, :], q["c_mm"], seq(i, x), q["c_hi"])

            def q_high(i, x):
                act.wait_ge(q["q_mm"], seq(i, x))
                for m in range(DC):
                    last = act.activation(q_part[x // UNITS % LANES][:, 0, m, :], ps[:, X_BANK + 1, m * S:(m + 1) * S],
                                          ACT.Identity, bias=vecs[:, VEC["bq"] + m:VEC["bq"] + m + 1])
                last.then_inc(q["q_hi"], 1)

            def k_high(i, x):
                act.wait_ge(q["k_mm"], seq(i, x))
                for m in range(DC):
                    last = act.activation(k_part[x // UNITS % LANES][:, m, 0, :], ps[:, bank_of(i, x, T_BANK), m * S:(m + 1) * S],
                                          ACT.Identity, bias=vecs[:, VEC["bk"] + m:VEC["bk"] + m + 1])
                last.then_inc(q["k_hi"], 1)

            def v_slices(l, s):
                return v_part[l][:, :, :, s * HD:(s + 1) * HD]

            def v_high(i, x):
                act.wait_ge(q["v_full"], seq(i, x))
                act.activation(v_slices(x // UNITS % LANES, 0), v_full[:, :, :].rearrange("p c (h d) -> p c h d", d=HD),
                               ACT.Copy).then_inc(q["v_hi"], 1)

            def v_middle(i, x):
                act.wait_ge(q["v_rest"], seq(i, x))
                act.activation(v_slices(x // UNITS % LANES, 1), v_rest[:, :, :].rearrange("p c (h d) -> p c h d", d=HD),
                               ACT.Copy).then_inc(q["v_mid"], 1)

            def exps(i, x):
                r = x % NP_
                for j in range(2):
                    act.wait_ge(scored, 2 * at(i, x) + (3 + j))
                    act.activation(prob[:, r, j * S:(j + 1) * S], prob[:, r, j * S:(j + 1) * S], ACT.Exp,
                                   bias=lowest[:, r, j:j + 1], scale=-1.0).then_inc(exped, 1)

            def turned_high(i, x):
                act.wait_ge(turned, at(i, x) + NP_)
                act.wait_ge(applied, at(i, x))
                act.activation(pT[:, x % NP_, 0, :], ps[:, T_BANK + x % 2, :], ACT.Copy).then_inc(t_hi, 1)

            def slot(k, i, here):
                s, first = k % UNITS, k // UNITS * UNITS
                if k == -TURNS:
                    v_middle(0, 0)
                if k + PARTS in here:
                    turned_high(i, k + PARTS)
                if k + EXPS in here:
                    exps(i, k + EXPS)
                if k >= 0 and first + UNITS in here:
                    for when, what in ((0, x_high), (3, q_high), (6, k_high), (11, v_high), (12, v_middle)):
                        if s == when:
                            what(i, first + UNITS)
                if k >= 0 and first - UNITS in here and s == 2:
                    ctx_high(i, first - UNITS)

            for what in (x_high, q_high, k_high, v_high):
                what(0, 0)
            run_slots(act, slot)

        @block.vector
        def _(dve):
            dve.sem_inc(scored, 4)
            dve.sem_inc(t_lo, 2)
            dve.sem_inc(group_read, 4)
            dve.sem_inc(q["x4"], 1)

            def x_low(i, x):
                dve.wait_ge(q["x_hi"], seq(i, x))
                dve.tensor_tensor(x_part[:, 1, :, :].rearrange("p c s -> p (c s)"), ps[:, X_BANK + 1, :],
                                  x_part[:, 0, :, :].rearrange("p c s -> p (c s)").bitcast(F32),
                                  ALU.subtract).then_inc(q["x_lo"], 1)

            def ctx_low(i, x):
                dve.wait_ge(q["c_hi"], seq(i, x))
                dve.tensor_tensor(c_part[:, 1, :, :].rearrange("p c s -> p (c s)"), ps[:, X_BANK, :],
                                  c_part[:, 0, :, :].rearrange("p c s -> p (c s)").bitcast(F32),
                                  ALU.subtract).then_inc(q["c_lo"], 1)

            def q_low(i, x):
                dve.wait_ge(q["q_hi"], seq(i, x))
                part = q_part[x // UNITS % LANES]
                for m in range(DC):
                    last = dve.scalar_tensor_tensor(part[:, 1, m, :], ps[:, X_BANK + 1, m * S:(m + 1) * S],
                                                    vecs[:, VEC["bq"] + m:VEC["bq"] + m + 1], part[:, 0, m, :].bitcast(F32),
                                                    ALU.add, ALU.subtract)
                last.then_inc(q["q_lo"], 1)

            def k_low(i, x):
                dve.wait_ge(q["k_hi"], seq(i, x))
                part = k_part[x // UNITS % LANES]
                for m in range(DC):
                    last = dve.scalar_tensor_tensor(part[:, m, 1, :], ps[:, bank_of(i, x, T_BANK), m * S:(m + 1) * S],
                                                    vecs[:, VEC["bk"] + m:VEC["bk"] + m + 1], part[:, m, 0, :].bitcast(F32),
                                                    ALU.add, ALU.subtract)
                last.then_inc(q["k_lo"], 1)

            def v_whole(i, x):
                dve.wait_ge(q["v_mm"], seq(i, x))
                if not isinstance(i, int) or LANES * i + x > 0:
                    dve.wait_ge(q["v_rest"], LANES * i + x // UNITS)
                dve.tensor_tensor(v_full[:, :, :], ps[:, bank_of(i, x, V_BANK), :].rearrange("p (c d) -> p c d", c=TC),
                                  rows[:, ROWS["bv"]:ROWS["bv"] + 1, :].to_broadcast([P, TC, D]), ALU.add).then_inc(q["v_full"], 1)

            def residual(i, x):
                dve.wait_ge(q["o_mm"], seq(i, x))
                dve.wait_ge(q["x3b"], seq(i, x))
                x4 = t["x3"][:, bass.ds(LANES * i + x // UNITS, 1), :, :].rearrange("p o c d -> p (o c) d")
                dve.tensor_tensor(x4, ps[:, X_BANK, :].rearrange("p (c d) -> p c d", c=TC), x4, ALU.add).then_inc(q["x4"], 1)

            def add_bias(i, x):
                u = x % UNITS
                pair, c = heads(u)
                r = x % NP_
                dve.wait_ge(score_mm, at(i, x) + FREE_KEYS)
                if u % GU == 0:
                    dve.wait_ge(bias_in[u // GU], 16 * seq(i, x))
                if u % GU == 1:
                    dve.wait_ge(bias_masked, GROUPS * (LANES * i + x // UNITS) + (u // GU + 1))
                wait_apart(dve, turned, at(i, x))
                for j in range(2):
                    dve.tensor_tensor_reduce(prob[:, r, j * S:(j + 1) * S], ps[:, S_BANK + x % 2, j * S:(j + 1) * S],
                                             bias[:, u // GU, 2 * (pair % 2) + j, c, :], -1.0, 3.0e38, ALU.add, ALU.min,
                                             lowest[:, r, j:j + 1]).then_inc(scored, 1)

            def turned_low(i, x):
                dve.wait_ge(t_hi, at(i, x))
                dve.tensor_tensor(pT[:, x % NP_, 1, :], ps[:, T_BANK + x % 2, :], pT[:, x % NP_, 0, :],
                                  ALU.subtract).then_inc(t_lo, 1)

            def sum_group(i, x):
                g = (x // GU) % 2
                res = ps[:, V_BANK + g, 0:TC * GH * VW].rearrange("p (e f) -> p e f", f=VW)
                dve.wait_ge(applied, at(i, x) + NP_)
                dve.tensor_reduce(sums[:, g, :, :], res[:, :, 0:3 * HD].rearrange("p e (s d) -> p e d s", d=HD), AX.X,
                                  ALU.add).then_inc(group_read, 1)
                dve.reciprocal(recip[:, g, :], res[:, :, 3 * HD]).then_inc(group_read, 1)

            def norm_group(i, x):
                u, l, g = x % UNITS, x // UNITS % LANES, (x // GU) % 2
                dve.wait_ge(group_read, 2 * (TURN // GU) * i + (2 * (x // GU + 1) + 4))
                at_ = u // GU * GH * HD
                for c in range(TC):
                    last = dve.tensor_tensor(ctx_rows[l][:, c, at_:at_ + GH * HD].rearrange("p (h d) -> p h d", d=HD),
                                             sums[:, g, c * GH:(c + 1) * GH, :],
                                             recip[:, g, c * GH:(c + 1) * GH].rearrange("p (e o) -> p e o", o=1)
                                             .to_broadcast([P, GH, HD]), ALU.mult)
                last.then_inc(normed, 1)

            def slot(k, i, here):
                s, first = k % UNITS, k // UNITS * UNITS
                if k + BIAS in here:
                    add_bias(i, k + BIAS)
                if k % GU == 0 and k - 1 in here:
                    sum_group(i, k - 1)
                if k >= 0 and first + UNITS in here:
                    for when, what in ((1, x_low), (4, q_low), (7, k_low), (10, v_whole)):
                        if s == when:
                            what(i, first + UNITS)
                if k >= 0 and first - UNITS in here:
                    for when, what in ((3, ctx_low), (6, residual)):
                        if s == when:
                            what(i, first - UNITS)
                if k + PARTS in here:
                    turned_low(i, k + PARTS)
                if k % GU == 0 and k - 1 in here:
                    norm_group(i, k - 1)

            for what in (x_low, q_low, k_low, v_whole):
                what(0, 0)
            run_slots(dve, slot)

        @block.gpsimd
        def _(pool):
            pool.wait_ge(once_in, 16)
            for l in range(LANES):
                pool.memset(v_part[l][:, :, :, 3 * HD:VW], 1.0).then_inc(once, 1)
            pool.tensor_scalar(masked[:, :], t["ident"][:, :], MASKED, 0.0, ALU.mult, ALU.add).then_inc(once, 1)

            def mask_bits(i, l):
                wait_apart(pool, mask_in[l], 16 * i + 16)
                pool.tensor_copy(mask[l][:, :], mask8[l][:, 0, :])
                pool.tensor_scalar(mask_sum[l][:, :], mask8[l][:, 1, :], MASKED, 0.0, ALU.mult, ALU.add).then_inc(q["mask"], 1)

            pool.sem_inc(score_mm, FREE_KEYS)
            pool.sem_inc(applied, NP_)
            pool.sem_inc(turned, NP_)
            with pool.Fori(0, PAIRS) as i:
                for l in range(LANES):
                    n = LANES * i + (l + 1)
                    pool.wait_ge(score_mm, TURN * i + (UNITS * (l - 1) + FREE_KEYS) if l else TURN * i + 1)
                    mask_bits(i, l)
                    pool.wait_ge(q["x_mm"], n)
                    x3 = t["x3"][:, bass.ds(LANES * i + l, 1), :, :].rearrange("p o c d -> p (o c) d")
                    pool.tensor_tensor(x3, x3, rows[:, ROWS["bo"]:ROWS["bo"] + 1, :].to_broadcast([P, TC, D]),
                                       ALU.add).then_inc(q["x3b"], 1)
                    wait_apart(pool, q["k_lo"], n)
                    wait_apart(pool, q["mask"], n)

                    def by_head(tile):
                        return tile[:, :, :].rearrange("p c (h d) -> p c h d", d=HD)

                    for pair in range(NH // 2):
                        if pair % 2 == 0:
                            g = pair // 2
                            pool.wait_ge(bias_in[g], 16 * n)
                            pool.tensor_tensor(bias[:, g, :, 1, :], bias[:, g, :, 1, :],
                                               mask_sum[l][:, :].rearrange("p (o s) -> p o s", o=1).to_broadcast([P, GH, S]),
                                               ALU.add).then_inc(bias_masked, 1)
                        if pair == 2:
                            pool.wait_ge(q["v_hi"], n)
                            pool.tensor_tensor(by_head(v_rest), by_head(v_full), v_part[l][:, :, :, 0:HD],
                                               ALU.subtract).then_inc(q["v_rest"], 1)
                        if pair == 3:
                            pool.wait_ge(q["v_mid"], n)
                            pool.tensor_tensor(v_part[l][:, :, :, 2 * HD:3 * HD], by_head(v_rest),
                                               v_part[l][:, :, :, HD:2 * HD], ALU.subtract).then_inc(q["v_lo"], 1)
                        wait_apart(pool, score_mm, TURN * i + (UNITS * l + 2 * pair + 2))
                        for j in range(2):
                            head = (2 * pair + j) % 8
                            last = pool.tensor_scalar(k_head[:, pair % KM, :, j, :], k_part[l][:, pair // 4, :, :],
                                                      head_rows[:, head:head + 1], 0.0, ALU.mult, ALU.add)
                        last.then_inc(k_ready, 1)
                wait_apart(pool, ff_in, 16 * i + 16)
                eighth = bass.ds(FP * i, FP)
                pool.tensor_copy(t["ff"][:, 0, eighth], ff_raw[:, :]).then_inc(ff_hi, 1)
                pool.wait_ge(ff_hi, i + 1)
                pool.tensor_tensor(t["ff"][:, 1, eighth], ff_raw[:, :], t["ff"][:, 0, eighth].bitcast(F32),
                                   ALU.subtract).then_inc(ff_lo, 1)


def feed_forward(nc, a, t, ps, out):
    vecs, rows = t["vecs"], t["rows"]
    w1 = t["ff"][:, :, 0:DC * FF].rearrange("p h (k m) -> p h k m", m=FF)
    w2 = t["ff"][:, :, DC * FF:].rearrange("p h (k m) -> p h k m", m=D)
    BANKS = FC // 2
    PAIRS = B // LANES
    with ExitStack() as ctx:
        def per_lane(name, shape, dt=F32):
            return [ctx.enter_context(nc.sbuf_tensor(f"{name}{l}", shape, dt)) for l in range(LANES)]

        def sem(name):
            return ctx.enter_context(nc.semaphore(name))

        norm = per_lane("c_norm", [P, TC, D])
        h = per_lane("c_h", [P, DC, S])
        h_part = per_lane("c_h_part", [P, 2, DC, S], F32R)
        act_ = per_lane("c_act", [P, FC, S])
        a_part = per_lane("c_act_part", [P, 2, FC, S], F32R)
        x5 = per_lane("c_x5", [P, TC, D])
        rot1 = per_lane("c_rot1", [P, TC, D])
        rot2 = per_lane("c_rot2", [P, TC, D])
        bn = per_lane("c_bn", [P, TC, 6])
        mv = per_lane("c_mv", [P, TC, 2])
        rv = per_lane("c_rv", [P, TC])
        rs = per_lane("c_rs", [P, TC])
        s = {n: sem(f"c_{n}") for n in ("own", "ve", "rstd", "norm", "normT", "h", "h_hi", "h_lo", "out_mm", "x4b",
                                        "x5", "rot1", "rot2", "rotated")}
        ff_mm, ff_act, ff_hi, ff_lo = sem("c_ff_mm"), sem("c_ff_act"), sem("c_ff_hi"), sem("c_ff_lo")
        stored = [sem(f"c_stored{l}") for l in range(LANES)]

        def bank(l, j):
            return ps[:, BANKS * l + j, :]

        def x4(i, l):
            return t["x3"][:, bass.ds(LANES * i + l, 1), :, :].rearrange("p o c d -> p (o c) d")

        def turns(eng, prepare, work):
            for l in range(LANES):
                prepare(0, l)
            with eng.Fori(0, PAIRS - 1) as i:
                work(i, lambda l: prepare(i + 1, l))
            work(PAIRS - 1, lambda l: None)

        block = ctx.enter_context(nc.Block())

        @block.sync
        def _(sp):
            with sp.Fori(0, PAIRS) as i:
                for l in range(LANES):
                    wait_apart(sp, s["rotated"], LANES * i + (l + 1))
                    sp.dma_start(out[LANES * i + l].rearrange("(c p) d -> p c d", p=P), rot1[l][:, :, :]).then_inc(stored[l], 16)
            for l in range(LANES):
                sp.wait_ge(stored[l], 16 * PAIRS + 16)

        @block.tensor
        def _(pe):
            def prepare(i, l):
                pe.wait_ge(s["norm"], LANES * i + (l + 1))
                for c in range(DC):
                    for r in range(TC):
                        last = pe.transpose(bank(l, 1)[:, c * S + r * P:c * S + (r + 1) * P], norm[l][:, r, c * P:(c + 1) * P],
                                            t["ident"][:, :])
                last.then_inc(s["normT"], 1)

            def work(i, next_):
                n = [LANES * i + (l + 1) for l in range(LANES)]
                for l in range(LANES):
                    pe.wait_ge(s["h_lo"], n[l])
                    for m in range(FC):
                        for k in range(DC):
                            last = matmul3(pe, bank(l, m // 2)[:, (m % 2) * S:(m % 2 + 1) * S], parts(w1, k, m * P, (m + 1) * P),
                                           parts(h_part[l], k, 0, S), k == 0, k == DC - 1)
                        if m % 2:
                            last.then_inc(ff_mm, 1)
                for l in range(LANES):
                    for c in range(TC):
                        for k in range(FC):
                            if c == 0 and k % 2 == 0:
                                pe.wait_ge(ff_lo, BANKS * LANES * i + (BANKS * l + k // 2 + 1))
                            last = matmul3(pe, bank(l, 0)[:, c * D:(c + 1) * D], parts(a_part[l], k, c * P, (c + 1) * P),
                                           parts(w2, k, 0, D), k == 0, k == FC - 1)
                    last.then_inc(s["out_mm"], 1)
                    next_(l)
            turns(pe, prepare, work)

        @block.scalar
        def _(act):
            def prepare(i, l):
                n = LANES * i + (l + 1)
                act.wait_ge(s["normT"], n)
                for c in range(DC):
                    last = act.activation(h[l][:, c, :], bank(l, 1)[:, c * S:(c + 1) * S], ACT.Identity,
                                          bias=vecs[:, VEC["beta2"] + c:VEC["beta2"] + c + 1],
                                          scale=vecs[:, VEC["g2"] + c:VEC["g2"] + c + 1])
                last.then_inc(s["h"], 1)
                act.wait_ge(s["h"], n)
                act.activation(h_part[l][:, 0, :, :], h[l][:, :, :], ACT.Copy).then_inc(s["h_hi"], 1)

            def work(i, next_):
                for l in range(LANES):
                    for j in range(BANKS):
                        n = BANKS * LANES * i + (BANKS * l + j + 1)
                        act.wait_ge(ff_mm, n)
                        for m in (2 * j, 2 * j + 1):
                            last = act.activation(act_[l][:, m, :], bank(l, j)[:, (m % 2) * S:(m % 2 + 1) * S],
                                                  ACT.Gelu_apprx_sigmoid, bias=vecs[:, VEC["ff_b1"] + m:VEC["ff_b1"] + m + 1])
                        last.then_inc(ff_act, 1)
                        act.wait_ge(ff_act, n)
                        act.activation(a_part[l][:, 0, 2 * j:2 * j + 2, :], act_[l][:, 2 * j:2 * j + 2, :],
                                       ACT.Copy).then_inc(ff_hi, 1)
                for l in range(LANES):
                    next_(l)
            turns(act, prepare, work)

        @block.vector
        def _(dve):
            def statistics(i, l):
                for r in range(TC):
                    last = dve.bn_stats(bn[l][:, r, :], t["x3"][:, bass.ds(LANES * i + l, 1), r, :].rearrange("p o d -> p (o d)"))
                last.then_inc(s["own"], 1)
                wait_apart(dve, s["own"], 2 * LANES * i + (2 * l + 1))
                for r in range(TC):
                    last = dve.bn_aggr(mv[l][:, r, :], bn[l][:, r, :])
                last.then_inc(s["own"], 1)
                dve.wait_ge(s["own"], 2 * LANES * i + (2 * l + 2))
                dve.tensor_scalar(rv[l][:, :], mv[l][:, :, 1], EPS, None, ALU.add).then_inc(s["ve"], 1)

            def normalised(i, l):
                dve.wait_ge(s["rstd"], LANES * i + (l + 1))
                for r in range(TC):
                    last = dve.tensor_scalar(norm[l][:, r, :], t["x3"][:, bass.ds(LANES * i + l, 1), r, :].rearrange("p o d -> p (o d)"),
                                             mv[l][:, r, 0:1], rs[l][:, r:r + 1], ALU.subtract, ALU.mult)
                last.then_inc(s["norm"], 1)

            def low(i, l):
                n = LANES * i + (l + 1)
                dve.wait_ge(s["h_hi"], n)
                dve.tensor_tensor(h_part[l][:, 1, :, :], h[l][:, :, :], h_part[l][:, 0, :, :].bitcast(F32),
                                  ALU.subtract).then_inc(s["h_lo"], 1)

            def work(i, more):
                if more:
                    for l in range(LANES):
                        statistics(i + 1, l)
                for l in range(LANES):
                    for j in range(BANKS):
                        dve.wait_ge(ff_hi, BANKS * LANES * i + (BANKS * l + j + 1))
                        dve.tensor_tensor(a_part[l][:, 1, 2 * j:2 * j + 2, :], act_[l][:, 2 * j:2 * j + 2, :],
                                          a_part[l][:, 0, 2 * j:2 * j + 2, :].bitcast(F32), ALU.subtract).then_inc(ff_lo, 1)
                    if more:
                        normalised(i + 1, l)
                for l in range(LANES):
                    n = LANES * i + (l + 1)
                    dve.wait_ge(s["out_mm"], n)
                    dve.wait_ge(s["x4b"], n)
                    if not more:
                        dve.wait_ge(s["rotated"], LANES * (i - 1) + (l + 1))
                    dve.tensor_tensor(x5[l][:, :, :], bank(l, 0).rearrange("p (c d) -> p c d", c=TC), x4(i, l),
                                      ALU.add).then_inc(s["x5"], 1)
                    if more:
                        low(i + 1, l)

            for step in (statistics, normalised, low):
                for l in range(LANES):
                    step(0, l)
            with dve.Fori(0, PAIRS - 1) as i:
                work(i, True)
            work(PAIRS - 1, False)

        @block.gpsimd
        def _(pool):
            def prepare(i, l):
                n = LANES * i + (l + 1)
                pool.wait_ge(s["ve"], n)
                pool.tensor_tensor(rs[l][:, :], rv[l][:, :], t["halves"][:, 0:TC], ALU.pow).then_inc(s["rstd"], 1)
                pool.wait_ge(s["norm"], n)
                pool.tensor_tensor(x4(i, l), x4(i, l), rows[:, ROWS["ff_b2"]:ROWS["ff_b2"] + 1, :].to_broadcast([P, TC, D]),
                                   ALU.add).then_inc(s["x4b"], 1)

            def work(i, next_):
                for l in range(LANES):
                    next_(l)
                for l in range(LANES):
                    n = LANES * i + (l + 1)
                    fours = [tile[:, :, :].rearrange("p c (g j) -> p (c g) j", j=4) for tile in (x5[l], rot1[l], rot2[l])]
                    pool.wait_ge(s["x5"], n)
                    pool.wait_ge(stored[l], 16 * i + 16)
                    pool.tensor_tensor(fours[1], fours[0], t["rot"][:, 0, bass.ds(LANES * i + l, 1), :]
                                       .to_broadcast([P, TC * D // 4, 4]), ALU.mult).then_inc(s["rot1"], 1)
                    for j in range(4):
                        last = pool.tensor_tensor(fours[2][:, :, j:j + 1], fours[0][:, :, (j ^ 1):(j ^ 1) + 1],
                                                  t["rot"][:, 1, bass.ds(LANES * i + l, 1), j:j + 1]
                                                  .to_broadcast([P, TC * D // 4, 1]), ALU.mult)
                    last.then_inc(s["rot2"], 1)
                    pool.wait_ge(s["rot1"], n)
                    pool.wait_ge(s["rot2"], n)
                    pool.tensor_tensor(rot1[l][:, :, :], rot1[l][:, :, :], rot2[l][:, :, :], ALU.add).then_inc(s["rotated"], 1)
            for l in range(LANES):
                pool.sem_inc(stored[l], 16)
            turns(pool, prepare, work)


_VEC_ORDER = ("L0_cond_b1", "L0_cond_b2", "L0_cond_bsc", "L0_cond_bsh", "L0_cond_b_in", "L1_cond_b1_nr", "L1_cond_b1_tsr",
              "L1_cond_b1_sr", "L1_cond_b2_sr", "L2_cond_bq", "L2_cond_bk", "L2_cond_b1", "L2_cond_g2", "L2_cond_beta2")
_ROW_ORDER = ("L0_cond_b_out", "L1_cond_b2_nr", "L1_cond_b2_tsr", "L1_cond_b3_sr", "L1_cond_gamma", "L1_cond_beta",
              "L2_cond_bv", "L2_cond_bo", "L2_cond_b2")
_WEIGHTS = {"W_in": "L0_cond_W_in", "W_out": "L0_cond_W_out", "nr_w1": "L1_cond_w1_nr", "nr_w2": "L1_cond_w2_nr",
            "tsr_w1": "L1_cond_w1_tsr", "tsr_w2": "L1_cond_w2_tsr", "sr_w1": "L1_cond_w1_sr", "sr_w2": "L1_cond_w2_sr",
            "sr_w3": "L1_cond_w3_sr", "Wq": "L2_cond_Wq", "Wk": "L2_cond_Wk", "Wv": "L2_cond_Wv", "Wo": "L2_cond_Wo"}
_AS_THEY_ARE = ("x", "condB_t", "itok_B_0_2", "itok_B_34_63", "fside_Bx16xSxS_0", "condB_theta", "condB_phi",
                "L0_cond_W1", "L0_cond_W2", "L0_cond_Wsc", "L0_cond_Wsh", "L0_cond_gamma", "L0_cond_beta",
                "L2_cond_W_ada", "L2_cond_b_ada")


def constants():
    def freqs(half):
        return np.exp(np.arange(half, dtype=np.float32) * np.float32(-np.log(10000.0) / (half - 1)))
    consts = np.zeros((P, 4), np.float32)
    consts[:, 0] = np.tile(freqs(E0 // 2), 2)
    consts[:, 1] = freqs(D // 2)
    consts[E0 // 2:, 2] = 0.25
    consts[E0 // 2:, 3] = np.pi / 2
    odd = np.zeros((P, 8), np.float32)
    for head in range(8):
        odd[head * HD:(head + 1) * HD, head] = 1.0
    return {"ident": np.eye(P, dtype=np.float32), "consts": consts, "head_rows": odd}


def by_partition(weight):
    k, m = weight.shape
    return weight.reshape(k // P, P, m).transpose(1, 0, 2).reshape(P, k // P * m)


def laid_out(inputs):
    arrays = {n: np.ascontiguousarray(inputs[n]) for n in _AS_THEY_ARE}
    arrays |= {n: np.ascontiguousarray(inputs[src]) for n, src in _WEIGHTS.items()}
    arrays["vec_rows"] = np.concatenate([np.asarray(inputs[n]) for n in _VEC_ORDER]).reshape(-1, P)
    arrays["rows"] = np.concatenate([np.asarray(inputs[n]) for n in _ROW_ORDER])
    arrays["mask"] = np.ascontiguousarray(inputs["mask_Bx1xSxS_bk0"])
    arrays["ff"] = np.concatenate([by_partition(np.asarray(inputs[n])) for n in ("L2_cond_W1", "L2_cond_W2")], axis=1)
    return arrays | constants()


def kernel(**inputs):
    import concourse.bacc as bacc
    from concourse.bass_utils import run_bass_kernel_spmd as run

    arrays = laid_out(inputs)
    nc = bacc.Bacc("TRN2", target_bir_lowering=False, num_devices=1)
    a = {n: nc.dram_tensor(f"in_{n}", v.shape, mybir.dt.from_np(v.dtype), kind="ExternalInput").ap()
         for n, v in arrays.items()}
    out = nc.dram_tensor("out", (B, S, D), F32, kind="ExternalOutput").ap()
    build_program(nc, a, out)
    r = run(nc, [{f"in_{n}": v for n, v in arrays.items()}], core_ids=[0])
    return r.results[0]["out"]
```
